# Optimizing a Trainium2 kernel written in Bass

```python
import numpy as np
import jax
import jax.numpy as jnp

def _softmax(x, axis=-1):
    return jax.nn.softmax(x, axis=axis)
def _gelu(x):
    return jax.nn.gelu(x, approximate=True)
def _silu(x):
    return jax.nn.silu(x)
def _sigmoid(x):
    return jax.nn.sigmoid(x)
def _layernorm(x, axis=-1, eps=1e-5):
    m = jnp.mean(x, axis=axis, keepdims=True)
    v = jnp.var(x, axis=axis, keepdims=True)
    return (x - m) / jnp.sqrt(v + eps)
def _scatter_add(tgt, idx, src, axis=0):
    return tgt.at[idx].add(src)
def _segment_sum(src, seg, n):
    return jax.ops.segment_sum(src, seg, n)

kernel_name = 'mk_conv_attn_hybrid_d4_conv_nhwc128_1035d7'

def setup_inputs(seed: int = 0):
    np.random.seed(seed)
    _w = jnp.asarray
    def _rec_inputs():
        import jax
        import jax.numpy as jnp
        _gk = jax.random.key(seed)
        x = -0.0005207 + 1.001 * jax.random.normal(jax.random.fold_in(_gk, 1), (4, 64, 64, 128), jnp.float32)
        return x
    x = _rec_inputs()
    def _L0_conv_setup():
        import jax, jax.numpy as jnp
        import numpy as np
        B, H, W, C = (4, 64, 64, 128)
        G = 4
        HC = C // G
        K = 3
        K2 = K * K
        PAD = K // 2
        SCALE = HC ** (-0.5)

        def conv2d(x, w, padding=1, dilation=1, groups=1):
            return jax.lax.conv_general_dilated(x, w, (1, 1), [(padding, padding), (padding, padding)], rhs_dilation=(dilation, dilation), dimension_numbers=('NCHW', 'OIHW', 'NCHW'), feature_group_count=groups)

        def pconv(x, w):
            c4 = w.shape[0]
            return jnp.concatenate([conv2d(x[:, :c4], w, padding=1), x[:, c4:]], axis=1)

        def conv1x1(x, w, b):
            return jnp.einsum('bchw,oc->bohw', x, w) + b[None, :, None, None]

        def deform_sample(img, offset, mask, dilation, pad):
            b, cg, h, w = img.shape
            ky, kx = jnp.meshgrid(jnp.arange(K), jnp.arange(K), indexing='ij')
            base_y = (ky.reshape(-1) * dilation - pad).astype(img.dtype)
            base_x = (kx.reshape(-1) * dilation - pad).astype(img.dtype)
            off = offset.reshape(b, K2, 2, h, w)
            py = jnp.arange(h, dtype=img.dtype)[None, None, :, None] + base_y[None, :, None, None] + off[:, :, 0]
            px = jnp.arange(w, dtype=img.dtype)[None, None, None, :] + base_x[None, :, None, None] + off[:, :, 1]
            y0 = jnp.floor(py)
            x0 = jnp.floor(px)
            wy = py - y0
            wx = px - x0
            flat = img.reshape(b, cg, h * w)

            def gather(iy, ix):
                valid = ((iy >= 0) & (iy < h) & (ix >= 0) & (ix < w)).astype(img.dtype)
                idx = (jnp.clip(iy, 0, h - 1) * w + jnp.clip(ix, 0, w - 1)).astype(jnp.int32)
                g = jax.vmap(lambda f, i: jnp.take(f, i, axis=1))(flat, idx.reshape(b, -1))
                return g.reshape(b, cg, K2, h, w) * valid[:, None]
            wy_ = wy[:, None]
            wx_ = wx[:, None]
            out = gather(y0, x0) * (1 - wy_) * (1 - wx_) + gather(y0, x0 + 1) * (1 - wy_) * wx_ + gather(y0 + 1, x0) * wy_ * (1 - wx_) + gather(y0 + 1, x0 + 1) * wy_ * wx_
            return out * mask[:, None]
        key = jax.random.key(seed)
        ks = jax.random.split(key, 14)
        d = {}
        d['x'] = jax.random.normal(ks[0], (B, H, W, C), jnp.float32)
        d['w_qkv'] = jax.random.normal(ks[1], (C, 3 * C), jnp.float32) * C ** (-0.5)
        d['b_qkv'] = jax.random.normal(ks[2], (3 * C,), jnp.float32) * 0.02
        d['w_dw'] = jax.random.normal(ks[3], (3 * C, 1, 3, 3), jnp.float32) * 0.2
        d['b_dw'] = jax.random.normal(ks[4], (3 * C,), jnp.float32) * 0.02
        d['pconv_off_w'] = jax.random.normal(ks[5], (G, C // 4, C // 4, 3, 3), jnp.float32) * 0.05
        d['w_off'] = jax.random.normal(ks[6], (G, 2 * K2, C), jnp.float32) * 0.01
        d['b_off'] = jax.random.normal(ks[7], (G, 2 * K2), jnp.float32) * 0.01
        d['pconv_mask_w'] = jax.random.normal(ks[8], (C // 4, C // 4, 3, 3), jnp.float32) * 0.05
        d['w_mask'] = jax.random.normal(ks[9], (K2, C), jnp.float32) * 0.01
        d['b_mask'] = jax.random.normal(ks[10], (K2,), jnp.float32) * 0.01
        d['w_proj'] = jax.random.normal(ks[11], (C, C), jnp.float32) * C ** (-0.5)
        d['b_proj'] = jax.random.normal(ks[12], (C,), jnp.float32) * 0.02
        return d
    _L0_conv_all = _L0_conv_setup()
    _L0_conv_in = {k: v for k, v in _L0_conv_all.items() if k in ('w_qkv', 'b_qkv', 'w_dw', 'b_dw', 'pconv_off_w', 'w_off', 'b_off', 'pconv_mask_w', 'w_mask', 'b_mask', 'w_proj', 'b_proj', )}
    del _L0_conv_all

    def _L1_conv_setup():
        import jax, jax.numpy as jnp
        import numpy as np
        B, H, W, C = (16, 96, 96, 128)
        FOCAL_LEVEL = 3
        FOCAL_WINDOW = 3
        FOCAL_FACTOR = 2
        LN_EPS = 0.001

        def dwconv_same(x, k):
            return jax.lax.conv_general_dilated(x, k, window_strides=(1, 1), padding='SAME', dimension_numbers=('NHWC', 'HWIO', 'NHWC'), feature_group_count=x.shape[-1])
        key = jax.random.key(seed)
        ks = jax.random.split(key, 12)
        s = 0.02
        out_f = 2 * C + (FOCAL_LEVEL + 1)
        inp = {'x': jax.random.normal(ks[0], (B, H, W, C), dtype=jnp.float32), 'Wf': jax.random.normal(ks[1], (C, out_f), dtype=jnp.float32) * s, 'bf': jnp.zeros((out_f,), dtype=jnp.float32), 'Wh': jax.random.normal(ks[2], (C, C), dtype=jnp.float32) * s, 'bh': jnp.zeros((C,), dtype=jnp.float32), 'gamma': jnp.ones((C,), dtype=jnp.float32), 'beta': jnp.zeros((C,), dtype=jnp.float32), 'Wp': jax.random.normal(ks[3], (C, C), dtype=jnp.float32) * s, 'bp': jnp.zeros((C,), dtype=jnp.float32)}
        for l in range(FOCAL_LEVEL):
            kk = FOCAL_FACTOR * l + FOCAL_WINDOW
            inp[f'k{l}'] = jax.random.normal(ks[4 + l], (kk, kk, 1, C), dtype=jnp.float32) * s
        return inp
    _L1_conv_all = _L1_conv_setup()
    _L1_conv_in = {k: v for k, v in _L1_conv_all.items() if k in ('Wf', 'bf', 'k0', 'k1', 'k2', 'Wh', 'bh', 'gamma', 'beta', 'Wp', 'bp', )}
    del _L1_conv_all

    def _L2_attn_setup():
        import jax, jax.numpy as jnp
        import numpy as np
        CHUNK = 64
        D_MODEL = 128
        D_STATE = 64
        HEADDIM = 64
        D_INNER = 2 * D_MODEL
        NHEADS = D_INNER // HEADDIM
        CONV_DIM = D_INNER + 2 * D_STATE
        K = 4
        D_IN_PROJ = 2 * D_INNER + 2 * D_STATE + NHEADS
        EPS = 1e-05

        def _segsum(t):
            L = t.shape[-1]
            cs = jnp.cumsum(t, -1)
            seg = cs[..., :, None] - cs[..., None, :]
            mask = jnp.tril(jnp.ones((L, L), bool))
            return jnp.where(mask, seg, -jnp.inf)

        def _ssd(xh, dt, A, Bm, Cm):
            b, l, h, p = xh.shape
            n = Bm.shape[-1]
            c = l // CHUNK
            xdt = xh * dt[..., None]
            dA = dt * A
            rc = lambda t: t.reshape(b, c, CHUNK, *t.shape[2:])
            xc, dAc, Bc, Cc = (rc(xdt), rc(dA), rc(Bm), rc(Cm))
            Acs = jnp.cumsum(dAc, axis=2)
            Lmat = jnp.exp(_segsum(dAc.transpose(0, 1, 3, 2)))
            Y_diag = jnp.einsum('bcln,bcsn,bchls,bcshp->bclhp', Cc, Bc, Lmat, xc)
            decay_st = jnp.exp(Acs[:, :, -1:, :] - Acs)
            states = jnp.einsum('bcln,bclh,bclhp->bchpn', Bc, decay_st, xc)
            chunk_decay = jnp.exp(Acs[:, :, -1])

            def step(carry, inp):
                st, dec = inp
                new = st + carry * dec[:, :, None, None]
                return (new, carry)
            init = jnp.zeros((b, h, p, n), xh.dtype)
            _, prev = jax.lax.scan(step, init, (states.transpose(1, 0, 2, 3, 4), chunk_decay.transpose(1, 0, 2)))
            prev = prev.transpose(1, 0, 2, 3, 4)
            Y_off = jnp.einsum('bcln,bchpn,bclh->bclhp', Cc, prev, jnp.exp(Acs))
            return (Y_diag + Y_off).reshape(b, l, h, p)

        def _mamba3(x, in_proj, conv_w, conv_b, A_log, dt_bias, D, norm_w, out_proj):
            b, l, _ = x.shape
            zxbcdt = x @ in_proj
            z, xbc, dt = jnp.split(zxbcdt, [D_INNER, D_INNER + CONV_DIM], axis=-1)
            xp = jnp.pad(xbc, ((0, 0), (K - 1, 0), (0, 0)))
            conv = sum((xp[:, i:i + l, :] * conv_w[:, i] for i in range(K))) + conv_b
            xbc = jax.nn.silu(conv)
            xh, Bm, Cm = jnp.split(xbc, [D_INNER, D_INNER + D_STATE], axis=-1)
            xh = xh.reshape(b, l, NHEADS, HEADDIM)
            dt = jax.nn.softplus(dt + dt_bias)
            A = -jnp.exp(A_log)
            y = _ssd(xh, dt, A, Bm, Cm) + xh * D[None, None, :, None]
            yg = y.reshape(b, l, D_INNER) * jax.nn.silu(z)
            yn = yg * jax.lax.rsqrt(jnp.mean(yg * yg, -1, keepdims=True) + EPS) * norm_w
            return yn @ out_proj
        key = jax.random.key(seed)
        ks = jax.random.split(key, 19)
        inp = {'x': jax.random.normal(ks[0], (16, 4096, D_MODEL), jnp.float32)}
        for i, pre in enumerate(['fwd', 'bwd']):
            o = 1 + 9 * i
            inp[pre + '_in_proj'] = jax.random.normal(ks[o], (D_MODEL, D_IN_PROJ), jnp.float32) * D_MODEL ** (-0.5)
            inp[pre + '_conv_w'] = jax.random.normal(ks[o + 1], (CONV_DIM, K), jnp.float32) * 0.3
            inp[pre + '_conv_b'] = jnp.zeros((CONV_DIM,), jnp.float32)
            inp[pre + '_A_log'] = jnp.log(jax.random.uniform(ks[o + 2], (NHEADS,), jnp.float32, 1.0, 16.0))
            inp[pre + '_dt_bias'] = jax.random.normal(ks[o + 3], (NHEADS,), jnp.float32) * 0.5
            inp[pre + '_D'] = jnp.ones((NHEADS,), jnp.float32)
            inp[pre + '_norm_w'] = jnp.ones((D_INNER,), jnp.float32)
            inp[pre + '_out_proj'] = jax.random.normal(ks[o + 4], (D_INNER, D_MODEL), jnp.float32) * D_INNER ** (-0.5)
        return inp
    _L2_attn_all = _L2_attn_setup()
    _L2_attn_in = {k: v for k, v in _L2_attn_all.items() if k in ('fwd_in_proj', 'fwd_conv_w', 'fwd_conv_b', 'fwd_A_log', 'fwd_dt_bias', 'fwd_D', 'fwd_norm_w', 'fwd_out_proj', 'bwd_in_proj', 'bwd_conv_w', 'bwd_conv_b', 'bwd_A_log', 'bwd_dt_bias', 'bwd_D', 'bwd_norm_w', 'bwd_out_proj', )}
    del _L2_attn_all

    def _L2_ffn_setup():
        import jax, jax.numpy as jnp
        import numpy as np
        B, N, D, C, E, K = (8, 8192, 128, 128, 8, 2)
        key = jax.random.key(seed)
        k0, k1, k2 = jax.random.split(key, 3)
        x = jax.random.normal(k0, (B, N, D), dtype=jnp.float32)
        router_w = jax.random.normal(k1, (D, E), dtype=jnp.float32) * 0.05
        router_b = jnp.zeros((E,), dtype=jnp.float32)
        expert_w = jax.random.normal(k2, (E, D, C), dtype=jnp.float32) * (1.0 / np.sqrt(D))
        expert_b = jnp.zeros((E, C), dtype=jnp.float32)
        return {'x': x, 'router_w': router_w, 'router_b': router_b, 'expert_w': expert_w, 'expert_b': expert_b}
    _L2_ffn_all = _L2_ffn_setup()
    _L2_ffn_in = {k: v for k, v in _L2_ffn_all.items() if k in ('router_w', 'router_b', 'expert_w', 'expert_b', )}
    del _L2_ffn_all

    def _L3_attn_setup():
        import jax, jax.numpy as jnp
        import numpy as np
        key = jax.random.key(seed)
        seq = jax.random.normal(key, (32, 2048, 128), dtype=jnp.float32)
        return {'seq': seq}
    _L3_attn_all = _L3_attn_setup()
    _L3_attn_in = {k: v for k, v in _L3_attn_all.items() if k in ()}
    del _L3_attn_all

    def _L3_ffn_setup():
        import jax, jax.numpy as jnp
        import numpy as np
        B, S, D, E, H, O, K = (512, 2048, 128, 64, 512, 128, 8)
        key = jax.random.key(seed)
        k0, k1, k2, k3 = jax.random.split(key, 4)
        x = jax.random.normal(k0, (B, S, D), dtype=jnp.float32)
        gate_w = jax.random.normal(k1, (E, D), dtype=jnp.float32) * (1.0 / np.sqrt(D))
        gate_b = jnp.zeros((E,), dtype=jnp.float32)
        weight1 = jax.random.uniform(k2, (E, D + 1, H), dtype=jnp.float32, minval=-1.0, maxval=1.0) * (1.0 / np.sqrt(D + 1))
        weight2 = jax.random.uniform(k3, (E, H + 1, O), dtype=jnp.float32, minval=-1.0, maxval=1.0) * (1.0 / np.sqrt(H + 1))
        return {'x': x, 'gate_w': gate_w, 'gate_b': gate_b, 'weight1': weight1, 'weight2': weight2}
    _L3_ffn_all = _L3_ffn_setup()
    _L3_ffn_in = {k: v for k, v in _L3_ffn_all.items() if k in ('gate_w', 'gate_b', 'weight1', 'weight2', )}
    del _L3_ffn_all

    return {
        "x": x,
        "L0_conv_w_qkv": _L0_conv_in["w_qkv"],
        "L0_conv_b_qkv": _L0_conv_in["b_qkv"],
        "L0_conv_w_dw": _L0_conv_in["w_dw"],
        "L0_conv_b_dw": _L0_conv_in["b_dw"],
        "L0_conv_pconv_off_w": _L0_conv_in["pconv_off_w"],
        "L0_conv_w_off": _L0_conv_in["w_off"],
        "L0_conv_b_off": _L0_conv_in["b_off"],
        "L0_conv_pconv_mask_w": _L0_conv_in["pconv_mask_w"],
        "L0_conv_w_mask": _L0_conv_in["w_mask"],
        "L0_conv_b_mask": _L0_conv_in["b_mask"],
        "L0_conv_w_proj": _L0_conv_in["w_proj"],
        "L0_conv_b_proj": _L0_conv_in["b_proj"],
        "L1_conv_Wf": _L1_conv_in["Wf"],
        "L1_conv_bf": _L1_conv_in["bf"],
        "L1_conv_k0": _L1_conv_in["k0"],
        "L1_conv_k1": _L1_conv_in["k1"],
        "L1_conv_k2": _L1_conv_in["k2"],
        "L1_conv_Wh": _L1_conv_in["Wh"],
        "L1_conv_bh": _L1_conv_in["bh"],
        "L1_conv_gamma": _L1_conv_in["gamma"],
        "L1_conv_beta": _L1_conv_in["beta"],
        "L1_conv_Wp": _L1_conv_in["Wp"],
        "L1_conv_bp": _L1_conv_in["bp"],
        "L2_attn_fwd_in_proj": _L2_attn_in["fwd_in_proj"],
        "L2_attn_fwd_conv_w": _L2_attn_in["fwd_conv_w"],
        "L2_attn_fwd_conv_b": _L2_attn_in["fwd_conv_b"],
        "L2_attn_fwd_A_log": _L2_attn_in["fwd_A_log"],
        "L2_attn_fwd_dt_bias": _L2_attn_in["fwd_dt_bias"],
        "L2_attn_fwd_D": _L2_attn_in["fwd_D"],
        "L2_attn_fwd_norm_w": _L2_attn_in["fwd_norm_w"],
        "L2_attn_fwd_out_proj": _L2_attn_in["fwd_out_proj"],
        "L2_attn_bwd_in_proj": _L2_attn_in["bwd_in_proj"],
        "L2_attn_bwd_conv_w": _L2_attn_in["bwd_conv_w"],
        "L2_attn_bwd_conv_b": _L2_attn_in["bwd_conv_b"],
        "L2_attn_bwd_A_log": _L2_attn_in["bwd_A_log"],
        "L2_attn_bwd_dt_bias": _L2_attn_in["bwd_dt_bias"],
        "L2_attn_bwd_D": _L2_attn_in["bwd_D"],
        "L2_attn_bwd_norm_w": _L2_attn_in["bwd_norm_w"],
        "L2_attn_bwd_out_proj": _L2_attn_in["bwd_out_proj"],
        "L2_ffn_router_w": _L2_ffn_in["router_w"],
        "L2_ffn_router_b": _L2_ffn_in["router_b"],
        "L2_ffn_expert_w": _L2_ffn_in["expert_w"],
        "L2_ffn_expert_b": _L2_ffn_in["expert_b"],
        "L3_ffn_gate_w": _L3_ffn_in["gate_w"],
        "L3_ffn_gate_b": _L3_ffn_in["gate_b"],
        "L3_ffn_weight1": _L3_ffn_in["weight1"],
        "L3_ffn_weight2": _L3_ffn_in["weight2"],
    }

def reference(x, L0_conv_w_qkv, L0_conv_b_qkv, L0_conv_w_dw, L0_conv_b_dw, L0_conv_pconv_off_w, L0_conv_w_off, L0_conv_b_off, L0_conv_pconv_mask_w, L0_conv_w_mask, L0_conv_b_mask, L0_conv_w_proj, L0_conv_b_proj, L1_conv_Wf, L1_conv_bf, L1_conv_k0, L1_conv_k1, L1_conv_k2, L1_conv_Wh, L1_conv_bh, L1_conv_gamma, L1_conv_beta, L1_conv_Wp, L1_conv_bp, L2_attn_fwd_in_proj, L2_attn_fwd_conv_w, L2_attn_fwd_conv_b, L2_attn_fwd_A_log, L2_attn_fwd_dt_bias, L2_attn_fwd_D, L2_attn_fwd_norm_w, L2_attn_fwd_out_proj, L2_attn_bwd_in_proj, L2_attn_bwd_conv_w, L2_attn_bwd_conv_b, L2_attn_bwd_A_log, L2_attn_bwd_dt_bias, L2_attn_bwd_D, L2_attn_bwd_norm_w, L2_attn_bwd_out_proj, L2_ffn_router_w, L2_ffn_router_b, L2_ffn_expert_w, L2_ffn_expert_b, L3_ffn_gate_w, L3_ffn_gate_b, L3_ffn_weight1, L3_ffn_weight2):
    import jax
    import jax.numpy as jnp
    def _L0_conv_ref(x, w_qkv, b_qkv, w_dw, b_dw, pconv_off_w, w_off, b_off, pconv_mask_w, w_mask, b_mask, w_proj, b_proj):
        import jax, jax.numpy as jnp
        import numpy as np
        B, H, W, C = (4, 64, 64, 128)
        G = 4
        HC = C // G
        K = 3
        K2 = K * K
        PAD = K // 2
        SCALE = HC ** (-0.5)

        def conv2d(x, w, padding=1, dilation=1, groups=1):
            return jax.lax.conv_general_dilated(x, w, (1, 1), [(padding, padding), (padding, padding)], rhs_dilation=(dilation, dilation), dimension_numbers=('NCHW', 'OIHW', 'NCHW'), feature_group_count=groups)

        def pconv(x, w):
            c4 = w.shape[0]
            return jnp.concatenate([conv2d(x[:, :c4], w, padding=1), x[:, c4:]], axis=1)

        def conv1x1(x, w, b):
            return jnp.einsum('bchw,oc->bohw', x, w) + b[None, :, None, None]

        def deform_sample(img, offset, mask, dilation, pad):
            b, cg, h, w = img.shape
            ky, kx = jnp.meshgrid(jnp.arange(K), jnp.arange(K), indexing='ij')
            base_y = (ky.reshape(-1) * dilation - pad).astype(img.dtype)
            base_x = (kx.reshape(-1) * dilation - pad).astype(img.dtype)
            off = offset.reshape(b, K2, 2, h, w)
            py = jnp.arange(h, dtype=img.dtype)[None, None, :, None] + base_y[None, :, None, None] + off[:, :, 0]
            px = jnp.arange(w, dtype=img.dtype)[None, None, None, :] + base_x[None, :, None, None] + off[:, :, 1]
            y0 = jnp.floor(py)
            x0 = jnp.floor(px)
            wy = py - y0
            wx = px - x0
            flat = img.reshape(b, cg, h * w)

            def gather(iy, ix):
                valid = ((iy >= 0) & (iy < h) & (ix >= 0) & (ix < w)).astype(img.dtype)
                idx = (jnp.clip(iy, 0, h - 1) * w + jnp.clip(ix, 0, w - 1)).astype(jnp.int32)
                g = jax.vmap(lambda f, i: jnp.take(f, i, axis=1))(flat, idx.reshape(b, -1))
                return g.reshape(b, cg, K2, h, w) * valid[:, None]
            wy_ = wy[:, None]
            wx_ = wx[:, None]
            out = gather(y0, x0) * (1 - wy_) * (1 - wx_) + gather(y0, x0 + 1) * (1 - wy_) * wx_ + gather(y0 + 1, x0) * wy_ * (1 - wx_) + gather(y0 + 1, x0 + 1) * wy_ * wx_
            return out * mask[:, None]
        b, h, w, c = x.shape
        n = h * w
        qkv = x @ w_qkv + b_qkv
        qkv = conv2d(qkv.transpose(0, 3, 1, 2), w_dw, padding=1, groups=3 * c) + b_dw[None, :, None, None]
        qkv = qkv.transpose(0, 2, 3, 1)
        q = qkv[..., :c]
        kv = qkv[..., c:].reshape(b, h, w, 2, G, HC).transpose(3, 0, 4, 5, 1, 2)
        q_img = q.transpose(0, 3, 1, 2)
        mask = jax.nn.sigmoid(conv1x1(pconv(q_img, pconv_mask_w), w_mask, b_mask))
        k_list, v_list = ([], [])
        for i in range(G):
            off = conv1x1(pconv(q_img, pconv_off_w[i]), w_off[i], b_off[i])
            dil = 2 * i + 1
            k_list.append(deform_sample(kv[0, :, i], off, mask, dil, dil * PAD))
            v_list.append(deform_sample(kv[1, :, i], off, mask, dil, dil * PAD))
        ks_ = jnp.stack(k_list, 1).reshape(b, G, HC, K2, n)
        vs_ = jnp.stack(v_list, 1).reshape(b, G, HC, K2, n)
        qf = (q.reshape(b, n, G, HC) * SCALE).transpose(0, 2, 1, 3)
        attn = jax.nn.softmax(jnp.einsum('bgnc,bgckn->bgnk', qf, ks_), axis=-1)
        out = jnp.einsum('bgnk,bgckn->bgnc', attn, vs_)
        out = out.transpose(0, 2, 1, 3).reshape(b, h, w, c)
        return out @ w_proj + b_proj

    def _L1_conv_ref(x, Wf, bf, k0, k1, k2, Wh, bh, gamma, beta, Wp, bp):
        import jax, jax.numpy as jnp
        import numpy as np
        B, H, W, C = (16, 96, 96, 128)
        FOCAL_LEVEL = 3
        FOCAL_WINDOW = 3
        FOCAL_FACTOR = 2
        LN_EPS = 0.001

        def dwconv_same(x, k):
            return jax.lax.conv_general_dilated(x, k, window_strides=(1, 1), padding='SAME', dimension_numbers=('NHWC', 'HWIO', 'NHWC'), feature_group_count=x.shape[-1])
        gelu = lambda t: jax.nn.gelu(t, approximate=False)
        y = jnp.einsum('bhwc,cd->bhwd', x, Wf) + bf
        q = y[..., :C]
        ctx = y[..., C:2 * C]
        gates = y[..., 2 * C:]
        ctx_all = jnp.zeros_like(ctx)
        for l, k in enumerate((k0, k1, k2)):
            ctx = gelu(dwconv_same(ctx, k))
            ctx_all = ctx_all + ctx * gates[..., l:l + 1]
        ctx_global = gelu(jnp.mean(ctx, axis=(1, 2), keepdims=True))
        ctx_all = ctx_all + ctx_global * gates[..., FOCAL_LEVEL:]
        modulator = jnp.einsum('bhwc,cd->bhwd', ctx_all, Wh) + bh
        x_out = q * modulator
        mu = jnp.mean(x_out, axis=-1, keepdims=True)
        var = jnp.mean(jnp.square(x_out - mu), axis=-1, keepdims=True)
        x_out = (x_out - mu) * jax.lax.rsqrt(var + LN_EPS) * gamma + beta
        x_out = jnp.einsum('bhwc,cd->bhwd', x_out, Wp) + bp
        return x_out

    def _L2_attn_ref(x, fwd_in_proj, fwd_conv_w, fwd_conv_b, fwd_A_log, fwd_dt_bias, fwd_D, fwd_norm_w, fwd_out_proj, bwd_in_proj, bwd_conv_w, bwd_conv_b, bwd_A_log, bwd_dt_bias, bwd_D, bwd_norm_w, bwd_out_proj):
        import jax, jax.numpy as jnp
        import numpy as np
        CHUNK = 64
        D_MODEL = 128
        D_STATE = 64
        HEADDIM = 64
        D_INNER = 2 * D_MODEL
        NHEADS = D_INNER // HEADDIM
        CONV_DIM = D_INNER + 2 * D_STATE
        K = 4
        D_IN_PROJ = 2 * D_INNER + 2 * D_STATE + NHEADS
        EPS = 1e-05

        def _segsum(t):
            L = t.shape[-1]
            cs = jnp.cumsum(t, -1)
            seg = cs[..., :, None] - cs[..., None, :]
            mask = jnp.tril(jnp.ones((L, L), bool))
            return jnp.where(mask, seg, -jnp.inf)

        def _ssd(xh, dt, A, Bm, Cm):
            b, l, h, p = xh.shape
            n = Bm.shape[-1]
            c = l // CHUNK
            xdt = xh * dt[..., None]
            dA = dt * A
            rc = lambda t: t.reshape(b, c, CHUNK, *t.shape[2:])
            xc, dAc, Bc, Cc = (rc(xdt), rc(dA), rc(Bm), rc(Cm))
            Acs = jnp.cumsum(dAc, axis=2)
            Lmat = jnp.exp(_segsum(dAc.transpose(0, 1, 3, 2)))
            Y_diag = jnp.einsum('bcln,bcsn,bchls,bcshp->bclhp', Cc, Bc, Lmat, xc)
            decay_st = jnp.exp(Acs[:, :, -1:, :] - Acs)
            states = jnp.einsum('bcln,bclh,bclhp->bchpn', Bc, decay_st, xc)
            chunk_decay = jnp.exp(Acs[:, :, -1])

            def step(carry, inp):
                st, dec = inp
                new = st + carry * dec[:, :, None, None]
                return (new, carry)
            init = jnp.zeros((b, h, p, n), xh.dtype)
            _, prev = jax.lax.scan(step, init, (states.transpose(1, 0, 2, 3, 4), chunk_decay.transpose(1, 0, 2)))
            prev = prev.transpose(1, 0, 2, 3, 4)
            Y_off = jnp.einsum('bcln,bchpn,bclh->bclhp', Cc, prev, jnp.exp(Acs))
            return (Y_diag + Y_off).reshape(b, l, h, p)

        def _mamba3(x, in_proj, conv_w, conv_b, A_log, dt_bias, D, norm_w, out_proj):
            b, l, _ = x.shape
            zxbcdt = x @ in_proj
            z, xbc, dt = jnp.split(zxbcdt, [D_INNER, D_INNER + CONV_DIM], axis=-1)
            xp = jnp.pad(xbc, ((0, 0), (K - 1, 0), (0, 0)))
            conv = sum((xp[:, i:i + l, :] * conv_w[:, i] for i in range(K))) + conv_b
            xbc = jax.nn.silu(conv)
            xh, Bm, Cm = jnp.split(xbc, [D_INNER, D_INNER + D_STATE], axis=-1)
            xh = xh.reshape(b, l, NHEADS, HEADDIM)
            dt = jax.nn.softplus(dt + dt_bias)
            A = -jnp.exp(A_log)
            y = _ssd(xh, dt, A, Bm, Cm) + xh * D[None, None, :, None]
            yg = y.reshape(b, l, D_INNER) * jax.nn.silu(z)
            yn = yg * jax.lax.rsqrt(jnp.mean(yg * yg, -1, keepdims=True) + EPS) * norm_w
            return yn @ out_proj
        h_f = _mamba3(x, fwd_in_proj, fwd_conv_w, fwd_conv_b, fwd_A_log, fwd_dt_bias, fwd_D, fwd_norm_w, fwd_out_proj)
        xr = x[:, ::-1, :]
        h_b = _mamba3(xr, bwd_in_proj, bwd_conv_w, bwd_conv_b, bwd_A_log, bwd_dt_bias, bwd_D, bwd_norm_w, bwd_out_proj)[:, ::-1, :]
        return h_f + h_b

    def _L2_ffn_ref(x, router_w, router_b, expert_w, expert_b):
        import jax, jax.numpy as jnp
        import numpy as np
        B, N, D, C, E, K = (8, 8192, 128, 128, 8, 2)
        router_probs = jax.nn.softmax(x @ router_w + router_b, axis=-1)
        top_p, top_i = jax.lax.top_k(router_probs, K)
        top_p = top_p / jnp.sum(top_p, axis=-1, keepdims=True)
        expert_out = jnp.einsum('bnd,edc->bnec', x, expert_w) + expert_b
        gathered = jnp.take_along_axis(expert_out, top_i[..., None], axis=2)
        return jnp.einsum('bnk,bnkc->bnc', top_p, gathered)

    def _L3_attn_ref(seq):
        import jax, jax.numpy as jnp
        import numpy as np
        attn = jnp.einsum('blc,bmc->blm', seq, seq)
        attn = jax.nn.softmax(attn, axis=2)
        out = jnp.einsum('blm,bmc->blc', attn, seq)
        return out

    def _L3_ffn_ref(x, gate_w, gate_b, weight1, weight2):
        import jax, jax.numpy as jnp
        import numpy as np
        B, S, D, E, H, O, K = (512, 2048, 128, 64, 512, 128, 8)
        Bn, Sn, Dn = x.shape
        logits = jnp.einsum('bsd,ed->bse', x, gate_w) + gate_b
        probs = jax.nn.softmax(logits, axis=1)
        vals, idx = jax.lax.top_k(probs.transpose(0, 2, 1), K)
        topv = vals.transpose(0, 2, 1)
        topi = idx.transpose(0, 2, 1)
        flat_idx = topi.reshape(Bn, K * E)
        gathered = jnp.take_along_axis(x, flat_idx[:, :, None], axis=1)
        gathered = gathered.reshape(Bn, K, E, Dn)
        pooled = jnp.einsum('bked,bke->bed', gathered, topv)
        ones = jnp.ones((E, Bn, 1), dtype=x.dtype)
        h = jnp.concatenate([pooled.transpose(1, 0, 2), ones], axis=-1)
        h = jax.nn.gelu(jnp.einsum('ebd,edh->ebh', h, weight1), approximate=False)
        h = jnp.concatenate([h, ones], axis=-1)
        out = jnp.einsum('ebh,eho->ebo', h, weight2)
        out = out.transpose(1, 0, 2)
        weighted = jnp.einsum('beo,bke->bkeo', out, topv).reshape(Bn, K * E, O)
        outputs = jnp.zeros((Bn, Sn, O), dtype=x.dtype)
        outputs = outputs.at[jnp.arange(Bn)[:, None], flat_idx].add(weighted)
        return outputs

    def _gn(v, G=32, eps=1e-5):
        B_, H_, W_, C_ = v.shape
        g = v.reshape(B_, H_, W_, G, C_ // G)
        m = jnp.mean(g, axis=(1, 2, 4), keepdims=True)
        s = jnp.var(g, axis=(1, 2, 4), keepdims=True)
        return ((g - m) / jnp.sqrt(s + eps)).reshape(v.shape)

    def _ln_c(v, eps=1e-6):
        m = jnp.mean(v, axis=-1, keepdims=True)
        s = jnp.var(v, axis=-1, keepdims=True)
        return (v - m) / jnp.sqrt(s + eps)

    def _ln_t(v, eps=1e-5):
        m = jnp.mean(v, axis=-1, keepdims=True)
        s = jnp.var(v, axis=-1, keepdims=True)
        return (v - m) / jnp.sqrt(s + eps)

    def _to_tokens(v):
        B_, H_, W_, C_ = v.shape
        return v.reshape(B_, H_ * W_, C_)
    def _from_tokens(t, like):
        return t.reshape(like.shape)

    x = x + _L0_conv_ref(_gn(x), L0_conv_w_qkv, L0_conv_b_qkv, L0_conv_w_dw, L0_conv_b_dw, L0_conv_pconv_off_w, L0_conv_w_off, L0_conv_b_off, L0_conv_pconv_mask_w, L0_conv_w_mask, L0_conv_b_mask, L0_conv_w_proj, L0_conv_b_proj)
    x = x + _L1_conv_ref(_gn(x), L1_conv_Wf, L1_conv_bf, L1_conv_k0, L1_conv_k1, L1_conv_k2, L1_conv_Wh, L1_conv_bh, L1_conv_gamma, L1_conv_beta, L1_conv_Wp, L1_conv_bp)
    t = _to_tokens(x)
    t = t + _L2_attn_ref(_ln_t(t), L2_attn_fwd_in_proj, L2_attn_fwd_conv_w, L2_attn_fwd_conv_b, L2_attn_fwd_A_log, L2_attn_fwd_dt_bias, L2_attn_fwd_D, L2_attn_fwd_norm_w, L2_attn_fwd_out_proj, L2_attn_bwd_in_proj, L2_attn_bwd_conv_w, L2_attn_bwd_conv_b, L2_attn_bwd_A_log, L2_attn_bwd_dt_bias, L2_attn_bwd_D, L2_attn_bwd_norm_w, L2_attn_bwd_out_proj)
    t = t + _L2_ffn_ref(_ln_t(t), L2_ffn_router_w, L2_ffn_router_b, L2_ffn_expert_w, L2_ffn_expert_b)
    t = t + _L3_attn_ref(_ln_t(t))
    t = t + _L3_ffn_ref(_ln_t(t), L3_ffn_gate_w, L3_ffn_gate_b, L3_ffn_weight1, L3_ffn_weight2)
    x = _from_tokens(t, x)
    return x


_drawn_inputs = setup_inputs


def setup_inputs(seed=0):
    import zlib

    import numpy as np

    out = dict(_drawn_inputs(seed))
    spreads = {'L1_conv_bf': (0.0, 0.1),
     'L1_conv_bh': (0.0, 0.1),
     'L1_conv_gamma': (1.0, 0.2),
     'L1_conv_beta': (0.0, 0.1),
     'L1_conv_bp': (0.0, 0.1),
     'L2_attn_fwd_conv_b': (0.0, 0.1),
     'L2_attn_fwd_D': (1.0, 0.2),
     'L2_attn_fwd_norm_w': (1.0, 0.2),
     'L2_attn_bwd_conv_b': (0.0, 0.1),
     'L2_attn_bwd_D': (1.0, 0.2),
     'L2_attn_bwd_norm_w': (1.0, 0.2),
     'L2_ffn_router_b': (0.0, 0.1),
     'L2_ffn_expert_b': (0.0, 0.1),
     'L3_ffn_gate_b': (0.0, 0.1)}
    factors = {'L0_conv_b_off': 4.323,
     'L0_conv_pconv_mask_w': 5.301,
     'L1_conv_k0': 6.003,
     'L1_conv_k1': 8.0,
     'L1_conv_k2': 8.0,
     'L1_conv_Wh': 7.034,
     'L3_ffn_gate_w': 8.0,
     'L3_ffn_weight1': 8.0,
     'L3_ffn_weight2': 8.0}
    for name, (base, spread) in spreads.items():
        noise = np.random.default_rng([zlib.crc32(name.encode()), seed]).standard_normal(out[name].shape)
        drawn = base * np.exp(spread * noise) if base else spread * noise
        out[name] = jnp.asarray(drawn.astype(out[name].dtype))
    for name, factor in factors.items():
        out[name] = (out[name] * factor).astype(out[name].dtype)
    return out
```

```python
from contextlib import ExitStack

import concourse.bass as bass
import numpy as np
from concourse import mybir

F32 = mybir.dt.float32
I32 = mybir.dt.int32
U32 = mybir.dt.uint32
ACT = mybir.ActivationFunctionType
ALU = mybir.AluOpType
AX = mybir.AxisListType

B, H, W, C = 4, 64, 64, 128
N = H * W
P = 128
T = N // P
BANK = 512
NB = N // BANK
ROWS = BANK // W

G, K2 = 4, 9
HC = C // G
GK = G * K2
NOFF = 2 * GK + K2
SCALE = HC ** -0.5
YT, XT = H + 2, W + 3
POS = YT * XT
PK_W, PK_I = C, C + 4 * GK
PK = C + 5 * GK



LOADS = 4


def load_tokens(engine, dst, src, b, loaded):
    h = T // LOADS
    for n in range(LOADS):
        tokens = src[bass.ds(b, 1), n * h * P:(n + 1) * h * P, :].rearrange("a (t p) c -> p (a t) c", p=P)
        engine.dma_start(dst[:, n * h:(n + 1) * h, :], tokens).then_inc(loaded, 16)


class Scope:

    def __init__(self, nc, stage, stack):
        self.nc, self.stage, self.stack, self.sems = nc, stage, stack, []

    def sb(self, name, shape, dt=F32):
        return self.stack.enter_context(self.nc.sbuf_tensor(f"{self.stage}_{name}", shape, dt))

    def ps(self, name, shape=(P, BANK)):
        return self.stack.enter_context(self.nc.psum_tensor(f"{self.stage}_{name}", list(shape), F32))

    def sem(self, name):
        handle = self.stack.enter_context(self.nc.semaphore(f"{self.stage}_{name}"))
        self.sems.append(handle)
        return handle

    def block(self):
        self.stack.callback(self.clear)
        return self.stack.enter_context(self.nc.Block())

    def clear(self):
        numbers = sorted(x.num for x in self.sems)
        first = numbers[0]
        for number, following in zip(numbers, numbers[1:] + [None]):
            if following != number + 1:
                self.nc.sync.sem_clear(range(first, number + 1))
                first = following
        self.nc.all_engine_barrier()


def group_norm_vector(nc, dve, xT, stats, gn, chain, moments, group_mean, group_var, var_ready, std_ready, mean_ps, var_ps):
    for n in range(NB):
        ins = nc.vector.bn_stats(stats[:, n, :], xT[:, n * BANK:(n + 1) * BANK])
    ins.then_inc(chain, 1)
    dve.wait_ge(chain, 1)
    dve.sem_inc(chain, -1)
    nc.vector.bn_aggr(gn[:, 0:2], stats[:]).then_inc(chain, 1)
    dve.wait_ge(chain, 1)
    dve.sem_inc(chain, -1)
    dve.sem_inc(moments, 1)
    dve.wait_ge(group_mean, 1)
    dve.sem_inc(group_mean, -1)
    nc.vector.tensor_copy(gn[:, 2:3], mean_ps).then_inc(chain, 1)
    dve.wait_ge(chain, 1)
    dve.sem_inc(chain, -1)
    nc.vector.tensor_tensor(gn[:, 3:4], gn[:, 0:1], gn[:, 2:3], ALU.subtract).then_inc(chain, 1)
    dve.wait_ge(chain, 1)
    dve.sem_inc(chain, -1)
    nc.vector.tensor_tensor(gn[:, 4:5], gn[:, 3:4], gn[:, 3:4], ALU.mult).then_inc(chain, 1)
    dve.wait_ge(chain, 1)
    dve.sem_inc(chain, -1)
    nc.vector.tensor_tensor(gn[:, 4:5], gn[:, 4:5], gn[:, 1:2], ALU.add).then_inc(chain, 1)
    dve.wait_ge(chain, 1)
    dve.sem_inc(chain, -1)
    dve.sem_inc(moments, 1)
    dve.wait_ge(group_var, 1)
    dve.sem_inc(group_var, -1)
    nc.vector.tensor_scalar(gn[:, 5:6], var_ps, 1e-5, None, ALU.add).then_inc(chain, 1)
    dve.wait_ge(chain, 1)
    dve.sem_inc(chain, -1)
    nc.vector.reciprocal(gn[:, 5:6], gn[:, 5:6]).then_inc(chain, 1)
    dve.wait_ge(chain, 1)
    dve.sem_inc(chain, -1)
    dve.sem_inc(var_ready, 1)
    dve.wait_ge(std_ready, 1)
    dve.sem_inc(std_ready, -1)
    nc.vector.tensor_scalar(xT[:], xT[:], gn[:, 2:3], gn[:, 6:7], ALU.subtract, ALU.mult).then_inc(chain, 1)
    dve.wait_ge(chain, 1)
    dve.sem_inc(chain, -1)


def group_norm_tensor(nc, pe, group, gn, moments, group_mean, group_var, mean_ps, var_ps):
    pe.wait_ge(moments, 1)
    pe.sem_inc(moments, -1)
    nc.tensor.matmul(mean_ps, group[:], gn[:, 0:1], start=True, stop=True).then_inc(group_mean, 1)
    pe.wait_ge(moments, 1)
    pe.sem_inc(moments, -1)
    nc.tensor.matmul(var_ps, group[:], gn[:, 4:5], start=True, stop=True).then_inc(group_var, 1)


def layer0_prepare(nc, x, w, records, table):
    with ExitStack() as stack:
        s = Scope(nc, "l0a", stack)
        ident, group = s.sb("ident", [P, P]), s.sb("group", [P, P])
        w_qkv, b_qkv = s.sb("w_qkv", [P, 3 * C]), s.sb("b_qkv", [P, 3])
        w_dw, b_dw = s.sb("w_dw", [P, 3, K2]), s.sb("b_dw", [P, 3])
        w_off, w_pconv = s.sb("w_off", [P, NOFF]), s.sb("w_pconv", [HC, 5, K2, HC])
        QROWS = 3 * HC + 1
        w_shift = s.sb("w_shift", [QROWS, 3, NOFF])
        base, row0 = s.sb("base", [P, T, 2 * GK]), s.sb("row0", [P, GK])
        zeros = s.sb("zeros", [P, 2 * 2 * C])
        xt, xT = s.sb("xt", [P, T, C]), s.sb("xT", [P, N])
        stats, gn = s.sb("stats", [P, NB, 6]), s.sb("gn", [P, 8])
        diag = s.sb("diag", [P, K2, P])
        padded = [s.sb(f"padded{n}", [P, H + 2, W + 2]) for n in range(2)]
        q_shift = s.sb("q_shift", [QROWS, H + 2, W])
        q_img, k_img, v_img = s.sb("q_img", [P, N]), s.sb("k_img", [P, N]), s.sb("v_img", [P, N])
        off = s.sb("off", [P, T, NOFF])
        rec = s.sb("rec", [P, T, PK])
        kv = xt[:].rearrange("p t c -> p (t c)").rearrange("p (t c) -> p t c", t=T // 2)
        ps = [s.ps(f"ps{n}") for n in range(2)]
        ps_off, ps_tr = [s.ps(f"ps_off{n}") for n in range(2)], [s.ps(f"ps_tr{n}") for n in range(2)]
        ps_small = s.ps("ps_small")
        mean_ps, var_ps = ps_small[:, 0:1], ps_small[:, 1:2]

        consts, tap_ready, taps_used = s.sem("consts"), s.sem("tap_ready"), s.sem("taps_used")
        x_loaded, xt_free, kv_free = s.sem("x_loaded"), s.sem("xt_free"), s.sem("kv_free")
        ps_ready, ps_free = s.sem("ps_ready"), s.sem("ps_free")
        off_ready, off_free = s.sem("off_ready"), s.sem("off_free")
        tr_ready, tr_free = s.sem("tr_ready"), s.sem("tr_free")
        xT_ready, normed = s.sem("xT_ready"), s.sem("normed")
        moments, group_mean, group_var = s.sem("moments"), s.sem("group_mean"), s.sem("group_var")
        var_ready, std_ready = s.sem("var_ready"), s.sem("std_ready")
        dve_chain, act_chain = s.sem("dve_chain"), s.sem("act_chain")
        padded_ready = [s.sem("padded_ready0"), s.sem("padded_ready1")]
        v_padded_ready, padded_free = s.sem("v_padded_ready"), [s.sem("padded_free0"), s.sem("padded_free1")]
        v_ready, diag_ready = s.sem("v_ready"), s.sem("diag_ready")
        images_ready = s.sem("images_ready")
        images_free, v_free = s.sem("images_free"), s.sem("v_free")
        kv_ready, kv_stored = s.sem("kv_ready"), s.sem("kv_stored")
        evacuated, mask_in, mask_out = s.sem("evacuated"), s.sem("mask_in"), s.sem("mask_out")
        rec_ready, rec_free, borders, rec_stored = s.sem("rec_ready"), s.sem("rec_free"), s.sem("borders"), s.sem("rec_stored")
        zero_ready, shift_zero = s.sem("zero_ready"), s.sem("shift_zero")
        q_ready, shift_ready, shift_free = s.sem("q_ready"), s.sem("shift_ready"), s.sem("shift_free")
        block = s.block()

        loads = [(ident, w["ident"]), (group, w["group"]), (w_qkv, w["w_qkv"]), (b_qkv, w["b_qkv"]), (w_dw, w["w_dw"]),
                 (b_dw, w["b_dw"]), (w_off, w["w_off"]), (w_pconv, w["w_pconv"]), (base, w["base"]), (row0, w["row0"])]
        NC = 16 * (len(loads) + 1)

        @block.sync
        def _(sp):
            for dst, src in loads:
                sp.dma_start(dst[:], src).then_inc(consts, 16)
            sp.wait_ge(shift_zero, 1)
            sp.dma_start(w_shift[3 * HC:QROWS, 0, :], w["b_off"]).then_inc(consts, 16)
            sp.wait_ge(zero_ready, 1)
            cells = table.rearrange("(i y x) c -> i y x c", i=B * G, y=YT)
            z = zeros[0:YT, :]
            n = 0
            for i in range(B * G):
                sp.dma_start(cells[i, :, 0, :], z[:, 0:C]).then_inc(borders, 16)
                sp.dma_start(cells[i, :, XT - 2:XT, :].rearrange("y x c -> y (x c)"), z[:, 0:2 * C]).then_inc(borders, 16)
                sp.dma_start(cells[i, 0, 1:XT - 2, 0:64], zeros[0:W, 0:64]).then_inc(borders, 16)
                sp.dma_start(cells[i, YT - 2, 1:XT - 2, 64:128], zeros[0:W, 0:64]).then_inc(borders, 16)
                sp.dma_start(cells[i, YT - 1, 1:XT - 2, :], zeros[0:W, 0:C]).then_inc(borders, 16)
                n += 5
            sp.wait_ge(borders, 16 * n)
            half_rows = T // 2 * 2
            with sp.Fori(0, B) as b:
                sp.wait_ge(xt_free, 1)
                sp.sem_inc(xt_free, -1)
                load_tokens(sp, xt, x, b, x_loaded)
                for half in range(2):
                    sp.wait_ge(kv_ready, 1)
                    sp.sem_inc(kv_ready, -1)
                    cells_b = table[bass.ds(b * (G * POS), G * POS), :].rearrange("(g y x) c -> g y x c", g=G, y=YT)
                    for g in range(G):
                        for r in range(2):
                            src = kv[r * W:(r + 1) * W, :, g * 64:(g + 1) * 64]
                            for slot in range(2):
                                y0 = half * half_rows + r + 1 - slot
                                dst = cells_b[g, y0:y0 + half_rows - 1:2, 1:1 + W, slot * 64:(slot + 1) * 64]
                                sp.dma_start(dst.rearrange("y x c -> x y c"), src).then_inc(kv_stored, 16)
                    sp.wait_ge(kv_stored, 16 * 16)
                    sp.sem_inc(kv_stored, -16 * 16)
                    sp.sem_inc([kv_free, xt_free][half], 1)
                sp.wait_ge(rec_ready, 1)
                sp.sem_inc(rec_ready, -1)
                sp.dma_start(records[bass.ds(b, 1)].rearrange("a p f -> p (a f)"), rec[:].rearrange("p t f -> p (t f)")).then_inc(rec_stored, 16)
                sp.wait_ge(rec_stored, 16)
                sp.sem_inc(rec_stored, -16)
                sp.sem_inc(rec_free, 1)

        q_rows = q_shift[:].rearrange("p y x -> p (y x)")

        @block.tensor
        def _(pe):
            pe.wait_ge(consts, NC)
            for tap in range(K2):
                dst = ps_off[tap // 5][0:HC, tap % 5 * NOFF:(tap % 5 + 1) * NOFF]
                for i in range(G):
                    yx = dst[:, 0:2 * GK].rearrange("p (d n) -> p d n", d=2)[:, :, i * K2:(i + 1) * K2]
                    wyx = w_off[0:HC, 0:2 * GK].rearrange("p (d n) -> p d n", d=2)[:, :, i * K2:(i + 1) * K2]
                    nc.tensor.matmul(yx, w_pconv[:, i, tap, :], wyx, start=True, stop=True)
                ins = nc.tensor.matmul(dst[:, 2 * GK:], w_pconv[:, G, tap, :], w_off[0:HC, 2 * GK:], start=True, stop=True)
            ins.then_inc(tap_ready, 1)
            pe.wait_ge(taps_used, 1)
            pe.wait_ge(diag_ready, 1)
            with pe.Fori(0, B) as b:
                pe.wait_ge(x_loaded, 16 * LOADS)
                pe.sem_inc(x_loaded, -16 * LOADS)
                for n in range(NB):
                    pe.wait_ge(ps_free, 1)
                    pe.sem_inc(ps_free, -1)
                    for t in range(4):
                        ins = nc.tensor.transpose(ps[n % 2][:, t * P:(t + 1) * P], xt[:, 4 * n + t, :], ident[:])
                    ins.then_inc(ps_ready, 1)
                group_norm_tensor(nc, pe, group, gn, moments, group_mean, group_var, mean_ps, var_ps)
                pe.wait_ge(normed, 1)
                pe.sem_inc(normed, -1)
                for j in range(3):
                    for n in range(NB):
                        pe.wait_ge(ps_free, 1)
                        pe.sem_inc(ps_free, -1)
                        nc.tensor.matmul(ps[n % 2][:], w_qkv[:, j * C:(j + 1) * C], xT[:, n * BANK:(n + 1) * BANK],
                                         start=True, stop=True).then_inc(ps_ready, 1)
                pe.wait_ge(v_padded_ready, 1)
                pe.sem_inc(v_padded_ready, -1)
                for n in range(NB):
                    pe.wait_ge(ps_free, 1)
                    pe.sem_inc(ps_free, -1)
                    for tap in range(K2):
                        y, xx = n * ROWS + tap // 3, tap % 3
                        ins = nc.tensor.matmul(ps[n % 2][:], diag[:, tap, :], padded[0][:, y:y + ROWS, xx:xx + W],
                                               start=(tap == 0), stop=(tap == K2 - 1))
                    ins.then_inc(ps_ready, 1)
                pe.wait_ge(images_ready, 2)
                pe.sem_inc(images_ready, -2)
                pe.wait_ge(v_ready, 1)
                pe.sem_inc(v_ready, -1)
                pe.wait_ge(shift_ready, 1)
                pe.sem_inc(shift_ready, -1)
                for t in range(T):
                        k = t % 2
                        pe.wait_ge(off_free, 1)
                        pe.sem_inc(off_free, -1)
                        nc.tensor.matmul(ps_off[k][:, 0:NOFF], q_img[:, t * P:(t + 1) * P], w_off[:], start=True, stop=False)
                        for dy in range(3):
                            ins = nc.tensor.matmul(ps_off[k][:, 0:NOFF], q_rows[:, t * P + dy * W:t * P + dy * W + P], w_shift[:, dy, :],
                                                   start=False, stop=(dy == 2))
                        ins.then_inc(off_ready, 1)
                        pe.wait_ge(tr_free, 1)
                        pe.sem_inc(tr_free, -1)
                        nc.tensor.transpose(ps_tr[k][:, 0:C], q_img[:, t * P:(t + 1) * P], ident[:])
                        nc.tensor.transpose(ps_tr[k][:, C:2 * C], k_img[:, t * P:(t + 1) * P], ident[:])
                        nc.tensor.transpose(ps_tr[k][:, 2 * C:3 * C], v_img[:, t * P:(t + 1) * P],
                                            ident[:]).then_inc(tr_ready, 1)

        @block.scalar
        def _(act):
            act.sem_inc(ps_free, 2)
            act.sem_inc(off_free, 2)
            act.sem_inc(tr_free, 2)
            act.wait_ge(consts, NC)
            with act.Fori(0, B) as b:
                for n in range(NB):
                    act.wait_ge(ps_ready, 1)
                    act.sem_inc(ps_ready, -1)
                    nc.scalar.copy(xT[:, n * BANK:(n + 1) * BANK], ps[n % 2][:]).then_inc(act_chain, 1)
                    act.wait_ge(act_chain, 1)
                    act.sem_inc(act_chain, -1)
                    act.sem_inc(ps_free, 1)
                act.sem_inc(xT_ready, 1)
                act.wait_ge(var_ready, 1)
                act.sem_inc(var_ready, -1)
                nc.scalar.activation(gn[:, 6:7], gn[:, 5:6], ACT.Sqrt).then_inc(std_ready, 1)
                for j in range(3):
                    act.wait_ge(padded_free[j % 2], 1)
                    act.sem_inc(padded_free[j % 2], -1)
                    for n in range(NB):
                        act.wait_ge(ps_ready, 1)
                        act.sem_inc(ps_ready, -1)
                        dst = padded[j % 2][:, 1 + n * ROWS:1 + (n + 1) * ROWS, 1:1 + W]
                        src = ps[n % 2][:].rearrange("p (y x) -> p y x", x=W)
                        nc.scalar.activation(dst, src, ACT.Identity, bias=b_qkv[:, j:j + 1]).then_inc(act_chain, 1)
                        act.wait_ge(act_chain, 1)
                        act.sem_inc(act_chain, -1)
                        act.sem_inc(ps_free, 1)
                    act.sem_inc([padded_ready[0], v_padded_ready, padded_ready[1]][[0, 2, 1][j]], 1)
                for n in range(NB):
                    act.wait_ge(ps_ready, 1)
                    act.sem_inc(ps_ready, -1)
                    nc.scalar.activation(v_img[:, n * BANK:(n + 1) * BANK], ps[n % 2][:], ACT.Identity, bias=b_dw[:, 2:3]).then_inc(act_chain, 1)
                    act.wait_ge(act_chain, 1)
                    act.sem_inc(act_chain, -1)
                    act.sem_inc(ps_free, 1)
                act.sem_inc(v_ready, 1)
                act.sem_inc(padded_free[0], 1)
                act.wait_ge(q_ready, 1)
                act.sem_inc(q_ready, -1)
                q3 = q_img[0:HC, :].rearrange("p (y x) -> p y x", x=W)
                nc.scalar.copy(q_shift[0:HC, 1:1 + H, 1:W], q3[:, :, 0:W - 1])
                nc.scalar.copy(q_shift[HC:2 * HC, 1:1 + H, :], q3)
                nc.scalar.copy(q_shift[2 * HC:3 * HC, 1:1 + H, 0:W - 1], q3[:, :, 1:W]).then_inc(act_chain, 1)
                act.wait_ge(act_chain, 1)
                act.sem_inc(act_chain, -1)
                act.sem_inc(shift_ready, 1)
                for half in range(2):
                    act.wait_ge(kv_free, 1)
                    act.sem_inc(kv_free, -1)
                    with act.Fori(0, T // 4) as pair:
                        for k in range(2):
                            t = pair * 2 + half * (T // 2) + k
                            act.wait_ge(off_ready, 1)
                            act.sem_inc(off_ready, -1)
                            nc.scalar.copy(off[:, bass.ds(t, 1), :].rearrange("p a c -> p (a c)"), ps_off[k][:, 0:NOFF]).then_inc(act_chain, 1)
                            act.wait_ge(act_chain, 1)
                            act.sem_inc(act_chain, -1)
                            act.sem_inc(off_free, 1)
                            act.wait_ge(tr_ready, 1)
                            act.sem_inc(tr_ready, -1)
                            nc.scalar.activation(rec[:, bass.ds(t, 1), 0:C].rearrange("p a c -> p (a c)"), ps_tr[k][:, 0:C],
                                                 ACT.Copy, scale=SCALE)
                            dst = kv[:, bass.ds(pair * 2 + k, 1), :].rearrange("p a (g s c) -> p (a g) s c", g=G, s=2)
                            src = ps_tr[k][:, C:3 * C].rearrange("p (s g c) -> p g s c", s=2, g=G)
                            nc.scalar.copy(dst, src).then_inc(act_chain, 1)
                            act.wait_ge(act_chain, 1)
                            act.sem_inc(act_chain, -1)
                            act.sem_inc(tr_free, 1)
                    act.sem_inc(kv_ready, 1)
                act.sem_inc(evacuated, 1)
                act.wait_ge(mask_in, 1)
                act.sem_inc(mask_in, -1)
                nc.scalar.activation(off[:, :, 2 * GK:], off[:, :, 2 * GK:], ACT.Exp, scale=-1.0).then_inc(mask_out, 1)

        def convolve(eng, api, j, img, out_img, chain):
            for tap in range(K2):
                src = img[:, tap // 3:tap // 3 + H, tap % 3:tap % 3 + W]
                if tap == 0:
                    ins = api.tensor_scalar(out_img, src, w_dw[:, j, 0:1], b_dw[:, j:j + 1], ALU.mult, ALU.add)
                else:
                    ins = api.scalar_tensor_tensor(out=out_img, in0=src, scalar=w_dw[:, j, tap:tap + 1], in1=out_img,
                                                   op0=ALU.mult, op1=ALU.add)
                ins.then_inc(chain, 1)
                eng.wait_ge(chain, 1)
                eng.sem_inc(chain, -1)

        @block.vector
        def _(dve):
            nc.vector.memset(zeros[:], 0.0).then_inc(zero_ready, 1)
            for img in (*padded, q_shift[0:3 * HC], w_shift):
                ins = nc.vector.memset(img[:], 0.0)
            nc.vector.memset(q_shift[3 * HC:QROWS], 1.0)
            ins.then_inc(dve_chain, 1)
            dve.wait_ge(dve_chain, 1)
            dve.sem_inc(dve_chain, -1)
            dve.sem_inc(shift_zero, 1)
            dve.sem_inc(padded_free[0], 1)
            dve.sem_inc(padded_free[1], 1)
            dve.sem_inc(xt_free, 1)
            dve.sem_inc(rec_free, 1)
            dve.wait_ge(consts, NC)
            dve.wait_ge(tap_ready, 1)
            nc.vector.memset(w_off[0:HC, :], 0.0)
            for tap in range(K2):
                dx = tap % 3
                ins = nc.vector.tensor_copy(w_shift[dx * HC:(dx + 1) * HC, tap // 3, :],
                                            ps_off[tap // 5][0:HC, tap % 5 * NOFF:(tap % 5 + 1) * NOFF])
            ins.then_inc(dve_chain, 1)
            dve.wait_ge(dve_chain, 1)
            dve.sem_inc(dve_chain, -1)
            dve.sem_inc(taps_used, 1)
            with dve.Fori(0, B) as b:
                dve.wait_ge(xT_ready, 1)
                dve.sem_inc(xT_ready, -1)
                dve.sem_inc(kv_free, 1)
                group_norm_vector(nc, dve, xT, stats, gn, dve_chain, moments, group_mean, group_var,
                                  var_ready, std_ready, mean_ps, var_ps)
                dve.sem_inc(normed, 1)
                dve.wait_ge(padded_ready[0], 1)
                dve.sem_inc(padded_ready[0], -1)
                convolve(dve, nc.vector, 0, padded[0], q_img[:].rearrange("p (y x) -> p y x", x=W), dve_chain)
                dve.sem_inc(q_ready, 1)
                dve.sem_inc(images_ready, 1)
                dve.sem_inc(padded_free[0], 1)
                dve.wait_ge(padded_ready[1], 1)
                dve.sem_inc(padded_ready[1], -1)
                convolve(dve, nc.vector, 1, padded[1], k_img[:].rearrange("p (y x) -> p y x", x=W), dve_chain)
                dve.sem_inc(images_ready, 1)
                dve.sem_inc(padded_free[1], 1)
                dve.wait_ge(evacuated, 1)
                dve.sem_inc(evacuated, -1)
                dve.wait_ge(rec_free, 1)
                dve.sem_inc(rec_free, -1)
                pt, cell, tmp = (q_buf[:, 0:T * 2 * GK].rearrange("p (t n) -> p t n", t=T) for q_buf in (k_img, v_img, xT))
                cell_i = tmp.bitcast(I32)
                nc.vector.tensor_tensor(pt, off[:, :, 0:2 * GK], base[:], ALU.add).then_inc(dve_chain, 1)
                dve.wait_ge(dve_chain, 1)
                dve.sem_inc(dve_chain, -1)
                nc.vector.tensor_scalar(pt, pt, -1.0, float(H), ALU.max, ALU.min).then_inc(dve_chain, 1)
                dve.wait_ge(dve_chain, 1)
                dve.sem_inc(dve_chain, -1)
                nc.vector.tensor_copy(cell_i, pt).then_inc(dve_chain, 1)
                dve.wait_ge(dve_chain, 1)
                dve.sem_inc(dve_chain, -1)
                nc.vector.tensor_copy(cell, cell_i).then_inc(dve_chain, 1)
                dve.wait_ge(dve_chain, 1)
                dve.sem_inc(dve_chain, -1)
                nc.vector.tensor_tensor(tmp, cell, pt, ALU.is_gt).then_inc(dve_chain, 1)
                dve.wait_ge(dve_chain, 1)
                dve.sem_inc(dve_chain, -1)
                nc.vector.tensor_tensor(cell, cell, tmp, ALU.subtract).then_inc(dve_chain, 1)
                dve.wait_ge(dve_chain, 1)
                dve.sem_inc(dve_chain, -1)
                nc.vector.tensor_tensor(pt, pt, cell, ALU.subtract).then_inc(dve_chain, 1)
                dve.wait_ge(dve_chain, 1)
                dve.sem_inc(dve_chain, -1)
                rows = tmp[:, :, 0:GK]
                nc.vector.scalar_tensor_tensor(out=rows, in0=cell[:, :, 0:GK], scalar=float(XT), in1=cell[:, :, GK:],
                                                         op0=ALU.mult, op1=ALU.add).then_inc(dve_chain, 1)
                dve.wait_ge(dve_chain, 1)
                dve.sem_inc(dve_chain, -1)
                row0_b = row0[:].unsqueeze(1).to_broadcast([P, T, GK])
                nc.vector.tensor_tensor(rows, rows, row0_b, ALU.add).then_inc(dve_chain, 1)
                dve.wait_ge(dve_chain, 1)
                dve.sem_inc(dve_chain, -1)
                nc.vector.tensor_copy(rec[:, :, PK_I:PK].bitcast(U32), rows).then_inc(dve_chain, 1)
                dve.wait_ge(dve_chain, 1)
                dve.sem_inc(dve_chain, -1)
                nc.vector.tensor_scalar(row0[:], row0[:], float(G * POS), None, ALU.add).then_inc(dve_chain, 1)
                dve.wait_ge(dve_chain, 1)
                dve.sem_inc(dve_chain, -1)
                dve.sem_inc(mask_in, 1)
                dve.wait_ge(mask_out, 1)
                dve.sem_inc(mask_out, -1)
                mask = off[:, :, 2 * GK:]
                nc.vector.tensor_scalar(mask, mask, 1.0, None, ALU.add).then_inc(dve_chain, 1)
                dve.wait_ge(dve_chain, 1)
                dve.sem_inc(dve_chain, -1)
                nc.vector.reciprocal(mask, mask).then_inc(dve_chain, 1)
                dve.wait_ge(dve_chain, 1)
                dve.sem_inc(dve_chain, -1)
                nc.vector.tensor_scalar(cell, pt, -1.0, 1.0, ALU.mult, ALU.add).then_inc(dve_chain, 1)
                dve.wait_ge(dve_chain, 1)
                dve.sem_inc(dve_chain, -1)
                for wy in (pt, cell):
                    for g in range(G):
                        v = wy[:, :, g * K2:(g + 1) * K2]
                        ins = nc.vector.tensor_tensor(v, v, mask, ALU.mult)
                ins.then_inc(dve_chain, 1)
                dve.wait_ge(dve_chain, 1)
                dve.sem_inc(dve_chain, -1)
                corners = rec[:, :, PK_W:PK_I].rearrange("p t (n c) -> p t n c", c=4)
                for c in range(4):
                    wx, wy = (cell, pt)[c // 2], (cell, pt)[c % 2]
                    ins = nc.vector.tensor_tensor(corners[:, :, :, c], wx[:, :, GK:], wy[:, :, 0:GK], ALU.mult)
                ins.then_inc(dve_chain, 1)
                dve.wait_ge(dve_chain, 1)
                dve.sem_inc(dve_chain, -1)
                dve.sem_inc(rec_ready, 1)

        @block.gpsimd
        def _(pool):
            pool.wait_ge(consts, NC)
            for tap in range(K2):
                ins = nc.gpsimd.tensor_scalar(diag[:, tap, :], ident[:], w_dw[:, 2, tap:tap + 1], None, ALU.mult)
            ins.then_inc(diag_ready, 1)


def layer0_attend(nc, x, x1, w, records, table, gathered):
    CELL = 4 * 2 * HC
    with ExitStack() as stack:
        s = Scope(nc, "l0b", stack)
        ident, w_proj, b_proj = s.sb("ident", [P, P]), s.sb("w_proj", [P, C]), s.sb("b_proj", [P, C])
        rec = [s.sb(f"rec{k}", [P, PK]) for k in range(2)]
        xin = [s.sb(f"xin{k}", [P, C]) for k in range(2)]
        xout = [s.sb(f"xout{k}", [P, C]) for k in range(2)]
        got = [s.sb(f"got{k}", [P, GK, CELL]) for k in range(2)]
        prod = s.sb("prod", [P, 4 * GK, HC])
        dots, coef = s.sb("dots", [P, 4 * GK]), s.sb("coef", [P, 4 * GK])
        logit, prob = s.sb("logit", [P, GK]), s.sb("prob", [P, GK])
        top, total = s.sb("top", [P, G]), s.sb("total", [P, G])
        o, oT = s.sb("o", [P, C]), s.sb("oT", [P, C])
        ps_t, ps_o = s.ps("ps_t"), s.ps("ps_o")
        consts = s.sem("consts")
        rec_loaded = [s.sem(f"rec_loaded{k}") for k in range(2)]
        rec_free = [s.sem(f"rec_free{k}") for k in range(2)]
        rec_here = [s.sem(f"rec_here{k}") for k in range(2)]
        got_free = [s.sem(f"got_free{k}") for k in range(2)]
        dve_chain, act_chain = s.sem("dve_chain"), s.sem("act_chain")
        logit_ready, prob_ready = s.sem("logit_ready"), s.sem("prob_ready")
        o_ready, o_free, t_ready, oT_ready, p_ready = (s.sem(x) for x in ("o_ready", "o_free", "t_ready", "oT_ready", "p_ready"))
        out_ready = [s.sem(f"out_ready{k}") for k in range(2)]
        out_stored = [s.sem(f"out_stored{k}") for k in range(2)]
        out_free = [s.sem(f"out_free{k}") for k in range(2)]
        block = s.block()
        loads = [(ident, w["ident"]), (w_proj, w["w_proj"]), (b_proj, w["b_proj"])]
        PAIRS = B * T // 2

        @block.sync
        def _(sp):
            for dst, src in loads:
                sp.dma_start(dst[:], src).then_inc(consts, 16)
            with sp.Fori(0, B) as b:
                with sp.Fori(0, T // 2) as pair:
                    for k in range(2):
                        t = pair * 2 + k
                        sp.wait_ge(rec_free[k], 1)
                        sp.sem_inc(rec_free[k], -1)
                        sp.dma_start(rec[k][:], records[bass.ds(b, 1), :, bass.ds(t * PK, PK)].rearrange("a p f -> p (a f)")
                                     ).then_inc(rec_loaded[k], 16)
                        sp.dma_start(xin[k][:], x[bass.ds(b, 1), bass.ds(t * P, P), :].rearrange("a p f -> p (a f)")
                                     ).then_inc(rec_loaded[k], 16)

        @block.gpsimd
        def _(pool):
            pool.sem_inc(rec_free[0], 1)
            pool.sem_inc(rec_free[1], 1)
            pool.sem_inc(got_free[0], 1)
            pool.sem_inc(got_free[1], 1)
            with pool.Fori(0, PAIRS) as pair:
                for k in range(2):
                    pool.wait_ge(rec_loaded[k], 32)
                    pool.sem_inc(rec_loaded[k], -32)
                    pool.sem_inc(rec_here[k], 1)
                    pool.wait_ge(got_free[k], 1)
                    pool.sem_inc(got_free[k], -1)
                    for n in range(GK):
                        nc.gpsimd.indirect_dma_start(
                            got[k][:, n, :], None, table,
                            bass.IndirectOffsetOnAxis(ap=rec[k][:, PK_I + n:PK_I + n + 1].bitcast(U32), axis=0),
                        ).then_inc(gathered[k], 16)

        @block.vector
        def _(dve):
            dve.wait_ge(consts, 16 * len(loads))
            with dve.Fori(0, PAIRS) as pair:
                for k in range(2):
                    dve.wait_ge(rec_here[k], 1)
                    dve.sem_inc(rec_here[k], -1)
                    nc.vector.tensor_tensor(xin[k][:], xin[k][:], b_proj[:], ALU.add).then_inc(dve_chain, 1)
                    dve.wait_ge(dve_chain, 1)
                    dve.sem_inc(dve_chain, -1)
                    dve.wait_ge(gathered[k], (pair + 1) * (16 * GK))
                    cells = got[k][:].rearrange("p n (c f) -> p (n c) f", c=4)
                    keys = cells[:, :, 0:HC].rearrange("p (g n) f -> p g n f", g=G)
                    q = rec[k][:, 0:C].rearrange("p (g f) -> p g f", g=G).unsqueeze(2).to_broadcast([P, G, 4 * K2, HC])
                    prod_g = prod[:].rearrange("p (g n) f -> p g n f", g=G)
                    nc.vector.tensor_tensor(prod_g, keys, q, ALU.mult).then_inc(dve_chain, 1)
                    dve.wait_ge(dve_chain, 1)
                    dve.sem_inc(dve_chain, -1)
                    nc.vector.tensor_reduce(dots[:], prod[:], AX.X, ALU.add).then_inc(dve_chain, 1)
                    dve.wait_ge(dve_chain, 1)
                    dve.sem_inc(dve_chain, -1)
                    weights = rec[k][:, PK_W:PK_I]
                    nc.vector.tensor_tensor(dots[:], dots[:], weights, ALU.mult).then_inc(dve_chain, 1)
                    dve.wait_ge(dve_chain, 1)
                    dve.sem_inc(dve_chain, -1)
                    nc.vector.tensor_reduce(logit[:], dots[:].rearrange("p (n c) -> p n c", c=4), AX.X, ALU.add).then_inc(dve_chain, 1)
                    dve.wait_ge(dve_chain, 1)
                    dve.sem_inc(dve_chain, -1)
                    by_group = logit[:].rearrange("p (g n) -> p g n", g=G)
                    nc.vector.tensor_reduce(top[:], by_group, AX.X, ALU.max).then_inc(dve_chain, 1)
                    dve.wait_ge(dve_chain, 1)
                    dve.sem_inc(dve_chain, -1)
                    nc.vector.tensor_tensor(by_group, by_group, top[:].unsqueeze(2).to_broadcast([P, G, K2]), ALU.subtract).then_inc(dve_chain, 1)
                    dve.wait_ge(dve_chain, 1)
                    dve.sem_inc(dve_chain, -1)
                    dve.sem_inc(logit_ready, 1)
                    dve.wait_ge(prob_ready, 1)
                    dve.sem_inc(prob_ready, -1)
                    probs = prob[:].rearrange("p (g n) -> p g n", g=G)
                    nc.vector.tensor_reduce(total[:], probs, AX.X, ALU.add).then_inc(dve_chain, 1)
                    dve.wait_ge(dve_chain, 1)
                    dve.sem_inc(dve_chain, -1)
                    nc.vector.reciprocal(total[:], total[:]).then_inc(dve_chain, 1)
                    dve.wait_ge(dve_chain, 1)
                    dve.sem_inc(dve_chain, -1)
                    nc.vector.tensor_tensor(probs, probs, total[:].unsqueeze(2).to_broadcast([P, G, K2]), ALU.mult).then_inc(dve_chain, 1)
                    dve.wait_ge(dve_chain, 1)
                    dve.sem_inc(dve_chain, -1)
                    nc.vector.tensor_tensor(coef[:].rearrange("p (n c) -> p n c", c=4), weights.rearrange("p (n c) -> p n c", c=4),
                                                      prob[:].unsqueeze(2).to_broadcast([P, GK, 4]), ALU.mult).then_inc(dve_chain, 1)
                    dve.wait_ge(dve_chain, 1)
                    dve.sem_inc(dve_chain, -1)
                    nc.vector.tensor_tensor(prod[:], cells[:, :, HC:], coef[:].unsqueeze(2).to_broadcast([P, 4 * GK, HC]),
                                                      ALU.mult).then_inc(dve_chain, 1)
                    dve.wait_ge(dve_chain, 1)
                    dve.sem_inc(dve_chain, -1)
                    dve.sem_inc(got_free[k], 1)
                    dve.wait_ge(o_free, 1)
                    dve.sem_inc(o_free, -1)
                    nc.vector.tensor_reduce(o[:].rearrange("p (g f) -> p g f", g=G),
                                                      prod[:].rearrange("p (g n) f -> p g f n", g=G), AX.X, ALU.add).then_inc(dve_chain, 1)
                    dve.wait_ge(dve_chain, 1)
                    dve.sem_inc(dve_chain, -1)
                    dve.sem_inc(o_ready, 1)
                    dve.wait_ge(p_ready, 1)
                    dve.sem_inc(p_ready, -1)
                    dve.wait_ge(out_free[k], 1)
                    dve.sem_inc(out_free[k], -1)
                    nc.vector.tensor_tensor(xout[k][:], ps_o[:, 0:C], xin[k][:], ALU.add).then_inc(dve_chain, 1)
                    dve.wait_ge(dve_chain, 1)
                    dve.sem_inc(dve_chain, -1)
                    dve.sem_inc(rec_free[k], 1)
                    dve.sem_inc(out_ready[k], 1)

        @block.tensor
        def _(pe):
            pe.wait_ge(consts, 16 * len(loads))
            pe.sem_inc(o_free, 1)
            with pe.Fori(0, B * T) as t:
                pe.wait_ge(o_ready, 1)
                pe.sem_inc(o_ready, -1)
                nc.tensor.transpose(ps_t[:, 0:P], o[:], ident[:]).then_inc(t_ready, 1)
                pe.wait_ge(oT_ready, 1)
                pe.sem_inc(oT_ready, -1)
                pe.sem_inc(o_free, 1)
                nc.tensor.matmul(ps_o[:, 0:C], oT[:], w_proj[:], start=True, stop=True).then_inc(p_ready, 1)

        @block.scalar
        def _(act):
            act.sem_inc(out_free[0], 1)
            act.sem_inc(out_free[1], 1)
            with act.Fori(0, B) as b:
                with act.Fori(0, T // 2) as pair:
                    for k in range(2):
                        act.wait_ge(logit_ready, 1)
                        act.sem_inc(logit_ready, -1)
                        nc.scalar.activation(prob[:], logit[:], ACT.Exp).then_inc(prob_ready, 1)
                        act.wait_ge(t_ready, 1)
                        act.sem_inc(t_ready, -1)
                        nc.scalar.copy(oT[:], ps_t[:, 0:P]).then_inc(oT_ready, 1)
                        act.wait_ge(out_ready[k], 1)
                        act.sem_inc(out_ready[k], -1)
                        act.dma_start(x1[bass.ds(b, 1), bass.ds((pair * 2 + k) * P, P), :].rearrange("a p f -> p (a f)"), xout[k][:]
                                      ).then_inc(out_stored[k], 16)
                        act.wait_ge(out_stored[k], 16)
                        act.sem_inc(out_stored[k], -16)
                        act.sem_inc(out_free[k], 1)


def layer0_inputs(i):
    f = np.float32
    w_off = np.concatenate([
        i["L0_conv_w_off"].reshape(G, K2, 2, C).transpose(2, 0, 1, 3).reshape(2 * GK, C), i["L0_conv_w_mask"]]).T
    b_off = np.concatenate([
        i["L0_conv_b_off"].reshape(G, K2, 2).transpose(2, 0, 1).reshape(2 * GK), i["L0_conv_b_mask"]])[None]
    pconv = np.concatenate([i["L0_conv_pconv_off_w"], i["L0_conv_pconv_mask_w"][None]])
    tok = np.arange(N).reshape(T, P).T
    tap, dil = np.arange(K2), 2 * np.arange(G)[:, None] + 1
    by, bx = ((tap // 3 * dil) - dil).reshape(-1), ((tap % 3 * dil) - dil).reshape(-1)
    base = np.concatenate([(tok // W)[:, :, None] + by, (tok % W)[:, :, None] + bx], -1)
    row0 = np.repeat(np.arange(G) * POS, K2) + XT + 1
    return {
        "w_qkv": i["L0_conv_w_qkv"], "b_qkv": i["L0_conv_b_qkv"].reshape(3, C).T,
        "w_dw": i["L0_conv_w_dw"].reshape(3, C, K2).transpose(1, 0, 2), "b_dw": i["L0_conv_b_dw"].reshape(3, C).T,
        "w_off": w_off, "b_off": b_off, "w_pconv": pconv.transpose(1, 0, 3, 4, 2).reshape(HC, 5, K2, HC),
        "base": base.astype(f), "row0": np.broadcast_to(row0, (P, GK)).astype(f),
        "w_proj": i["L0_conv_w_proj"], "b_proj": np.broadcast_to(i["L0_conv_b_proj"], (P, C)),
    }

def layer1(nc, x, out, w):
    LEVELS = (3, 5, 7)
    PAD = LEVELS[-1] // 2
    TAPS = sum(k * k for k in LEVELS)
    FIRST = [sum(k * k for k in LEVELS[:n]) for n in range(3)]
    PE_BANKS = 3
    PE_ROWS = PE_BANKS * ROWS
    with ExitStack() as stack:
        s = Scope(nc, "l1", stack)
        ident, group, center = s.sb("ident", [P, P]), s.sb("group", [P, P]), s.sb("center", [P, P])
        w_f, w_gate, b_gate = s.sb("w_f", [P, 2 * C]), s.sb("w_gate", [P, 4, P]), s.sb("b_gate", [P, 4])
        b_f, taps, diag = s.sb("b_f", [P, 2]), s.sb("taps", [P, TAPS]), s.sb("diag", [P, TAPS, P])
        w_h, b_h, gamma, beta = s.sb("w_h", [P, C]), s.sb("b_h", [P, 1]), s.sb("gamma", [P, 1]), s.sb("beta", [P, 1])
        w_p, b_p, beta_rows, ones = s.sb("w_p", [P, C]), s.sb("b_p", [P, C]), s.sb("beta_rows", [P, P]), s.sb("ones", [P, P])
        w_pg, row = s.sb("w_pg", [P, C]), s.sb("row", [P, C])
        xt, xT = s.sb("xt", [P, T, C]), s.sb("xT", [P, N])
        stats, gn = s.sb("stats", [P, NB, 6]), s.sb("gn", [P, 8])
        q_img, acc, ctx_all = s.sb("q_img", [P, N]), s.sb("acc", [P, N]), s.sb("ctx_all", [P, N])
        img = [s.sb(f"img{n}", [P, H + 2 * PAD, W + 2 * PAD]) for n in range(2)]
        gated = [s.sb(f"gated{n}", [P, BANK]) for n in range(2)]
        sums, cg, rstd = s.sb("sums", [P, PE_BANKS + 1]), s.sb("cg", [P, 2]), s.sb("rstd", [P, T])
        ps, ps_conv, ps_gate = ([s.ps(f"{name}{n}") for n in range(2)] for name in ("ps", "ps_conv", "ps_gate"))
        ps_small = s.ps("ps_small")
        mean_ps, var_ps, ln_ps = ps_small[:, 0:1], ps_small[:, 1:2], ps_small[:, 64:64 + T]

        names = ("consts x_loaded xt_free ps_ready xT_ready normed normed_pool moments group_mean group_var var_ready std_ready "
                 "dve_chain act_chain pool_chain diag_ready row_ready row_out pe_img_ready dve_img_ready conv_ready "
                 "conv_free rows_ready_dve gate_ready gate_free q_ready level_done mean_in mean_out "
                 "mod_ready mod_free mod_done center_ready center_free centered ln_ready lnstd_in lnstd_out "
                 "resid_ready out_ready out_free stored").split()
        sem = {n: s.sem(n) for n in names}
        (consts, x_loaded, xt_free, ps_ready, xT_ready, normed, normed_pool, moments, group_mean, group_var, var_ready, std_ready,
         dve_chain, act_chain, pool_chain, diag_ready, row_ready, row_out, pe_img_ready, dve_img_ready, conv_ready,
         conv_free, rows_ready_dve, gate_ready, gate_free, q_ready, level_done, mean_in, mean_out,
         mod_ready, mod_free, mod_done, center_ready, center_free, centered, ln_ready, lnstd_in, lnstd_out,
         resid_ready, out_ready, out_free, stored) = (sem[n] for n in names)
        ps_free = [s.sem(f"ps_free{n}") for n in range(2)]
        loads = [(ident, "ident"), (group, "group"), (center, "center"), (w_f, "w_f"), (w_gate, "w_gate"), (b_gate, "b_gate"),
                 (b_f, "b_f"), (taps, "taps"), (w_h, "w_h"), (b_h, "b_h"), (gamma, "gamma"), (beta, "beta"), (w_p, "w_p"),
                 (b_p, "b_p"), (ones, "ones")]
        NC = 16 * len(loads)
        block = s.block()

        @block.sync
        def _(sp):
            for dst, name in loads:
                sp.dma_start(dst[:], w[name]).then_inc(consts, 16)
            with sp.Fori(0, B) as b:
                sp.wait_ge(xt_free, 1)
                sp.sem_inc(xt_free, -1)
                load_tokens(sp, xt, x, b, x_loaded)
                sp.wait_ge(out_ready, 1)
                sp.sem_inc(out_ready, -1)
                for n in range(LOADS):
                    h = T // LOADS
                    dst = out[bass.ds(b, 1), n * h * P:(n + 1) * h * P, :].rearrange("a (t p) c -> p (a t) c", p=P)
                    sp.dma_start(dst, xt[:, n * h:(n + 1) * h, :]).then_inc(stored, 16)
                sp.wait_ge(stored, 16 * LOADS)
                sp.sem_inc(stored, -16 * LOADS)
                sp.sem_inc(xt_free, 1)

        @block.tensor
        def _(pe):
            pe.wait_ge(consts, NC)
            pe.wait_ge(row_ready, 1)
            pe.sem_inc(row_ready, -1)
            nc.tensor.matmul(ps_small[:, 128:256], beta_rows[:], w_p[:], start=True, stop=True).then_inc(row_out, 1)
            pe.wait_ge(diag_ready, 1)
            with pe.Fori(0, B) as b:
                pe.wait_ge(x_loaded, 16 * LOADS)
                pe.sem_inc(x_loaded, -16 * LOADS)
                for n in range(NB):
                    pe.wait_ge(ps_free[n % 2], 1)
                    pe.sem_inc(ps_free[n % 2], -1)
                    for t in range(4):
                        ins = nc.tensor.transpose(ps[n % 2][:, t * P:(t + 1) * P], xt[:, 4 * n + t, :], ident[:])
                    ins.then_inc(ps_ready, 1)
                group_norm_tensor(nc, pe, group, gn, moments, group_mean, group_var, mean_ps, var_ps)
                pe.wait_ge(normed, 1)
                pe.sem_inc(normed, -1)
                for j in (1, 0):
                    for n in range(NB):
                        pe.wait_ge(ps_free[n % 2], 1)
                        pe.sem_inc(ps_free[n % 2], -1)
                        nc.tensor.matmul(ps[n % 2][:], w_f[:, j * C:(j + 1) * C], xT[:, n * BANK:(n + 1) * BANK],
                                         start=True, stop=True).then_inc(ps_ready, 1)

                def convolve(level):
                    k = LEVELS[level]
                    o = PAD - k // 2
                    pe.wait_ge(pe_img_ready, 1)
                    pe.sem_inc(pe_img_ready, -1)
                    for n in range(PE_BANKS):
                        pe.wait_ge(conv_free, 1)
                        pe.sem_inc(conv_free, -1)
                        for tap in range(k * k):
                            y, xx = n * ROWS + o + tap // k, o + tap % k
                            ins = nc.tensor.matmul(ps_conv[n % 2][:], diag[:, FIRST[level] + tap, :],
                                                   img[level % 2][:, y:y + ROWS, xx:xx + W], start=(tap == 0), stop=(tap == k * k - 1))
                        ins.then_inc(conv_ready, 1)

                def gate(level):
                    for n in range(NB):
                        pe.wait_ge(gate_free, 1)
                        pe.sem_inc(gate_free, -1)
                        nc.tensor.matmul(ps_gate[n % 2][:], w_gate[:, level, :], xT[:, n * BANK:(n + 1) * BANK],
                                         start=True, stop=True).then_inc(gate_ready, 1)

                convolve(0)
                convolve(1)
                gate(0)
                convolve(2)
                gate(1)
                gate(2)
                gate(3)
                for n in range(NB):
                    pe.wait_ge(mod_ready, 1)
                    pe.sem_inc(mod_ready, -1)
                    pe.wait_ge(ps_free[n % 2], 1)
                    pe.sem_inc(ps_free[n % 2], -1)
                    nc.tensor.matmul(ps[n % 2][:], w_h[:], ctx_all[:, n * BANK:(n + 1) * BANK], start=True, stop=True
                                     ).then_inc(mod_free, 1)
                for n in range(NB):
                    pe.wait_ge(mod_done, 1)
                    pe.sem_inc(mod_done, -1)
                    pe.wait_ge(ps_free[n % 2], 1)
                    pe.sem_inc(ps_free[n % 2], -1)
                    nc.tensor.matmul(ps[n % 2][:], center[:], q_img[:, n * BANK:(n + 1) * BANK], start=True, stop=True
                                     ).then_inc(center_ready, 1)
                pe.wait_ge(centered, 1)
                pe.sem_inc(centered, -1)
                for t in range(T):
                    ins = nc.tensor.matmul(ln_ps[:, t:t + 1], xT[:, t * P:(t + 1) * P], ones[:, 0:1], start=True, stop=True)
                ins.then_inc(ln_ready, 1)
                for n in range(NB):
                    pe.wait_ge(ps_free[n % 2], 1)
                    pe.sem_inc(ps_free[n % 2], -1)
                    for t in range(4):
                        ins = nc.tensor.matmul(ps[n % 2][:, t * P:(t + 1) * P], acc[:, (4 * n + t) * P:(4 * n + t + 1) * P], w_pg[:],
                                               start=True, stop=True)
                    ins.then_inc(out_free, 1)

        @block.scalar
        def _(act):
            act.sem_inc(ps_free[0], 1)
            act.sem_inc(ps_free[1], 1)
            act.sem_inc(conv_free, 2)
            act.wait_ge(consts, NC)

            def gelu(dst, src, n, chain=True):
                nc.scalar.activation(dst, src, ACT.Gelu, accum_out=sums[:, n:n + 1]).then_inc(act_chain, 1)
                act.wait_ge(act_chain, 1)
                act.sem_inc(act_chain, -1)

            with act.Fori(0, B) as b:
                for n in range(NB):
                    act.wait_ge(ps_ready, 1)
                    act.sem_inc(ps_ready, -1)
                    nc.scalar.copy(xT[:, n * BANK:(n + 1) * BANK], ps[n % 2][:]).then_inc(act_chain, 1)
                    act.wait_ge(act_chain, 1)
                    act.sem_inc(act_chain, -1)
                    act.sem_inc(ps_free[n % 2], 1)
                act.sem_inc(xT_ready, 1)
                act.wait_ge(var_ready, 1)
                act.sem_inc(var_ready, -1)
                nc.scalar.activation(gn[:, 6:7], gn[:, 5:6], ACT.Sqrt).then_inc(std_ready, 1)
                for j in (1, 0):
                    for n in range(NB):
                        act.wait_ge(ps_ready, 1)
                        act.sem_inc(ps_ready, -1)
                        src = ps[n % 2][:]
                        if j == 1:
                            dst = img[0][:, PAD + n * ROWS:PAD + (n + 1) * ROWS, PAD:PAD + W]
                            src = src.rearrange("p (y x) -> p y x", x=W)
                        else:
                            dst = q_img[:, n * BANK:(n + 1) * BANK]
                        nc.scalar.activation(dst, src, ACT.Identity, bias=b_f[:, j:j + 1]).then_inc(act_chain, 1)
                        act.wait_ge(act_chain, 1)
                        act.sem_inc(act_chain, -1)
                        act.sem_inc(ps_free[n % 2], 1)
                    if j == 1:
                        act.sem_inc(pe_img_ready, 1)
                        act.sem_inc(dve_img_ready, 1)
                act.sem_inc(q_ready, 1)
                for level in range(3):
                    dst = img[(level + 1) % 2]
                    src = acc[:].rearrange("p (y x) -> p y x", x=W)
                    if level == 2:
                        act.wait_ge(level_done, 1)
                        act.sem_inc(level_done, -1)
                    for n in range(PE_BANKS):
                        act.wait_ge(conv_ready, 1)
                        act.sem_inc(conv_ready, -1)
                        gelu(dst[:, PAD + n * ROWS:PAD + (n + 1) * ROWS, PAD:PAD + W],
                             ps_conv[n % 2][:].rearrange("p (y x) -> p y x", x=W), n)
                        act.sem_inc(conv_free, 1)
                    act.wait_ge(rows_ready_dve, 1)
                    act.sem_inc(rows_ready_dve, -1)
                    gelu(dst[:, PAD + PE_ROWS:PAD + H, PAD:PAD + W], src[:, PE_ROWS:H, :], PE_BANKS)
                    act.sem_inc(dve_img_ready, 1)
                    if level < 2:
                        act.sem_inc(pe_img_ready, 1)
                act.wait_ge(mean_in, 1)
                act.sem_inc(mean_in, -1)
                nc.scalar.activation(cg[:, 1:2], cg[:, 0:1], ACT.Gelu).then_inc(mean_out, 1)
                for n in range(NB):
                    act.wait_ge(center_ready, 1)
                    act.sem_inc(center_ready, -1)
                    nc.scalar.copy(acc[:, n * BANK:(n + 1) * BANK], ps[n % 2][:])
                    nc.scalar.activation(xT[:, n * BANK:(n + 1) * BANK], ps[n % 2][:], ACT.Square).then_inc(act_chain, 1)
                    act.wait_ge(act_chain, 1)
                    act.sem_inc(act_chain, -1)
                    act.sem_inc(ps_free[n % 2], 1)
                act.sem_inc(centered, 1)
                act.wait_ge(lnstd_in, 1)
                act.sem_inc(lnstd_in, -1)
                nc.scalar.activation(rstd[:], rstd[:], ACT.Sqrt).then_inc(lnstd_out, 1)

        def convolve_rows(dve, level):
            first, rows = PE_ROWS, H - PE_ROWS
            k = LEVELS[level]
            o = PAD - k // 2
            out_rows = acc[:].rearrange("p (y x) -> p y x", x=W)[:, first:first + rows, :]
            for tap in range(k * k):
                y, xx, c = first + o + tap // k, o + tap % k, FIRST[level] + tap
                src = img[level % 2][:, y:y + rows, xx:xx + W]
                if tap == 0:
                    ins = nc.vector.tensor_scalar(out_rows, src, taps[:, c:c + 1], None, ALU.mult)
                else:
                    ins = nc.vector.scalar_tensor_tensor(out=out_rows, in0=src, scalar=taps[:, c:c + 1], in1=out_rows,
                                                         op0=ALU.mult, op1=ALU.add)
                ins.then_inc(dve_chain, 1)
                dve.wait_ge(dve_chain, 1)
                dve.sem_inc(dve_chain, -1)

        @block.gpsimd
        def _(pool):
            pool.wait_ge(consts, NC)
            for n in range(TAPS):
                ins = nc.gpsimd.tensor_scalar(diag[:, n, :], ident[:], taps[:, n:n + 1], None, ALU.mult)
            ins.then_inc(pool_chain, 1)
            pool.wait_ge(pool_chain, 1)
            pool.sem_inc(pool_chain, -1)
            pool.sem_inc(diag_ready, 1)
            with pool.Fori(0, B) as b:
                pool.wait_ge(normed_pool, 1)
                pool.sem_inc(normed_pool, -1)
                nc.gpsimd.tensor_tensor(xt[:], xt[:], row[:].unsqueeze(1).to_broadcast([P, T, C]), ALU.add).then_inc(pool_chain, 1)
                pool.wait_ge(pool_chain, 1)
                pool.sem_inc(pool_chain, -1)
                pool.sem_inc(resid_ready, 1)

        @block.vector
        def _(dve):
            for im in img:
                nc.vector.memset(im[:], 0.0)
            dve.wait_ge(consts, NC)
            nc.vector.tensor_scalar(w_pg[:], w_p[:], gamma[:, 0:1], None, ALU.mult)
            nc.vector.tensor_scalar(beta_rows[:], ones[:], beta[:, 0:1], None, ALU.mult)
            dve.drain().then_inc(dve_chain, 1)
            dve.wait_ge(dve_chain, 1)
            dve.sem_inc(dve_chain, -1)
            dve.sem_inc(row_ready, 1)
            dve.wait_ge(diag_ready, 1)
            dve.wait_ge(row_out, 1)
            dve.sem_inc(row_out, -1)
            nc.vector.tensor_tensor(row[:], ps_small[:, 128:256], b_p[:], ALU.add).then_inc(dve_chain, 1)
            dve.wait_ge(dve_chain, 1)
            dve.sem_inc(dve_chain, -1)
            dve.sem_inc(xt_free, 1)
            dve.sem_inc(gate_free, 2)

            def gate(level):
                for n in range(NB):
                    dve.wait_ge(gate_ready, 1)
                    dve.sem_inc(gate_ready, -1)
                    rows = slice(PAD + n * ROWS, PAD + (n + 1) * ROWS)
                    total = ctx_all[:, n * BANK:(n + 1) * BANK]
                    if level < 3:
                        dst = total if level == 0 else gated[n % 2][:]
                        nc.vector.scalar_tensor_tensor(
                            out=dst.rearrange("p (y x) -> p y x", x=W), in0=ps_gate[n % 2][:].rearrange("p (y x) -> p y x", x=W),
                            scalar=b_gate[:, level:level + 1], in1=img[(level + 1) % 2][:, rows, PAD:PAD + W],
                            op0=ALU.add, op1=ALU.mult).then_inc(dve_chain, 1)
                        dve.wait_ge(dve_chain, 1)
                        dve.sem_inc(dve_chain, -1)
                    else:
                        nc.vector.tensor_scalar(gated[n % 2][:], ps_gate[n % 2][:], b_gate[:, 3:4], cg[:, 1:2],
                                                          ALU.add, ALU.mult).then_inc(dve_chain, 1)
                        dve.wait_ge(dve_chain, 1)
                        dve.sem_inc(dve_chain, -1)
                    dve.sem_inc(gate_free, 1)
                    if level:
                        nc.vector.tensor_tensor(total, total, gated[n % 2][:], ALU.add).then_inc(dve_chain, 1)
                        dve.wait_ge(dve_chain, 1)
                        dve.sem_inc(dve_chain, -1)
                    if level == 3:
                        dve.sem_inc(mod_ready, 1)

            with dve.Fori(0, B) as b:
                dve.wait_ge(xT_ready, 1)
                dve.sem_inc(xT_ready, -1)
                group_norm_vector(nc, dve, xT, stats, gn, dve_chain, moments, group_mean, group_var,
                                  var_ready, std_ready, mean_ps, var_ps)
                dve.sem_inc(normed, 1)
                dve.sem_inc(normed_pool, 1)
                for level in range(3):
                    dve.wait_ge(dve_img_ready, 1)
                    dve.sem_inc(dve_img_ready, -1)
                    convolve_rows(dve, level)
                    dve.sem_inc(rows_ready_dve, 1)
                    if level:
                        gate(level - 1)
                    if level == 1:
                        dve.sem_inc(level_done, 1)
                dve.wait_ge(dve_img_ready, 1)
                dve.sem_inc(dve_img_ready, -1)
                gate(2)
                nc.vector.tensor_reduce(cg[:, 0:1], sums[:], AX.X, ALU.add).then_inc(dve_chain, 1)
                dve.wait_ge(dve_chain, 1)
                dve.sem_inc(dve_chain, -1)
                nc.vector.tensor_scalar(cg[:, 0:1], cg[:, 0:1], 1.0 / N, None, ALU.mult).then_inc(dve_chain, 1)
                dve.wait_ge(dve_chain, 1)
                dve.sem_inc(dve_chain, -1)
                dve.sem_inc(mean_in, 1)
                dve.wait_ge(mean_out, 1)
                dve.sem_inc(mean_out, -1)
                gate(3)
                dve.wait_ge(q_ready, 1)
                dve.sem_inc(q_ready, -1)
                for n in range(NB):
                    dve.wait_ge(mod_free, 1)
                    dve.sem_inc(mod_free, -1)
                    q = q_img[:, n * BANK:(n + 1) * BANK]
                    nc.vector.scalar_tensor_tensor(out=q, in0=ps[n % 2][:], scalar=b_h[:, 0:1], in1=q,
                                                             op0=ALU.add, op1=ALU.mult).then_inc(dve_chain, 1)
                    dve.wait_ge(dve_chain, 1)
                    dve.sem_inc(dve_chain, -1)
                    dve.sem_inc(ps_free[n % 2], 1)
                    dve.sem_inc(mod_done, 1)
                dve.wait_ge(ln_ready, 1)
                dve.sem_inc(ln_ready, -1)
                nc.vector.tensor_scalar(rstd[:], ln_ps, 1.0 / C, 1e-3, ALU.mult, ALU.add).then_inc(dve_chain, 1)
                dve.wait_ge(dve_chain, 1)
                dve.sem_inc(dve_chain, -1)
                nc.vector.reciprocal(rstd[:], rstd[:]).then_inc(dve_chain, 1)
                dve.wait_ge(dve_chain, 1)
                dve.sem_inc(dve_chain, -1)
                dve.sem_inc(lnstd_in, 1)
                dve.wait_ge(lnstd_out, 1)
                dve.sem_inc(lnstd_out, -1)
                dve.wait_ge(resid_ready, 1)
                dve.sem_inc(resid_ready, -1)
                for n in range(NB):
                    dve.wait_ge(out_free, 1)
                    dve.sem_inc(out_free, -1)
                    for t in range(4 * n, 4 * n + 4):
                        ins = nc.vector.scalar_tensor_tensor(out=xt[:, t, :], in0=ps[n % 2][:, t % 4 * P:(t % 4 + 1) * P],
                                                             scalar=rstd[:, t:t + 1], in1=xt[:, t, :], op0=ALU.mult, op1=ALU.add)
                    ins.then_inc(dve_chain, 1)
                    dve.wait_ge(dve_chain, 1)
                    dve.sem_inc(dve_chain, -1)
                    dve.sem_inc(ps_free[n % 2], 1)
                dve.sem_inc(out_ready, 1)


def layer1_inputs(i):
    wf = i["L1_conv_Wf"]
    col = {n: i[f"L1_conv_{n}"].reshape(C, 1) for n in ("bh", "gamma", "beta")}
    bf = i["L1_conv_bf"]
    return {
        "w_f": wf[:, :2 * C], "w_gate": np.broadcast_to(wf[:, 2 * C:, None], (C, 4, P)),
        "b_gate": np.broadcast_to(bf[2 * C:], (P, 4)), "b_f": bf[:2 * C].reshape(2, C).T,
        "taps": np.concatenate([i[f"L1_conv_k{n}"].reshape(-1, C) for n in range(3)]).T,
        "w_h": i["L1_conv_Wh"], "b_h": col["bh"], "gamma": col["gamma"], "beta": col["beta"],
        "w_p": i["L1_conv_Wp"], "b_p": np.broadcast_to(i["L1_conv_bp"], (P, C)),
    }

def token_norm_vector(nc, dve, xt, xn, stats, mv, rstd, eps, chain, var_ready, std_ready):
    for t in range(T):
        ins = nc.vector.bn_stats(stats[:, t, :], xt[:, t, :])
    ins.then_inc(chain, 1)
    dve.wait_ge(chain, 1)
    dve.sem_inc(chain, -1)
    for t in range(T):
        ins = nc.vector.bn_aggr(mv[:, t, :], stats[:, t, :])
    ins.then_inc(chain, 1)
    dve.wait_ge(chain, 1)
    dve.sem_inc(chain, -1)
    nc.vector.tensor_scalar(rstd[:], mv[:, :, 1], eps, None, ALU.add).then_inc(chain, 1)
    dve.wait_ge(chain, 1)
    dve.sem_inc(chain, -1)
    nc.vector.reciprocal(rstd[:], rstd[:]).then_inc(chain, 1)
    dve.wait_ge(chain, 1)
    dve.sem_inc(chain, -1)
    dve.sem_inc(var_ready, 1)
    dve.wait_ge(std_ready, 1)
    dve.sem_inc(std_ready, -1)
    for t in range(T):
        ins = nc.vector.tensor_scalar(xn[:, t, :], xt[:, t, :], mv[:, t, 0:1], rstd[:, t:t + 1], ALU.subtract, ALU.mult)
    ins.then_inc(chain, 1)
    dve.wait_ge(chain, 1)
    dve.sem_inc(chain, -1)


NH, HD, DS = 4, 64, 64
DI = NH * HD
CONV = DI + 2 * DS
KC = 4


def layer2_mamba(nc, x, out, w):
    with ExitStack() as stack:
        s = Scope(nc, "l2a", stack)
        ident, ones = s.sb("ident", [P, P]), s.sb("ones", [P, P])
        upto, behind = s.sb("upto", [P, 2, P]), s.sb("behind", [P, 2, P])
        quarter = s.sb("quarter", [P, 2, P])
        w_conv = s.sb("w_conv", [P, 2, KC, CONV])
        w_xbc, w_z, w_dt = s.sb("w_xbc", [P, 2, CONV]), s.sb("w_z", [P, 2, DI]), s.sb("w_dt", [P, 2 * NH])
        b_conv, b_dt = s.sb("b_conv", [1, 2, CONV]), s.sb("b_dt", [P, 2 * NH])
        a_log, d_half = s.sb("a_log", [P, 2 * NH]), s.sb("d_half", [P, 2 * NH])
        w_out, norm = s.sb("w_out", [P, 2, 2, C]), s.sb("norm", [P, 2, 2])
        xt, xT = s.sb("xt", [P, T, C]), s.sb("xT", [P, KC - 1 + N + KC - 1])
        hidden = [s.sb(f"hidden{d}", [P, T, C]) for d in range(2)]
        stats, mv, rstd = s.sb("stats", [P, T, 6]), s.sb("mv", [P, T, 2]), s.sb("rstd", [P, T])
        dt, soft, dA = s.sb("dt", [P, 2, T, NH]), s.sb("soft", [P, 2, T, NH]), s.sb("dA", [P, 2, T, NH])
        decay = s.sb("decay", [P, 2, 3, T, NH])
        squares, rms = s.sb("squares", [P, 2, T]), s.sb("rms", [P, 2, T])
        tanh_x, tanh_z = s.sb("tanh_x", [P, CONV]), s.sb("tanh_z", [P, DI])
        xbc, gate_z = [[s.sb(f"{n}{d}", [P, k]) for d in range(2)] for n, k in (("xbc", CONV), ("gate_z", DI))]
        xdt, xdec, xD = [[s.sb(f"{n}{d}", [P, DI]) for d in range(2)] for n in ("xdt", "xdec", "xD")]
        steps_, L = [[s.sb(f"{n}{d}", [P, NH, P]) for d in range(2)] for n in ("steps", "L")]
        M, cb, bcT = s.sb("M", [P, NH, P]), s.sb("cb", [P, P]), s.sb("bcT", [DS, 2, P])
        state = [s.sb(f"state{d}", [DS, DI]) for d in range(2)]
        y, ygT, scrap = s.sb("y", [P, DI]), s.sb("ygT", [P, 2, P]), s.sb("scrap", [P, DI])
        ps_x, ps_z, ps_bc, ps_seg, ps_y, ps_s, ps_t, ps_o = (s.ps("ps_" + n) for n in ("x", "z", "bc", "seg", "y", "s", "t", "o"))

        names = ("consts x_loaded xt_free normed x_ready x_done var_ready std_ready dve_chain act_chain pool_chain weights_ready "
                 "setup_exp setup_done dt_ready dt_used abs_ready soft_ready dA_ready cum_ready decay_ready scan_go_pe scan_go_pool xbc_ready tanh_x_ready "
                 "bc_ready z_ready z_free tanh_z_ready tr_ready bct_ready cb_ready cbm_ready steps_ready seg_ready l_ready m_ready "
                 "xdt_ready xdec_ready xd_ready y_ready yg_ready yg_ready_act yt_ready ygt_ready out_ready batch_done rms_in rms_out "
                 "result_ready stored").split()
        S = {n: s.sem(n) for n in names}
        loads = [(ident, "ident"), (ones, "ones"), (upto, "upto2"), (behind, "behind2"), (w_conv, "conv_w"), (w_xbc, "w_xbc"),
                 (w_z, "w_z"), (w_dt, "w_dt"), (b_conv, "conv_b"), (b_dt, "dt_bias"), (a_log, "A_log"), (d_half, "D"),
                 (w_out, "w_out"), (norm, "norm_w")]
        NC = 16 * len(loads)
        block = s.block()
        STEPS = [(n % 2, n // 2 if n % 2 == 0 else T - 1 - n // 2) for n in range(2 * T)]

        @block.sync
        def _(sp):
            for dst, name in loads:
                sp.dma_start(dst[:], w[name]).then_inc(S["consts"], 16)
            with sp.Fori(0, B) as b:
                sp.wait_ge(S["xt_free"], 1)
                sp.sem_inc(S["xt_free"], -1)
                load_tokens(sp, xt, x, b, S["x_loaded"])
                sp.wait_ge(S["result_ready"], 1)
                sp.sem_inc(S["result_ready"], -1)
                for n in range(LOADS):
                    h = T // LOADS
                    dst = out[bass.ds(b, 1), n * h * P:(n + 1) * h * P, :].rearrange("a (t p) c -> p (a t) c", p=P)
                    sp.dma_start(dst, xt[:, n * h:(n + 1) * h, :]).then_inc(S["stored"], 16)
                sp.wait_ge(S["stored"], 16 * LOADS)
                sp.sem_inc(S["stored"], -16 * LOADS)
                sp.sem_inc(S["xt_free"], 1)

        @block.tensor
        def _(pe):
            pe.wait_ge(S["consts"], NC)
            pe.wait_ge(S["weights_ready"], 1)
            banks = [ps_x, ps_z]

            def project_x(n):
                d, t = STEPS[n]
                for i in range(KC):
                    at = t * P + (i if d == 0 else 2 * (KC - 1) - i)
                    nc.tensor.matmul(ps_x[:, 0:CONV], xT[:, at:at + P], w_conv[:, d, i, :], start=(i == 0), stop=False)
                nc.tensor.matmul(ps_x[:, 0:CONV], ones[0:1, :], b_conv[:, d, :], start=False, stop=True).then_inc(S["xbc_ready"], 1)

            def project_z(n):
                d, t = STEPS[n]
                pe.wait_ge(S["z_free"], 1)
                pe.sem_inc(S["z_free"], -1)
                nc.tensor.matmul(ps_z[:, 0:DI], xT[:, KC - 1 + t * P:KC - 1 + (t + 1) * P], w_z[:, d, :], start=True, stop=True
                                 ).then_inc(S["z_ready"], 1)

            def segments(n):
                pe.wait_ge(S["steps_ready"], 1)
                pe.sem_inc(S["steps_ready"], -1)
                nc.tensor.matmul(ps_seg[:], behind[:, STEPS[n][0], :], steps_[n % 2][:].rearrange("p h l -> p (h l)"),
                                 start=True, stop=True).then_inc(S["seg_ready"], 1)

            def finish(n):
                d, t = STEPS[n]
                pe.wait_ge(S["yg_ready"], 1)
                pe.sem_inc(S["yg_ready"], -1)
                nc.tensor.transpose(ps_t[:, 0:P], y[:, 0:P], ident[:])
                nc.tensor.transpose(ps_t[:, P:2 * P], y[:, P:2 * P], ident[:]).then_inc(S["yt_ready"], 1)
                pe.wait_ge(S["ygt_ready"], 1)
                pe.sem_inc(S["ygt_ready"], -1)
                nc.tensor.matmul(ps_o[:, 0:C], ygT[:, 0, :], w_out[:, d, 0, :], start=True, stop=False)
                nc.tensor.matmul(ps_o[:, 0:C], ygT[:, 1, :], w_out[:, d, 1, :], start=False, stop=True).then_inc(S["out_ready"], 1)

            with pe.Fori(0, B) as b:
                pe.wait_ge(S["normed"], 1)
                pe.sem_inc(S["normed"], -1)
                for n in range(NB):
                    if n >= 2:
                        pe.wait_ge(S["x_done"], 1)
                        pe.sem_inc(S["x_done"], -1)
                    for k in range(4):
                        ins = nc.tensor.transpose(banks[n % 2][:, k * P:(k + 1) * P], hidden[0][:, 4 * n + k, :], ident[:])
                    ins.then_inc(S["x_ready"], 1)
                pe.wait_ge(S["x_done"], 2)
                pe.sem_inc(S["x_done"], -2)
                for t in range(T):
                    ins = nc.tensor.matmul(ps_seg[:, t * 2 * NH:(t + 1) * 2 * NH], xT[:, KC - 1 + t * P:KC - 1 + (t + 1) * P], w_dt[:],
                                           start=True, stop=True)
                ins.then_inc(S["dt_ready"], 1)
                pe.wait_ge(S["dA_ready"], 1)
                pe.sem_inc(S["dA_ready"], -1)
                for d, bank in ((0, ps_y), (1, ps_s)):
                    rhs = dA[:, d].rearrange("p t h -> p (t h)")
                    for k, mask in enumerate((upto[:, d, :], behind[:, d, :], ones[:])):
                        ins = nc.tensor.matmul(bank[:, k * P:(k + 1) * P], mask, rhs, start=True, stop=True)
                ins.then_inc(S["cum_ready"], 1)
                pe.wait_ge(S["scan_go_pe"], 1)
                pe.sem_inc(S["scan_go_pe"], -1)
                project_x(0)
                project_z(0)
                segments(0)
                for n, (d, t) in enumerate(STEPS):
                    last = n == 2 * T - 1
                    pe.wait_ge(S["bc_ready"], 1)
                    pe.sem_inc(S["bc_ready"], -1)
                    nc.tensor.transpose(ps_bc[0:DS, 0:P], xbc[d][:, DI:DI + DS], ident[:])
                    nc.tensor.transpose(ps_bc[0:DS, P:2 * P], xbc[d][:, DI + DS:], ident[:]).then_inc(S["tr_ready"], 1)
                    if not last:
                        project_x(n + 1)
                    pe.wait_ge(S["bct_ready"], 1)
                    pe.sem_inc(S["bct_ready"], -1)
                    nc.tensor.matmul(ps_bc[:, 2 * P:3 * P], bcT[:, 0, :], bcT[:, 1, :], start=True, stop=True).then_inc(S["cb_ready"], 1)
                    if not last:
                        project_z(n + 1)
                        segments(n + 1)
                    if n:
                        finish(n - 1)
                    pe.wait_ge(S["m_ready"], 1)
                    pe.sem_inc(S["m_ready"], -1)
                    for h in range(NH):
                        nc.tensor.matmul(ps_y[:, h * HD:(h + 1) * HD], M[:, h, :], xdt[d][:, h * HD:(h + 1) * HD], start=True, stop=True)
                    nc.tensor.matmul(ps_y[:, DI:2 * DI], bcT[:, 1, :], state[d][:], start=True, stop=True)
                    pe.wait_ge(S["xdec_ready"], 1)
                    pe.sem_inc(S["xdec_ready"], -1)
                    nc.tensor.matmul(ps_s[0:DS, 0:DI], xbc[d][:, DI:DI + DS], xdec[d][:], start=True, stop=True).then_inc(S["y_ready"], 1)
                finish(2 * T - 1)

        @block.scalar
        def _(act):
            act.wait_ge(S["consts"], NC)
            nc.scalar.activation(a_log[:], a_log[:], ACT.Exp).then_inc(S["setup_exp"], 1)

            def activate_x(n):
                act.wait_ge(S["xbc_ready"], 1)
                act.sem_inc(S["xbc_ready"], -1)
                nc.scalar.activation(tanh_x[:], ps_x[:, 0:CONV], ACT.Tanh, scale=0.5).then_inc(S["tanh_x_ready"], 1)

            def activate_z(n):
                act.wait_ge(S["z_ready"], 1)
                act.sem_inc(S["z_ready"], -1)
                nc.scalar.activation(tanh_z[:], ps_z[:, 0:DI], ACT.Tanh, scale=0.5).then_inc(S["tanh_z_ready"], 1)

            def exponentials(n):
                act.wait_ge(S["seg_ready"], 1)
                act.sem_inc(S["seg_ready"], -1)
                nc.scalar.activation(L[n % 2][:].rearrange("p h l -> p (h l)"), ps_seg[:], ACT.Exp).then_inc(S["l_ready"], 1)

            def finish(n):
                d, t = STEPS[n]
                act.wait_ge(S["yt_ready"], 1)
                act.sem_inc(S["yt_ready"], -1)
                nc.scalar.copy(ygT[:].rearrange("p a l -> p (a l)"), ps_t[:, 0:DI]).then_inc(S["ygt_ready"], 1)
                act.wait_ge(S["out_ready"], 1)
                act.sem_inc(S["out_ready"], -1)
                nc.scalar.copy(hidden[d][:, t, :], ps_o[:, 0:C]).then_inc(act_chain, 1)
                act.wait_ge(act_chain, 1)
                act.sem_inc(act_chain, -1)

            act_chain = S["act_chain"]
            with act.Fori(0, B) as b:
                act.wait_ge(S["var_ready"], 1)
                act.sem_inc(S["var_ready"], -1)
                nc.scalar.activation(rstd[:], rstd[:], ACT.Sqrt).then_inc(S["std_ready"], 1)
                for n in range(NB):
                    act.wait_ge(S["x_ready"], 1)
                    act.sem_inc(S["x_ready"], -1)
                    nc.scalar.copy(xT[:, KC - 1 + n * BANK:KC - 1 + (n + 1) * BANK], (ps_x, ps_z)[n % 2][:]).then_inc(S["x_done"], 1)
                act.wait_ge(S["abs_ready"], 1)
                act.sem_inc(S["abs_ready"], -1)
                nc.scalar.activation(soft[:], soft[:], ACT.Exp, scale=-1.0).then_inc(act_chain, 1)
                act.wait_ge(act_chain, 1)
                act.sem_inc(act_chain, -1)
                nc.scalar.activation(soft[:], soft[:], ACT.Ln, bias=1.0).then_inc(S["soft_ready"], 1)
                act.wait_ge(S["cum_ready"], 1)
                act.sem_inc(S["cum_ready"], -1)
                for d, bank in ((0, ps_y), (1, ps_s)):
                    ins = nc.scalar.activation(decay[:, d].rearrange("p k t h -> p (k t h)"), bank[:, 0:3 * P], ACT.Exp)
                ins.then_inc(S["decay_ready"], 1)
                activate_x(0)
                activate_z(0)
                exponentials(0)
                for n, (d, t) in enumerate(STEPS):
                    act.wait_ge(S["tr_ready"], 1)
                    act.sem_inc(S["tr_ready"], -1)
                    nc.scalar.copy(bcT[:].rearrange("p a l -> p (a l)"), ps_bc[0:DS, 0:2 * P]).then_inc(S["bct_ready"], 1)
                    if n < 2 * T - 1:
                        activate_x(n + 1)
                        activate_z(n + 1)
                        exponentials(n + 1)
                    if n:
                        finish(n - 1)
                    act.wait_ge(S["yg_ready_act"], 1)
                    act.sem_inc(S["yg_ready_act"], -1)
                    nc.scalar.activation(scrap[:], y[:], ACT.Square, accum_out=squares[:, d, t:t + 1]).then_inc(act_chain, 1)
                    act.wait_ge(act_chain, 1)
                    act.sem_inc(act_chain, -1)
                finish(2 * T - 1)
                act.sem_inc(S["batch_done"], 1)
                act.wait_ge(S["rms_in"], 1)
                act.sem_inc(S["rms_in"], -1)
                nc.scalar.activation(rms[:], rms[:], ACT.Sqrt).then_inc(S["rms_out"], 1)

        def heads(ap):
            return ap.rearrange("p (h c) -> p h c", h=NH)

        def per_head(ap, parts=P, width=HD):
            return ap.unsqueeze(2).to_broadcast([parts, NH, width])

        @block.gpsimd
        def _(pool):
            pool.wait_ge(S["consts"], NC)

            def make_steps(n):
                d, t = STEPS[n]
                nc.gpsimd.tensor_tensor(steps_[n % 2][:], upto[:, d:d + 1, :].to_broadcast([P, NH, P]),
                                                   per_head(dA[:, d, t, :], P, P), ALU.mult).then_inc(S["pool_chain"], 1)
                pool.wait_ge(S["pool_chain"], 1)
                pool.sem_inc(S["pool_chain"], -1)
                pool.sem_inc(S["steps_ready"], 1)

            def scale_x(n):
                d, t = STEPS[n]
                pool.wait_ge(S["xdt_ready"], 1)
                pool.sem_inc(S["xdt_ready"], -1)
                nc.gpsimd.tensor_tensor(heads(xdec[d][:]), heads(xdt[d][:]), per_head(decay[:, d, 1, t, :]), ALU.mult).then_inc(S["pool_chain"], 1)
                pool.wait_ge(S["pool_chain"], 1)
                pool.sem_inc(S["pool_chain"], -1)
                pool.sem_inc(S["xdec_ready"], 1)
                nc.gpsimd.tensor_tensor(heads(xD[d][:]), heads(xbc[d][:, 0:DI]), per_head(d_half[:, d * NH:(d + 1) * NH]),
                                                   ALU.mult).then_inc(S["pool_chain"], 1)
                pool.wait_ge(S["pool_chain"], 1)
                pool.sem_inc(S["pool_chain"], -1)
                pool.sem_inc(S["xd_ready"], 1)

            with pool.Fori(0, B) as b:
                pool.wait_ge(S["scan_go_pool"], 1)
                pool.sem_inc(S["scan_go_pool"], -1)
                make_steps(0)
                make_steps(1)
                scale_x(0)
                for n, (d, t) in enumerate(STEPS):
                    pool.wait_ge(S["l_ready"], 1)
                    pool.sem_inc(S["l_ready"], -1)
                    pool.wait_ge(S["cbm_ready"], 1)
                    pool.sem_inc(S["cbm_ready"], -1)
                    nc.gpsimd.tensor_tensor(M[:], L[n % 2][:], cb[:].unsqueeze(1).to_broadcast([P, NH, P]), ALU.mult).then_inc(S["pool_chain"], 1)
                    pool.wait_ge(S["pool_chain"], 1)
                    pool.sem_inc(S["pool_chain"], -1)
                    pool.sem_inc(S["m_ready"], 1)
                    if n + 2 < 2 * T:
                        make_steps(n + 2)
                    if n + 1 < 2 * T:
                        scale_x(n + 1)

        @block.vector
        def _(dve):
            chain = S["dve_chain"]
            nc.vector.memset(xT[:, 0:KC - 1], 0.0)
            nc.vector.memset(xT[:, KC - 1 + N:], 0.0)
            dve.wait_ge(S["consts"], NC)
            for d in range(2):
                for i in range(KC):
                    nc.vector.tensor_tensor(w_conv[:, d, i, :], w_conv[:, d, i, :], w_xbc[:, d, :], ALU.mult)
                for k in range(2):
                    nc.vector.tensor_scalar(w_out[:, d, k, :], w_out[:, d, k, :], norm[:, d, k:k + 1], None, ALU.mult)
            nc.vector.tensor_scalar(quarter[:], upto[:], 0.25, None, ALU.mult)
            nc.vector.tensor_scalar(d_half[:], d_half[:], 0.5, None, ALU.mult)
            dve.wait_ge(S["setup_exp"], 1)
            nc.vector.tensor_scalar(a_log[:], a_log[:], -1.0, None, ALU.mult).then_inc(chain, 1)
            dve.wait_ge(chain, 1)
            dve.sem_inc(chain, -1)
            dve.sem_inc(S["weights_ready"], 1)
            dve.sem_inc(S["xt_free"], 1)

            def make_x(n):
                d, t = STEPS[n]
                dve.wait_ge(S["tanh_x_ready"], 1)
                dve.sem_inc(S["tanh_x_ready"], -1)
                nc.vector.scalar_tensor_tensor(out=xbc[d][:], in0=tanh_x[:], scalar=1.0, in1=ps_x[:, 0:CONV],
                                                         op0=ALU.add, op1=ALU.mult).then_inc(chain, 1)
                dve.wait_ge(chain, 1)
                dve.sem_inc(chain, -1)
                dve.sem_inc(S["bc_ready"], 1)
                nc.vector.tensor_tensor(heads(xdt[d][:]), heads(xbc[d][:, 0:DI]), per_head(dt[:, d, t, :]), ALU.mult).then_inc(chain, 1)
                dve.wait_ge(chain, 1)
                dve.sem_inc(chain, -1)
                dve.sem_inc(S["xdt_ready"], 1)

            def make_z(n):
                dve.wait_ge(S["tanh_z_ready"], 1)
                dve.sem_inc(S["tanh_z_ready"], -1)
                nc.vector.scalar_tensor_tensor(out=gate_z[STEPS[n][0]][:], in0=tanh_z[:], scalar=1.0, in1=ps_z[:, 0:DI],
                                                         op0=ALU.add, op1=ALU.mult).then_inc(chain, 1)
                dve.wait_ge(chain, 1)
                dve.sem_inc(chain, -1)
                dve.sem_inc(S["z_free"], 1)

            with dve.Fori(0, B) as b:
                dve.wait_ge(S["x_loaded"], 16 * LOADS)
                dve.sem_inc(S["x_loaded"], -16 * LOADS)
                token_norm_vector(nc, dve, xt, hidden[0], stats, mv, rstd, 1e-5, chain, S["var_ready"], S["std_ready"])
                for d in range(2):
                    ins = nc.vector.memset(state[d][:], 0.0)
                ins.then_inc(chain, 1)
                dve.wait_ge(chain, 1)
                dve.sem_inc(chain, -1)
                dve.sem_inc(S["normed"], 1)
                dve.wait_ge(S["dt_ready"], 1)
                dve.sem_inc(S["dt_ready"], -1)
                raw = ps_seg[:, 0:T * 2 * NH].rearrange("p (t d h) -> p d t h", d=2, h=NH)
                bias = b_dt[:].rearrange("p (d h) -> p d h", d=2).unsqueeze(2).to_broadcast([P, 2, T, NH])
                for d in range(2):
                    ins = nc.vector.tensor_tensor(dt[:, d], raw[:, d], bias[:, d], ALU.add)
                ins.then_inc(chain, 1)
                dve.wait_ge(chain, 1)
                dve.sem_inc(chain, -1)
                flat = [v[:].rearrange("p d t h -> p (d t h)") for v in (dt, soft, dA)]
                nc.vector.scalar_tensor_tensor(out=flat[1], in0=flat[0], scalar=-1.0, in1=flat[0],
                                                         op0=ALU.mult, op1=ALU.max).then_inc(chain, 1)
                dve.wait_ge(chain, 1)
                dve.sem_inc(chain, -1)
                dve.sem_inc(S["abs_ready"], 1)
                dve.wait_ge(S["soft_ready"], 1)
                dve.sem_inc(S["soft_ready"], -1)
                nc.vector.scalar_tensor_tensor(out=flat[0], in0=flat[0], scalar=0.0, in1=flat[1],
                                                         op0=ALU.max, op1=ALU.add).then_inc(chain, 1)
                dve.wait_ge(chain, 1)
                dve.sem_inc(chain, -1)
                a = a_log[:].rearrange("p (d h) -> p d h", d=2)
                for d in range(2):
                    ins = nc.vector.tensor_tensor(dA[:, d], dt[:, d], a[:, d:d + 1, :].to_broadcast([P, T, NH]), ALU.mult)
                ins.then_inc(chain, 1)
                dve.wait_ge(chain, 1)
                dve.sem_inc(chain, -1)
                dve.sem_inc(S["dA_ready"], 1)
                nc.vector.tensor_scalar(flat[0], flat[0], 0.5, None, ALU.mult).then_inc(chain, 1)
                dve.wait_ge(chain, 1)
                dve.sem_inc(chain, -1)
                dve.wait_ge(S["decay_ready"], 1)
                dve.sem_inc(S["decay_ready"], -1)
                for d in range(2):
                    v = decay[:, d, 0:2].rearrange("p k t h -> p (k t h)")
                    ins = nc.vector.tensor_scalar(v, v, 0.5, None, ALU.mult)
                ins.then_inc(chain, 1)
                dve.wait_ge(chain, 1)
                dve.sem_inc(chain, -1)
                dve.sem_inc(S["scan_go_pe"], 1)
                dve.sem_inc(S["scan_go_pool"], 1)
                dve.sem_inc(S["z_free"], 1)
                make_x(0)
                make_z(0)
                for n, (d, t) in enumerate(STEPS):
                    dve.wait_ge(S["cb_ready"], 1)
                    dve.sem_inc(S["cb_ready"], -1)
                    nc.vector.tensor_tensor(cb[:], ps_bc[:, 2 * P:3 * P], quarter[:, d, :], ALU.mult).then_inc(chain, 1)
                    dve.wait_ge(chain, 1)
                    dve.sem_inc(chain, -1)
                    dve.sem_inc(S["cbm_ready"], 1)
                    if n < 2 * T - 1:
                        make_x(n + 1)
                        make_z(n + 1)
                    dve.wait_ge(S["y_ready"], 1)
                    dve.sem_inc(S["y_ready"], -1)
                    nc.vector.tensor_tensor(heads(y[:]), heads(ps_y[:, DI:2 * DI]), per_head(decay[:, d, 0, t, :]), ALU.mult).then_inc(chain, 1)
                    dve.wait_ge(chain, 1)
                    dve.sem_inc(chain, -1)
                    nc.vector.tensor_tensor(y[:], y[:], ps_y[:, 0:DI], ALU.add).then_inc(chain, 1)
                    dve.wait_ge(chain, 1)
                    dve.sem_inc(chain, -1)
                    dve.wait_ge(S["xd_ready"], 1)
                    dve.sem_inc(S["xd_ready"], -1)
                    nc.vector.tensor_tensor(y[:], y[:], xD[d][:], ALU.add).then_inc(chain, 1)
                    dve.wait_ge(chain, 1)
                    dve.sem_inc(chain, -1)
                    nc.vector.tensor_tensor(y[:], y[:], gate_z[d][:], ALU.mult).then_inc(chain, 1)
                    dve.wait_ge(chain, 1)
                    dve.sem_inc(chain, -1)
                    dve.sem_inc(S["yg_ready"], 1)
                    dve.sem_inc(S["yg_ready_act"], 1)
                    nc.vector.tensor_tensor(heads(state[d][:]), heads(state[d][:]), per_head(decay[0:DS, d, 2, t, :], DS), ALU.mult).then_inc(chain, 1)
                    dve.wait_ge(chain, 1)
                    dve.sem_inc(chain, -1)
                    nc.vector.tensor_tensor(state[d][:], state[d][:], ps_s[0:DS, 0:DI], ALU.add).then_inc(chain, 1)
                    dve.wait_ge(chain, 1)
                    dve.sem_inc(chain, -1)
                dve.wait_ge(S["z_free"], 1)
                dve.sem_inc(S["z_free"], -1)
                dve.wait_ge(S["batch_done"], 1)
                dve.sem_inc(S["batch_done"], -1)
                nc.vector.tensor_scalar(rms[:], squares[:], 1.0 / DI, 4e-5, ALU.mult, ALU.add).then_inc(chain, 1)
                dve.wait_ge(chain, 1)
                dve.sem_inc(chain, -1)
                nc.vector.reciprocal(rms[:], rms[:]).then_inc(chain, 1)
                dve.wait_ge(chain, 1)
                dve.sem_inc(chain, -1)
                dve.sem_inc(S["rms_in"], 1)
                dve.wait_ge(S["rms_out"], 1)
                dve.sem_inc(S["rms_out"], -1)
                for d in range(2):
                    for t in range(T):
                        ins = nc.vector.scalar_tensor_tensor(out=xt[:, t, :], in0=hidden[d][:, t, :], scalar=rms[:, d, t:t + 1],
                                                             in1=xt[:, t, :], op0=ALU.mult, op1=ALU.add)
                    ins.then_inc(chain, 1)
                    dve.wait_ge(chain, 1)
                    dve.sem_inc(chain, -1)
                dve.sem_inc(S["result_ready"], 1)


def layer2_mamba_inputs(i):
    dirs = [{k[len(f"L2_attn_{d}_"):]: v for k, v in i.items() if k.startswith(f"L2_attn_{d}_")} for d in ("fwd", "bwd")]
    both = lambda name, f: np.stack([f(d[name]) for d in dirs], 1)
    rows = lambda a: np.broadcast_to(a.reshape(1, -1), (P, a.size))
    return {
        "conv_w": np.broadcast_to(np.stack([d["conv_w"].T for d in dirs])[None], (P, 2, KC, CONV)),
        "w_xbc": both("in_proj", lambda a: a[:, DI:DI + CONV]), "w_z": both("in_proj", lambda a: a[:, :DI]),
        "w_dt": both("in_proj", lambda a: a[:, DI + CONV:]).reshape(C, 2 * NH),
        "conv_b": np.stack([d["conv_b"] for d in dirs])[None], "dt_bias": rows(np.stack([d["dt_bias"] for d in dirs])),
        "A_log": rows(np.stack([d["A_log"] for d in dirs])), "D": rows(np.stack([d["D"] for d in dirs])),
        "w_out": both("out_proj", lambda a: a.reshape(2, P, C).transpose(1, 0, 2)),
        "norm_w": both("norm_w", lambda a: a.reshape(2, P).T),
    }

def store_tokens(engine, dst, src, b, stored):
    h = T // LOADS
    for n in range(LOADS):
        tokens = dst[bass.ds(b, 1), n * h * P:(n + 1) * h * P, :].rearrange("a (t p) c -> p (a t) c", p=P)
        engine.dma_start(tokens, src[:, n * h:(n + 1) * h, :]).then_inc(stored, 16)


NE = 8


def layer2_experts(nc, x, out, w):
    with ExitStack() as stack:
        s = Scope(nc, "l2f", stack)
        ident, w_r, b_r = s.sb("ident", [P, P]), s.sb("w_r", [P, NE]), s.sb("b_r", [P, NE])
        w_e, b_e, order = s.sb("w_e", [P, NE * C]), s.sb("b_e", [NE, C]), s.sb("order", [P, NE])
        xt, xn, xT = s.sb("xt", [P, T, C]), s.sb("xn", [P, T, C]), s.sb("xT", [P, N])
        stats, mv, rstd = s.sb("stats", [P, T, 6]), s.sb("mv", [P, T, 2]), s.sb("rstd", [P, T])
        prob, pick, first, gates = (s.sb(n, [P, T, NE]) for n in ("prob", "pick", "first", "gates"))
        top = s.sb("top", [P, T])
        gT, other = s.sb("gT", [NE, N]), s.sb("other", [P, C])
        experts = [[s.ps(f"experts{n}{k}") for k in range(2)] for n in range(2)]
        ps_bias, ps_r, ps_t = s.ps("ps_bias"), s.ps("ps_r"), [s.ps(f"ps_t{n}") for n in range(1)]
        ps_tr = [ps_t[0], ps_bias]
        names = ("consts x_loaded xt_free var_ready std_ready normed tr_ready tr_free logits_ready exp_in exp_out gates_ready gT_ready gT_free "
                 "gT_done experts_ready stored result_ready dve_chain act_chain").split()
        S = {n: s.sem(n) for n in names}
        experts_free = [s.sem(f"experts_free{n}") for n in range(2)]
        bias_free = s.sem("bias_free")
        loads = [(ident, "ident"), (w_r, "w_r"), (b_r, "b_r"), (w_e, "w_e"), (b_e, "b_e"), (order, "order")]
        NC = 16 * len(loads)
        block = s.block()

        @block.sync
        def _(sp):
            for dst, name in loads:
                sp.dma_start(dst[:], w[name]).then_inc(S["consts"], 16)
            with sp.Fori(0, B) as b:
                sp.wait_ge(S["xt_free"], 1)
                sp.sem_inc(S["xt_free"], -1)
                load_tokens(sp, xt, x, b, S["x_loaded"])
                sp.wait_ge(S["result_ready"], 1)
                sp.sem_inc(S["result_ready"], -1)
                store_tokens(sp, out, xt, b, S["stored"])
                sp.wait_ge(S["stored"], 16 * LOADS)
                sp.sem_inc(S["stored"], -16 * LOADS)
                sp.sem_inc(S["xt_free"], 1)

        @block.tensor
        def _(pe):
            pe.wait_ge(S["consts"], NC)
            with pe.Fori(0, B) as b:
                pe.wait_ge(S["normed"], 1)
                pe.sem_inc(S["normed"], -1)
                for n in range(NB):
                    pe.wait_ge(S["tr_free"], 1)
                    pe.sem_inc(S["tr_free"], -1)
                    for k in range(4):
                        ins = nc.tensor.transpose(ps_tr[n % 2][:, k * P:(k + 1) * P], xn[:, 4 * n + k, :], ident[:])
                    ins.then_inc(S["tr_ready"], 1)
                pe.wait_ge(S["tr_free"], 2)
                pe.sem_inc(S["tr_free"], -2)
                for t in range(T):
                    ins = nc.tensor.matmul(ps_r[:, t * NE:(t + 1) * NE], xT[:, t * P:(t + 1) * P], w_r[:], start=True, stop=True)
                ins.then_inc(S["logits_ready"], 1)

                def products(t):
                    pe.wait_ge(experts_free[t % 2], 1)
                    pe.sem_inc(experts_free[t % 2], -1)
                    for k in range(2):
                        ins = nc.tensor.matmul(experts[t % 2][k][:], xT[:, t * P:(t + 1) * P], w_e[:, k * BANK:(k + 1) * BANK],
                                               start=True, stop=True)
                    return ins

                products(0)
                products(1)
                pe.wait_ge(S["gates_ready"], 1)
                pe.sem_inc(S["gates_ready"], -1)
                for n in range(NB):
                    pe.wait_ge(S["gT_free"], 1)
                    pe.sem_inc(S["gT_free"], -1)
                    for k in range(4):
                        ins = nc.tensor.transpose(ps_tr[n % 2][0:NE, k * P:(k + 1) * P], gates[:, 4 * n + k, :], ident[:])
                    ins.then_inc(S["gT_ready"], 1)
                pe.wait_ge(S["gT_free"], 2)
                pe.sem_inc(S["gT_free"], -2)
                pe.sem_inc(S["gT_done"], 1)
                for t in range(T):
                    if t >= 2:
                        products(t)
                    pe.wait_ge(bias_free, 1)
                    pe.sem_inc(bias_free, -1)
                    nc.tensor.matmul(ps_bias[:, 0:C], gT[:, t * P:(t + 1) * P], b_e[:], start=True, stop=True
                                     ).then_inc(S["experts_ready"], 1)

        @block.scalar
        def _(act):
            act.wait_ge(S["consts"], NC)
            with act.Fori(0, B) as b:
                act.wait_ge(S["var_ready"], 1)
                act.sem_inc(S["var_ready"], -1)
                nc.scalar.activation(rstd[:], rstd[:], ACT.Sqrt).then_inc(S["std_ready"], 1)
                act.sem_inc(S["tr_free"], 2)
                for n in range(NB):
                    act.wait_ge(S["tr_ready"], 1)
                    act.sem_inc(S["tr_ready"], -1)
                    nc.scalar.copy(xT[:, n * BANK:(n + 1) * BANK], ps_tr[n % 2][:]).then_inc(S["act_chain"], 1)
                    act.wait_ge(S["act_chain"], 1)
                    act.sem_inc(S["act_chain"], -1)
                    act.sem_inc(S["tr_free"], 1)
                act.wait_ge(S["exp_in"], 1)
                act.sem_inc(S["exp_in"], -1)
                nc.scalar.activation(prob[:], prob[:], ACT.Exp).then_inc(S["exp_out"], 1)
                act.sem_inc(S["gT_free"], 2)
                for n in range(NB):
                    act.wait_ge(S["gT_ready"], 1)
                    act.sem_inc(S["gT_ready"], -1)
                    nc.scalar.copy(gT[:, n * BANK:(n + 1) * BANK], ps_tr[n % 2][0:NE, :]).then_inc(S["act_chain"], 1)
                    act.wait_ge(S["act_chain"], 1)
                    act.sem_inc(S["act_chain"], -1)
                    act.sem_inc(S["gT_free"], 1)

        @block.vector
        def _(dve):
            chain = S["dve_chain"]
            dve.wait_ge(S["consts"], NC)
            dve.sem_inc(S["xt_free"], 1)
            for n in range(2):
                dve.sem_inc(experts_free[n], 1)
            dve.sem_inc(bias_free, 1)

            def by_token(ap):
                return ap.unsqueeze(2).to_broadcast([P, T, NE])

            def one_hot(dst, scores):
                nc.vector.tensor_reduce(top[:], scores, AX.X, ALU.max).then_inc(chain, 1)
                dve.wait_ge(chain, 1)
                dve.sem_inc(chain, -1)
                nc.vector.tensor_tensor(dst, scores, by_token(top[:]), ALU.is_equal).then_inc(chain, 1)
                dve.wait_ge(chain, 1)
                dve.sem_inc(chain, -1)
                nc.vector.tensor_tensor(dst, dst, order[:].unsqueeze(1).to_broadcast([P, T, NE]), ALU.mult).then_inc(chain, 1)
                dve.wait_ge(chain, 1)
                dve.sem_inc(chain, -1)
                nc.vector.tensor_reduce(top[:], dst, AX.X, ALU.max).then_inc(chain, 1)
                dve.wait_ge(chain, 1)
                dve.sem_inc(chain, -1)
                nc.vector.tensor_tensor(dst, dst, by_token(top[:]), ALU.is_equal).then_inc(chain, 1)
                dve.wait_ge(chain, 1)
                dve.sem_inc(chain, -1)

            with dve.Fori(0, B) as b:
                dve.wait_ge(S["x_loaded"], 16 * LOADS)
                dve.sem_inc(S["x_loaded"], -16 * LOADS)
                token_norm_vector(nc, dve, xt, xn, stats, mv, rstd, 1e-5, chain, S["var_ready"], S["std_ready"])
                dve.sem_inc(S["normed"], 1)
                dve.wait_ge(S["logits_ready"], 1)
                dve.sem_inc(S["logits_ready"], -1)
                logits = ps_r[:, 0:T * NE].rearrange("p (t e) -> p t e", e=NE)
                nc.vector.tensor_tensor(prob[:], logits, b_r[:].unsqueeze(1).to_broadcast([P, T, NE]), ALU.add).then_inc(chain, 1)
                dve.wait_ge(chain, 1)
                dve.sem_inc(chain, -1)
                nc.vector.tensor_reduce(top[:], prob[:], AX.X, ALU.max).then_inc(chain, 1)
                dve.wait_ge(chain, 1)
                dve.sem_inc(chain, -1)
                nc.vector.tensor_tensor(prob[:], prob[:], by_token(top[:]), ALU.subtract).then_inc(chain, 1)
                dve.wait_ge(chain, 1)
                dve.sem_inc(chain, -1)
                dve.sem_inc(S["exp_in"], 1)
                dve.wait_ge(S["exp_out"], 1)
                dve.sem_inc(S["exp_out"], -1)
                nc.vector.tensor_reduce(top[:], prob[:], AX.X, ALU.add).then_inc(chain, 1)
                dve.wait_ge(chain, 1)
                dve.sem_inc(chain, -1)
                nc.vector.reciprocal(top[:], top[:]).then_inc(chain, 1)
                dve.wait_ge(chain, 1)
                dve.sem_inc(chain, -1)
                nc.vector.tensor_tensor(prob[:], prob[:], by_token(top[:]), ALU.mult).then_inc(chain, 1)
                dve.wait_ge(chain, 1)
                dve.sem_inc(chain, -1)
                one_hot(first[:], prob[:])
                nc.vector.scalar_tensor_tensor(out=pick[:], in0=first[:], scalar=-2.0, in1=prob[:],
                                                         op0=ALU.mult, op1=ALU.add).then_inc(chain, 1)
                dve.wait_ge(chain, 1)
                dve.sem_inc(chain, -1)
                one_hot(gates[:], pick[:])
                nc.vector.tensor_tensor(gates[:], gates[:], first[:], ALU.add).then_inc(chain, 1)
                dve.wait_ge(chain, 1)
                dve.sem_inc(chain, -1)
                nc.vector.tensor_tensor(gates[:], gates[:], prob[:], ALU.mult).then_inc(chain, 1)
                dve.wait_ge(chain, 1)
                dve.sem_inc(chain, -1)
                nc.vector.tensor_reduce(top[:], gates[:], AX.X, ALU.add).then_inc(chain, 1)
                dve.wait_ge(chain, 1)
                dve.sem_inc(chain, -1)
                nc.vector.reciprocal(top[:], top[:]).then_inc(chain, 1)
                dve.wait_ge(chain, 1)
                dve.sem_inc(chain, -1)
                nc.vector.tensor_tensor(gates[:], gates[:], by_token(top[:]), ALU.mult).then_inc(chain, 1)
                dve.wait_ge(chain, 1)
                dve.sem_inc(chain, -1)
                dve.sem_inc(S["gates_ready"], 1)
                dve.wait_ge(S["gT_done"], 1)
                dve.sem_inc(S["gT_done"], -1)
                for t in range(T):
                    dve.wait_ge(S["experts_ready"], 1)
                    dve.sem_inc(S["experts_ready"], -1)
                    nc.vector.tensor_tensor(xt[:, t, :], xt[:, t, :], ps_bias[:, 0:C], ALU.add)
                    for e in range(NE // 2):
                        product, g = experts[t % 2][1][:, e * C:(e + 1) * C], gates[:, t, NE // 2 + e:NE // 2 + e + 1]
                        if e == 0:
                            nc.vector.tensor_scalar(other[:], product, g, None, ALU.mult).then_inc(chain, 1)
                            dve.wait_ge(chain, 1)
                            dve.sem_inc(chain, -1)
                            dve.sem_inc(bias_free, 1)
                        else:
                            nc.vector.scalar_tensor_tensor(out=other[:], in0=product, scalar=g, in1=other[:],
                                                                     op0=ALU.mult, op1=ALU.add).then_inc(chain, 1)
                            dve.wait_ge(chain, 1)
                            dve.sem_inc(chain, -1)
                        ins = nc.vector.scalar_tensor_tensor(out=xt[:, t, :], in0=experts[t % 2][0][:, e * C:(e + 1) * C],
                                                             scalar=gates[:, t, e:e + 1], in1=xt[:, t, :], op0=ALU.mult, op1=ALU.add)
                    ins.then_inc(chain, 1)
                    dve.wait_ge(chain, 1)
                    dve.sem_inc(chain, -1)
                    dve.sem_inc(experts_free[t % 2], 1)
                    nc.vector.tensor_tensor(xt[:, t, :], xt[:, t, :], other[:], ALU.add).then_inc(chain, 1)
                    dve.wait_ge(chain, 1)
                    dve.sem_inc(chain, -1)
                dve.sem_inc(S["result_ready"], 1)


def layer2_experts_inputs(i):
    return {
        "w_r": i["L2_ffn_router_w"], "b_r": np.broadcast_to(i["L2_ffn_router_b"], (P, NE)),
        "w_e": i["L2_ffn_expert_w"].transpose(1, 0, 2).reshape(C, NE * C), "b_e": i["L2_ffn_expert_b"],
        "order": np.broadcast_to(np.arange(NE, 0, -1, dtype=np.float32), (P, NE)),
    }


def layer3_attention(nc, x, out, w):
    AHEAD = 2
    with ExitStack() as stack:
        s = Scope(nc, "l3a", stack)
        ident = s.sb("ident", [P, P])
        shift = s.sb("shift", [P, 1])
        xt, xn, xT = s.sb("xt", [P, T, C]), s.sb("xn", [P, T, C]), s.sb("xT", [P, N])
        stats, mv, rstd = s.sb("stats", [P, T, 6]), s.sb("mv", [P, T, 2]), s.sb("rstd", [P, T])
        E = [s.sb(f"E{n}", [P, BANK]) for n in range(4)]
        sums, total, oT = s.sb("sums", [P, NB, T]), s.sb("total", [P, T]), s.sb("oT", [P, N])
        ps_s, ps_o = [s.ps(f"ps_s{n}") for n in range(4)], s.ps("ps_o")
        ps_t = [s.ps(f"ps_t{n}") for n in range(2)]
        names = ("consts x_loaded xt_free var_ready std_ready normed tr_ready tr_free s_ready s_free e_ready o_ready o_free oT_done "
                 "back_ready stored result_ready dve_chain act_chain sums_ready shift_ready").split()
        S = {n: s.sem(n) for n in names}
        back_free = s.sem("back_free")
        block = s.block()

        @block.sync
        def _(sp):
            sp.dma_start(ident[:], w["ident"]).then_inc(S["consts"], 16)
            with sp.Fori(0, B) as b:
                sp.wait_ge(S["xt_free"], 1)
                sp.sem_inc(S["xt_free"], -1)
                load_tokens(sp, xt, x, b, S["x_loaded"])
                sp.wait_ge(S["result_ready"], 1)
                sp.sem_inc(S["result_ready"], -1)
                store_tokens(sp, out, xt, b, S["stored"])
                sp.wait_ge(S["stored"], 16 * LOADS)
                sp.sem_inc(S["stored"], -16 * LOADS)
                sp.sem_inc(S["xt_free"], 1)

        @block.tensor
        def _(pe):
            pe.wait_ge(S["consts"], 16)
            with pe.Fori(0, B) as b:
                pe.wait_ge(S["normed"], 1)
                pe.sem_inc(S["normed"], -1)
                for n in range(NB):
                    pe.wait_ge(S["tr_free"], 1)
                    pe.sem_inc(S["tr_free"], -1)
                    for k in range(4):
                        ins = nc.tensor.transpose(ps_t[n % 2][:, k * P:(k + 1) * P], xn[:, 4 * n + k, :], ident[:])
                    ins.then_inc(S["tr_ready"], 1)
                pe.wait_ge(S["tr_free"], 2)
                pe.sem_inc(S["tr_free"], -2)
                with pe.Fori(0, NB) as n:
                    def scores(m):
                        pe.wait_ge(S["s_free"], 1)
                        pe.sem_inc(S["s_free"], -1)
                        nc.tensor.matmul(ps_s[m % 4][:], xT[:, m * P:(m + 1) * P], xT[:, bass.ds(n * BANK, BANK)],
                                         start=True, stop=True).then_inc(S["s_ready"], 1)

                    for m in range(AHEAD):
                        scores(m)
                    pe.wait_ge(S["o_free"], 1)
                    pe.sem_inc(S["o_free"], -1)
                    for m in range(T):
                        if m + AHEAD < T:
                            scores(m + AHEAD)
                        pe.wait_ge(S["e_ready"], 1)
                        pe.sem_inc(S["e_ready"], -1)
                        ins = nc.tensor.matmul(ps_o[:], xn[:, m, :], E[m % 4][:], start=(m == 0), stop=(m == T - 1))
                    ins.then_inc(S["o_ready"], 1)
                pe.wait_ge(S["oT_done"], 1)
                pe.sem_inc(S["oT_done"], -1)
                for n in range(NB):
                    pe.wait_ge(back_free, 1)
                    pe.sem_inc(back_free, -1)
                    for k in range(4):
                        t = 4 * n + k
                        ins = nc.tensor.transpose(ps_t[n % 2][:, k * P:(k + 1) * P], oT[:, t * P:(t + 1) * P], ident[:])
                    ins.then_inc(S["back_ready"], 1)

        @block.scalar
        def _(act):
            act.sem_inc(S["s_free"], 4)
            act.sem_inc(S["o_free"], 1)
            act.wait_ge(S["shift_ready"], 1)
            with act.Fori(0, B) as b:
                act.wait_ge(S["var_ready"], 1)
                act.sem_inc(S["var_ready"], -1)
                nc.scalar.activation(rstd[:], rstd[:], ACT.Sqrt).then_inc(S["std_ready"], 1)
                act.sem_inc(S["tr_free"], 2)
                for n in range(NB):
                    act.wait_ge(S["tr_ready"], 1)
                    act.sem_inc(S["tr_ready"], -1)
                    nc.scalar.copy(xT[:, n * BANK:(n + 1) * BANK], ps_t[n % 2][:]).then_inc(S["act_chain"], 1)
                    act.wait_ge(S["act_chain"], 1)
                    act.sem_inc(S["act_chain"], -1)
                    act.sem_inc(S["tr_free"], 1)
                with act.Fori(0, NB) as n:
                    for m in range(T):
                        act.wait_ge(S["s_ready"], 1)
                        act.sem_inc(S["s_ready"], -1)
                        row_sum = sums[:, bass.ds(n, 1), m:m + 1].rearrange("p a c -> p (a c)")
                        nc.scalar.activation(E[m % 4][:], ps_s[m % 4][:], ACT.Exp, bias=shift[:], accum_out=row_sum).then_inc(S["act_chain"], 1)
                        act.wait_ge(S["act_chain"], 1)
                        act.sem_inc(S["act_chain"], -1)
                        act.sem_inc(S["s_free"], 1)
                        act.sem_inc(S["e_ready"], 1)
                    act.wait_ge(S["o_ready"], 1)
                    act.sem_inc(S["o_ready"], -1)
                    nc.scalar.copy(oT[:, bass.ds(n * BANK, BANK)], ps_o[:]).then_inc(S["act_chain"], 1)
                    act.wait_ge(S["act_chain"], 1)
                    act.sem_inc(S["act_chain"], -1)
                    act.sem_inc(S["o_free"], 1)
                act.sem_inc(S["oT_done"], 1)
                act.sem_inc(S["sums_ready"], 1)

        @block.vector
        def _(dve):
            chain = S["dve_chain"]
            nc.vector.memset(shift[:], -C / 2.0).then_inc(S["shift_ready"], 1)
            dve.sem_inc(S["xt_free"], 1)
            dve.sem_inc(back_free, 2)
            with dve.Fori(0, B) as b:
                dve.wait_ge(S["x_loaded"], 16 * LOADS)
                dve.sem_inc(S["x_loaded"], -16 * LOADS)
                token_norm_vector(nc, dve, xt, xn, stats, mv, rstd, 1e-5, chain, S["var_ready"], S["std_ready"])
                dve.sem_inc(S["normed"], 1)
                dve.wait_ge(S["sums_ready"], 1)
                dve.sem_inc(S["sums_ready"], -1)
                nc.vector.tensor_reduce(total[:], sums[:].rearrange("p n t -> p t n"), AX.X, ALU.add).then_inc(chain, 1)
                dve.wait_ge(chain, 1)
                dve.sem_inc(chain, -1)
                nc.vector.reciprocal(total[:], total[:]).then_inc(chain, 1)
                dve.wait_ge(chain, 1)
                dve.sem_inc(chain, -1)
                for n in range(NB):
                    dve.wait_ge(S["back_ready"], 1)
                    dve.sem_inc(S["back_ready"], -1)
                    for t in range(4 * n, 4 * n + 4):
                        ins = nc.vector.scalar_tensor_tensor(out=xt[:, t, :], in0=ps_t[n % 2][:, t % 4 * P:(t % 4 + 1) * P],
                                                             scalar=total[:, t:t + 1], in1=xt[:, t, :], op0=ALU.mult, op1=ALU.add)
                    ins.then_inc(chain, 1)
                    dve.wait_ge(chain, 1)
                    dve.sem_inc(chain, -1)
                    dve.sem_inc(back_free, 1)
                dve.sem_inc(S["result_ready"], 1)


EX, HID = 64, 512
KH = HID // P


def layer3_experts(nc, x, out, chosen, w):
    with ExitStack() as outer:
        so = Scope(nc, "l3f", outer)
        pooled = so.sb("pooled", [P, B, EX])
        rows = so.sb("rows", [EX, B, C])
        ident = so.sb("ident", [P, P])
        with ExitStack() as stack:
            s = Scope(nc, "l3g", stack)
            gate_w, gate_b = s.sb("gate_w", [P, EX]), s.sb("gate_b", [EX, 1])
            xt, xn, xT = s.sb("xt", [P, T, C]), s.sb("xn", [P, T, C]), s.sb("xT", [P, N])
            stats, mv, rstd = s.sb("stats", [P, T, 6]), s.sb("mv", [P, T, 2]), s.sb("rstd", [P, T])
            prob, rest = s.sb("prob", [EX, N]), s.sb("rest", [EX, N])
            small, best = s.sb("small", [EX, 4]), s.sb("best", [EX, 8])
            chosen_T = s.sb("chosen_T", [P, T, EX])
            ps_t, ps_p = [s.ps(f"ps_t{n}") for n in range(2)], s.ps("ps_p")
            names = ("consts x_loaded xt_free var_ready std_ready normed tr_ready tr_free l_ready l_free logits_ready exp_in exp_out "
                     "chosen_ready chosen_store chosen_stored c_ready c_free pooled_ready pooled_done prob_free dve_chain act_chain").split()
            S = {n: s.sem(n) for n in names}
            block = s.block()

            @block.sync
            def _(sp):
                for dst, name in ((ident, "ident"), (gate_w, "gate_w"), (gate_b, "gate_b")):
                    sp.dma_start(dst[:], w[name]).then_inc(S["consts"], 16)
                with sp.Fori(0, B) as b:
                    sp.wait_ge(S["xt_free"], 1)
                    sp.sem_inc(S["xt_free"], -1)
                    load_tokens(sp, xt, x, b, S["x_loaded"])
                    sp.wait_ge(S["chosen_store"], 1)
                    sp.sem_inc(S["chosen_store"], -1)
                    sp.dma_start(chosen[bass.ds(b, 1)].rearrange("a e n -> e (a n)"), rest[:]).then_inc(S["chosen_stored"], 16)
                    sp.wait_ge(S["chosen_stored"], 16)
                    sp.sem_inc(S["chosen_stored"], -16)
                    sp.sem_inc(S["prob_free"], 1)

            @block.tensor
            def _(pe):
                pe.wait_ge(S["consts"], 48)
                with pe.Fori(0, B) as b:
                    pe.wait_ge(S["normed"], 1)
                    pe.sem_inc(S["normed"], -1)
                    for n in range(NB):
                        pe.wait_ge(S["tr_free"], 1)
                        pe.sem_inc(S["tr_free"], -1)
                        for k in range(4):
                            ins = nc.tensor.transpose(ps_t[n % 2][:, k * P:(k + 1) * P], xn[:, 4 * n + k, :], ident[:])
                        ins.then_inc(S["tr_ready"], 1)
                    pe.wait_ge(S["tr_free"], 2)
                    pe.sem_inc(S["tr_free"], -2)
                    for n in range(NB):
                        pe.wait_ge(S["l_free"], 1)
                        pe.sem_inc(S["l_free"], -1)
                        nc.tensor.matmul(ps_t[n % 2][0:EX, :], gate_w[:], xT[:, n * BANK:(n + 1) * BANK], start=True, stop=True
                                         ).then_inc(S["l_ready"], 1)
                    pe.wait_ge(S["l_free"], 2)
                    pe.sem_inc(S["l_free"], -2)
                    pe.wait_ge(S["chosen_ready"], 1)
                    pe.sem_inc(S["chosen_ready"], -1)
                    for n in range(NB // 2):
                        pe.wait_ge(S["c_free"], 1)
                        pe.sem_inc(S["c_free"], -1)
                        for k in range(8):
                            t = 8 * n + k
                            ins = nc.tensor.transpose(ps_t[n % 2][:, k * EX:(k + 1) * EX], rest[:, t * P:(t + 1) * P], ident[0:EX, 0:EX])
                        ins.then_inc(S["c_ready"], 1)
                    pe.wait_ge(S["c_free"], 2)
                    pe.sem_inc(S["c_free"], -2)
                    for t in range(T):
                        ins = nc.tensor.matmul(ps_p[:, 0:EX], xn[:, t, :], chosen_T[:, t, :], start=(t == 0), stop=(t == T - 1))
                    ins.then_inc(S["pooled_ready"], 1)

            @block.scalar
            def _(act):
                act.wait_ge(S["consts"], 48)
                chain = S["act_chain"]
                with act.Fori(0, B) as b:
                    act.wait_ge(S["var_ready"], 1)
                    act.sem_inc(S["var_ready"], -1)
                    nc.scalar.activation(rstd[:], rstd[:], ACT.Sqrt).then_inc(S["std_ready"], 1)
                    act.sem_inc(S["tr_free"], 2)
                    for n in range(NB):
                        act.wait_ge(S["tr_ready"], 1)
                        act.sem_inc(S["tr_ready"], -1)
                        nc.scalar.copy(xT[:, n * BANK:(n + 1) * BANK], ps_t[n % 2][:]).then_inc(chain, 1)
                        act.wait_ge(chain, 1)
                        act.sem_inc(chain, -1)
                        act.sem_inc(S["tr_free"], 1)
                    act.sem_inc(S["l_free"], 2)
                    for n in range(NB):
                        act.wait_ge(S["l_ready"], 1)
                        act.sem_inc(S["l_ready"], -1)
                        nc.scalar.activation(prob[:, n * BANK:(n + 1) * BANK], ps_t[n % 2][0:EX, :], ACT.Identity,
                                                       bias=gate_b[:, 0:1]).then_inc(chain, 1)
                        act.wait_ge(chain, 1)
                        act.sem_inc(chain, -1)
                        act.sem_inc(S["l_free"], 1)
                    act.sem_inc(S["logits_ready"], 1)
                    act.wait_ge(S["exp_in"], 1)
                    act.sem_inc(S["exp_in"], -1)
                    nc.scalar.activation(prob[:], prob[:], ACT.Exp, bias=small[:, 1:2], accum_out=small[:, 2:3]).then_inc(S["exp_out"], 1)
                    act.sem_inc(S["c_free"], 2)
                    for n in range(NB // 2):
                        act.wait_ge(S["c_ready"], 1)
                        act.sem_inc(S["c_ready"], -1)
                        nc.scalar.copy(chosen_T[:, 8 * n:8 * n + 8, :].rearrange("p t e -> p (t e)"), ps_t[n % 2][:]).then_inc(chain, 1)
                        act.wait_ge(chain, 1)
                        act.sem_inc(chain, -1)
                        act.sem_inc(S["c_free"], 1)
                    act.wait_ge(S["pooled_ready"], 1)
                    act.sem_inc(S["pooled_ready"], -1)
                    nc.scalar.copy(pooled[:, bass.ds(b, 1), :].rearrange("p a e -> p (a e)"), ps_p[:, 0:EX]).then_inc(chain, 1)
                    act.wait_ge(chain, 1)
                    act.sem_inc(chain, -1)
                    act.sem_inc(S["pooled_done"], 1)

            @block.vector
            def _(dve):
                chain = S["dve_chain"]
                dve.sem_inc(S["xt_free"], 1)
                dve.sem_inc(S["prob_free"], 1)
                with dve.Fori(0, B) as b:
                    dve.wait_ge(S["x_loaded"], 16 * LOADS)
                    dve.sem_inc(S["x_loaded"], -16 * LOADS)
                    token_norm_vector(nc, dve, xt, xn, stats, mv, rstd, 1e-5, chain, S["var_ready"], S["std_ready"])
                    dve.sem_inc(S["normed"], 1)
                    dve.sem_inc(S["xt_free"], 1)
                    dve.wait_ge(S["logits_ready"], 1)
                    dve.sem_inc(S["logits_ready"], -1)
                    nc.vector.tensor_reduce(small[:, 0:1], prob[:], AX.X, ALU.max).then_inc(chain, 1)
                    dve.wait_ge(chain, 1)
                    dve.sem_inc(chain, -1)
                    nc.vector.tensor_scalar(small[:, 1:2], small[:, 0:1], -1.0, None, ALU.mult).then_inc(chain, 1)
                    dve.wait_ge(chain, 1)
                    dve.sem_inc(chain, -1)
                    dve.sem_inc(S["exp_in"], 1)
                    dve.wait_ge(S["exp_out"], 1)
                    dve.sem_inc(S["exp_out"], -1)
                    nc.vector.reciprocal(small[:, 3:4], small[:, 2:3]).then_inc(chain, 1)
                    dve.wait_ge(chain, 1)
                    dve.sem_inc(chain, -1)
                    nc.vector.tensor_scalar(prob[:], prob[:], small[:, 3:4], None, ALU.mult).then_inc(chain, 1)
                    dve.wait_ge(chain, 1)
                    dve.sem_inc(chain, -1)
                    nc.vector.max(best[:], prob[:]).then_inc(chain, 1)
                    dve.wait_ge(chain, 1)
                    dve.sem_inc(chain, -1)
                    dve.wait_ge(S["prob_free"], 1)
                    dve.sem_inc(S["prob_free"], -1)
                    nc.vector.match_replace(rest[:], best[:], prob[:], -1.0).then_inc(chain, 1)
                    dve.wait_ge(chain, 1)
                    dve.sem_inc(chain, -1)
                    nc.vector.scalar_tensor_tensor(out=rest[:], in0=rest[:], scalar=0.0, in1=prob[:],
                                                             op0=ALU.is_lt, op1=ALU.mult).then_inc(chain, 1)
                    dve.wait_ge(chain, 1)
                    dve.sem_inc(chain, -1)
                    dve.sem_inc(S["chosen_ready"], 1)
                    dve.sem_inc(S["chosen_store"], 1)
                    dve.wait_ge(S["pooled_done"], 1)
                    dve.sem_inc(S["pooled_done"], -1)

        EG = 4
        with ExitStack() as stack:
            s = Scope(nc, "l3m", stack)
            w1 = [s.sb(f"w1_{n}", [P, EG, HID]) for n in range(2)]
            w2 = [s.sb(f"w2_{n}", [P, EG, KH, C]) for n in range(2)]
            b1, b2, b1T = s.sb("b1", [EX, HID]), s.sb("b2", [EX, C]), s.sb("b1T", [P, KH, EX])
            pre = [s.sb(f"pre{n}", [P, EG, KH, B]) for n in range(2)]
            hid = [s.sb(f"hid{n}", [P, EG, KH, B]) for n in range(2)]
            oT = s.sb("oT", [P, EX, B])
            ps_b = s.ps("ps_b")
            ps_h, ps_o = [s.ps(f"ps_h{n}") for n in range(2)], [s.ps(f"ps_o{n}") for n in range(2)]
            names = ("consts bias_ready bias_done h_ready pre_ready hid_ready o_ready o_done all_done rows_ready dve_chain act_chain").split()
            S = {n: s.sem(n) for n in names}
            loaded, weights_free = [s.sem(f"loaded{n}") for n in range(2)], [s.sem(f"weights_free{n}") for n in range(2)]
            block = s.block()

            @block.sync
            def _(sp):
                sp.dma_start(b1[:], w["weight1"][:, C, :]).then_inc(S["consts"], 16)
                sp.dma_start(b2[:], w["weight2"][:, HID, :]).then_inc(S["consts"], 16)
                with sp.Fori(0, EX // EG // 2) as pair:
                    for k in range(2):
                        e0 = pair * (2 * EG) + k * EG
                        sp.wait_ge(weights_free[k], 1)
                        sp.sem_inc(weights_free[k], -1)
                        sp.dma_start(w1[k][:], w["weight1"][bass.ds(e0, EG), 0:C, :].rearrange("e c h -> c e h")).then_inc(loaded[k], 16)
                        for e in range(EG):
                            src = w["weight2"][bass.ds(e0 + e, 1), 0:HID, :].rearrange("e (k h) o -> h (e k) o", k=KH)
                            sp.dma_start(w2[k][:, e], src).then_inc(loaded[k], 16)

            @block.tensor
            def _(pe):
                pe.sem_inc(weights_free[0], 1)
                pe.sem_inc(weights_free[1], 1)
                pe.wait_ge(S["consts"], 32)
                for k in range(KH):
                    ins = nc.tensor.transpose(ps_b[:, k * EX:(k + 1) * EX], b1[:, k * P:(k + 1) * P], ident[0:EX, 0:EX])
                ins.then_inc(S["bias_ready"], 1)
                with pe.Fori(0, EX // EG // 2) as pair:
                    for k in range(2):
                        pe.wait_ge(loaded[k], 16 * (1 + EG))
                        pe.sem_inc(loaded[k], -16 * (1 + EG))
                        for e in range(EG):
                            rhs = pooled[:, :, bass.ds(pair * (2 * EG) + k * EG + e, 1)].rearrange("p b e -> p (b e)")
                            for j in range(KH):
                                at = (e * KH + j) * B
                                ins = nc.tensor.matmul(ps_h[k][:, at:at + B], w1[k][:, e, j * P:(j + 1) * P], rhs, start=True, stop=True)
                        ins.then_inc(S["h_ready"], 1)
                        pe.wait_ge(S["hid_ready"], 1)
                        pe.sem_inc(S["hid_ready"], -1)
                        for e in range(EG):
                            for j in range(KH):
                                ins = nc.tensor.matmul(ps_o[k][:, e * B:(e + 1) * B], w2[k][:, e, j, :], hid[k][:, e, j, :],
                                                       start=(j == 0), stop=(j == KH - 1))
                        ins.then_inc(S["o_ready"], 1)
                        pe.wait_ge(S["o_done"], 1)
                        pe.sem_inc(S["o_done"], -1)
                        pe.sem_inc(weights_free[k], 1)
                for b in range(B):
                    ins = nc.tensor.transpose(ps_b[0:EX, b * P:(b + 1) * P], oT[:, :, b], ident[:])
                ins.then_inc(S["all_done"], 1)

            @block.scalar
            def _(act):
                with act.Fori(0, EX // EG // 2) as pair:
                    for k in range(2):
                        act.wait_ge(S["pre_ready"], 1)
                        act.sem_inc(S["pre_ready"], -1)
                        nc.scalar.activation(hid[k][:], pre[k][:], ACT.Gelu).then_inc(S["hid_ready"], 1)
                        act.wait_ge(S["o_ready"], 1)
                        act.sem_inc(S["o_ready"], -1)
                        dst = oT[:, bass.ds(pair * (2 * EG) + k * EG, EG), :].rearrange("p e b -> p (e b)")
                        nc.scalar.copy(dst, ps_o[k][:, 0:EG * B]).then_inc(S["o_done"], 1)

            @block.vector
            def _(dve):
                chain = S["dve_chain"]
                dve.wait_ge(S["consts"], 32)
                dve.wait_ge(S["bias_ready"], 1)
                dve.sem_inc(S["bias_ready"], -1)
                nc.vector.tensor_copy(b1T[:].rearrange("p k e -> p (k e)"), ps_b[:, 0:KH * EX]).then_inc(chain, 1)
                dve.wait_ge(chain, 1)
                dve.sem_inc(chain, -1)
                with dve.Fori(0, EX // EG // 2) as pair:
                    for k in range(2):
                        dve.wait_ge(S["h_ready"], 1)
                        dve.sem_inc(S["h_ready"], -1)
                        for j in range(KH):
                            bias = b1T[:, j, bass.ds(pair * (2 * EG) + k * EG, EG)].unsqueeze(2).to_broadcast([P, EG, B])
                            src = ps_h[k][:, 0:EG * KH * B].rearrange("p (e j b) -> p e j b", e=EG, j=KH)[:, :, j, :]
                            ins = nc.vector.tensor_tensor(pre[k][:, :, j, :], src, bias, ALU.add)
                        ins.then_inc(S["pre_ready"], 1)
                dve.wait_ge(S["all_done"], 1)
                dve.sem_inc(S["all_done"], -1)
                bias = b2[:].unsqueeze(1).to_broadcast([EX, B, C])
                nc.vector.tensor_tensor(rows[:], ps_b[0:EX, 0:B * C].rearrange("p (b o) -> p b o", b=B), bias, ALU.add).then_inc(chain, 1)
                dve.wait_ge(chain, 1)
                dve.sem_inc(chain, -1)

        with ExitStack() as stack:
            s = Scope(nc, "l3s", stack)
            xt, pick = [s.sb(f"xt{n}", [P, T, C]) for n in range(2)], [s.sb(f"pick{n}", [EX, N]) for n in range(2)]
            ps = [s.ps(f"ps{n}") for n in range(4)]
            names = "ps_ready ps_free stored dve_chain".split()
            S = {n: s.sem(n) for n in names}
            loaded, ready, free = ([s.sem(f"{m}{n}") for n in range(2)] for m in ("loaded", "ready", "free"))
            block = s.block()
            pairs = B // 2

            @block.sync
            def _(sp):
                with sp.Fori(0, pairs) as pair:
                    for k in range(2):
                        b = pair * 2 + k
                        sp.wait_ge(free[k], 1)
                        sp.sem_inc(free[k], -1)
                        sp.dma_start(pick[k][:], chosen[bass.ds(b, 1)].rearrange("a e n -> e (a n)")).then_inc(loaded[k], 16)
                        load_tokens(sp, xt[k], x, b, loaded[k])

            @block.gpsimd
            def _(pool):
                pass

            @block.scalar
            def _(act):
                for k in range(2):
                    act.sem_inc(free[k], 1)
                with act.Fori(0, pairs) as pair:
                    for k in range(2):
                        act.wait_ge(ready[k], 1)
                        act.sem_inc(ready[k], -1)
                        store_tokens(act, out, xt[k], pair * 2 + k, S["stored"])
                        act.wait_ge(S["stored"], 16 * LOADS)
                        act.sem_inc(S["stored"], -16 * LOADS)
                        act.sem_inc(free[k], 1)

            @block.tensor
            def _(pe):
                with pe.Fori(0, pairs) as pair:
                    for k in range(2):
                        pe.wait_ge(loaded[k], 16 * (1 + LOADS))
                        pe.sem_inc(loaded[k], -16 * (1 + LOADS))
                        for n in range(NB):
                            pe.wait_ge(S["ps_free"], 1)
                            pe.sem_inc(S["ps_free"], -1)
                            rhs = rows[:, bass.ds(pair * 2 + k, 1), :].rearrange("p a o -> p (a o)")
                            for t in range(4 * n, 4 * n + 4):
                                ins = nc.tensor.matmul(ps[n % 4][:, t % 4 * P:(t % 4 + 1) * P], pick[k][:, t * P:(t + 1) * P], rhs,
                                                       start=True, stop=True)
                            ins.then_inc(S["ps_ready"], 1)

            @block.vector
            def _(dve):
                dve.sem_inc(S["ps_free"], 4)
                with dve.Fori(0, pairs) as pair:
                    for k in range(2):
                        for n in range(NB):
                            dve.wait_ge(S["ps_ready"], 1)
                            dve.sem_inc(S["ps_ready"], -1)
                            tokens = xt[k][:, 4 * n:4 * n + 4, :].rearrange("p t c -> p (t c)")
                            nc.vector.tensor_tensor(tokens, tokens, ps[n % 4][:], ALU.add).then_inc(S["dve_chain"], 1)
                            dve.wait_ge(S["dve_chain"], 1)
                            dve.sem_inc(S["dve_chain"], -1)
                            dve.sem_inc(S["ps_free"], 1)
                        dve.sem_inc(ready[k], 1)


def layer3_experts_inputs(i):
    return {"gate_w": i["L3_ffn_gate_w"].T, "gate_b": i["L3_ffn_gate_b"].reshape(EX, 1),
            "weight1": i["L3_ffn_weight1"], "weight2": i["L3_ffn_weight2"]}


def shape_tables():
    f = np.float32
    k = np.arange(P)
    return {
        "ident": np.eye(P, dtype=f), "ones": np.ones((P, P), f),
        "group": (k[:, None] // 4 == k[None] // 4).astype(f) / 4,
        "center": np.eye(P, dtype=f) - f(1) / P,
        "upto2": np.stack([k[:, None] <= k[None], k[:, None] >= k[None]], 1).astype(f),
        "behind2": np.stack([k[:, None] > k[None], k[:, None] < k[None]], 1).astype(f),
    }


INPUTS = (("l0", layer0_inputs), ("l1", layer1_inputs), ("l2a", layer2_mamba_inputs), ("l2f", layer2_experts_inputs),
          ("l3f", layer3_experts_inputs), ("c", lambda i: shape_tables()))


def build(nc, aps, x, out):
    def scratch(name, shape):
        return nc.dram_tensor(name, shape, F32, kind="Internal").ap()

    tables = aps["c"]
    records, table = scratch("records", (B, P, T * PK)), scratch("table", (B * G * POS, C))
    t = [scratch(f"tokens{n}", (B, N, C)) for n in range(1, 6)]
    layer0_prepare(nc, x, aps["l0"] | tables, records, table)
    gathered = [nc.alloc_semaphore(f"gathered{k}") for k in range(2)]
    layer0_attend(nc, x, t[0], aps["l0"] | tables, records, table, gathered)
    layer1(nc, t[0], t[1], aps["l1"] | tables)
    layer2_mamba(nc, t[1], t[2], aps["l2a"] | tables)
    layer2_experts(nc, t[2], t[3], aps["l2f"] | tables)
    layer3_attention(nc, t[3], t[4], tables)
    layer3_experts(nc, t[4], out, scratch("chosen", (B, EX, N)), aps["l3f"] | tables)


def kernel(**inputs):
    import numpy as _np
    import concourse.bacc as _bacc
    from concourse import mybir as _mybir
    from concourse.bass_utils import run_bass_kernel_spmd as _run

    nc = _bacc.Bacc("TRN2", target_bir_lowering=False, num_devices=1)
    inputs = {k: _np.asarray(v) for k, v in inputs.items()}
    arrays, aps = {}, {}

    def give(name, a):
        a = _np.ascontiguousarray(a)
        arrays[f"in_{name}_dram"] = a
        return nc.dram_tensor(f"in_{name}_dram", a.shape, _mybir.dt.from_np(a.dtype), kind="ExternalInput").ap()

    for group, lay_out in INPUTS:
        aps[group] = {name: give(f"{group}_{name}", a) for name, a in lay_out(inputs).items()}
    x = give("x", inputs["x"].reshape(B, N, C))
    out = nc.dram_tensor("out_0_dram", (B, N, C), _mybir.dt.float32, kind="ExternalOutput").ap()
    build(nc, aps, x, out)
    r = _run(nc, [arrays], core_ids=[0])
    return r.results[0]["out_0_dram"].reshape(B, H, W, C)
```

```python
from contextlib import ExitStack

import concourse.bass as bass
import numpy as np
from concourse import mybir

F32 = mybir.dt.float32
I32 = mybir.dt.int32
U32 = mybir.dt.uint32
ACT = mybir.ActivationFunctionType
ALU = mybir.AluOpType
AX = mybir.AxisListType

B, H, W, C = 4, 64, 64, 128
N = H * W
P = 128
T = N // P
BANK = 512
NB = N // BANK
ROWS = BANK // W

G, K2 = 4, 9
HC = C // G
GK = G * K2
NOFF = 2 * GK + K2
SCALE = HC ** -0.5
YT, XT = H + 2, W + 3
POS = YT * XT
PK_W, PK_I = C, C + 4 * GK
PK = C + 5 * GK



LOADS = 4


def load_tokens(engine, dst, src, b, loaded):
    h = T // LOADS
    for n in range(LOADS):
        tokens = src[bass.ds(b, 1), n * h * P:(n + 1) * h * P, :].rearrange("a (t p) c -> p (a t) c", p=P)
        engine.dma_start(dst[:, n * h:(n + 1) * h, :], tokens).then_inc(loaded, 16)


class Scope:

    def __init__(self, nc, stage, stack):
        self.nc, self.stage, self.stack, self.sems = nc, stage, stack, []

    def sb(self, name, shape, dt=F32):
        return self.stack.enter_context(self.nc.sbuf_tensor(f"{self.stage}_{name}", shape, dt))

    def ps(self, name, shape=(P, BANK)):
        return self.stack.enter_context(self.nc.psum_tensor(f"{self.stage}_{name}", list(shape), F32))

    def sem(self, name):
        handle = self.stack.enter_context(self.nc.semaphore(f"{self.stage}_{name}"))
        self.sems.append(handle)
        return handle

    def block(self):
        self.stack.callback(self.clear)
        return self.stack.enter_context(self.nc.Block())

    def clear(self):
        numbers = sorted(x.num for x in self.sems)
        first = numbers[0]
        for number, following in zip(numbers, numbers[1:] + [None]):
            if following != number + 1:
                self.nc.sync.sem_clear(range(first, number + 1))
                first = following
        self.nc.all_engine_barrier()


def group_norm_vector(nc, dve, xT, stats, gn, chain, moments, group_mean, group_var, var_ready, std_ready, mean_ps, var_ps):
    for n in range(NB):
        ins = nc.vector.bn_stats(stats[:, n, :], xT[:, n * BANK:(n + 1) * BANK])
    ins.then_inc(chain, 1)
    dve.wait_ge(chain, 1)
    dve.sem_inc(chain, -1)
    nc.vector.bn_aggr(gn[:, 0:2], stats[:]).then_inc(chain, 1)
    dve.wait_ge(chain, 1)
    dve.sem_inc(chain, -1)
    dve.sem_inc(moments, 1)
    dve.wait_ge(group_mean, 1)
    dve.sem_inc(group_mean, -1)
    nc.vector.tensor_copy(gn[:, 2:3], mean_ps).then_inc(chain, 1)
    dve.wait_ge(chain, 1)
    dve.sem_inc(chain, -1)
    nc.vector.tensor_tensor(gn[:, 3:4], gn[:, 0:1], gn[:, 2:3], ALU.subtract).then_inc(chain, 1)
    dve.wait_ge(chain, 1)
    dve.sem_inc(chain, -1)
    nc.vector.tensor_tensor(gn[:, 4:5], gn[:, 3:4], gn[:, 3:4], ALU.mult).then_inc(chain, 1)
    dve.wait_ge(chain, 1)
    dve.sem_inc(chain, -1)
    nc.vector.tensor_tensor(gn[:, 4:5], gn[:, 4:5], gn[:, 1:2], ALU.add).then_inc(chain, 1)
    dve.wait_ge(chain, 1)
    dve.sem_inc(chain, -1)
    dve.sem_inc(moments, 1)
    dve.wait_ge(group_var, 1)
    dve.sem_inc(group_var, -1)
    nc.vector.tensor_scalar(gn[:, 5:6], var_ps, 1e-5, None, ALU.add).then_inc(chain, 1)
    dve.wait_ge(chain, 1)
    dve.sem_inc(chain, -1)
    nc.vector.reciprocal(gn[:, 5:6], gn[:, 5:6]).then_inc(chain, 1)
    dve.wait_ge(chain, 1)
    dve.sem_inc(chain, -1)
    dve.sem_inc(var_ready, 1)
    dve.wait_ge(std_ready, 1)
    dve.sem_inc(std_ready, -1)
    nc.vector.tensor_scalar(xT[:], xT[:], gn[:, 2:3], gn[:, 6:7], ALU.subtract, ALU.mult).then_inc(chain, 1)
    dve.wait_ge(chain, 1)
    dve.sem_inc(chain, -1)


def group_norm_tensor(nc, pe, group, gn, moments, group_mean, group_var, mean_ps, var_ps):
    pe.wait_ge(moments, 1)
    pe.sem_inc(moments, -1)
    nc.tensor.matmul(mean_ps, group[:], gn[:, 0:1], start=True, stop=True).then_inc(group_mean, 1)
    pe.wait_ge(moments, 1)
    pe.sem_inc(moments, -1)
    nc.tensor.matmul(var_ps, group[:], gn[:, 4:5], start=True, stop=True).then_inc(group_var, 1)


def layer0_prepare(nc, x, w, records, table, in_table, row0, b, mark, more):
    START = mark == "a"
    first_places, q_places, k_places0, k_places1, *rest = more.share(9, 5, 3, 3, *[20 / T] * T, 5, 5)
    tile_places, mask_places, end_places = rest[:T], rest[T], rest[T + 1]
    with ExitStack() as stack:
        s = Scope(nc, "l0" + mark, stack)
        ident, group = s.sb("ident", [P, P]), s.sb("group", [P, P])
        w_qkv, b_qkv = s.sb("w_qkv", [P, 3 * C]), s.sb("b_qkv", [P, 3])
        w_dw, b_dw = s.sb("w_dw", [P, 3, K2]), s.sb("b_dw", [P, 3])
        w_off = s.sb("w_off", [P, NOFF])
        QROWS = 3 * HC + 1
        w_shift = s.sb("w_shift", [QROWS, 3, NOFF])
        base = s.sb("base", [P, T, 2 * GK])
        zeros = s.sb("zeros", [P, 2 * 2 * C])
        xt, xT = s.sb("xt", [P, T, C]), s.sb("xT", [P, N])
        stats, gn = s.sb("stats", [P, NB, 6]), s.sb("gn", [P, 8])
        diag = s.sb("diag", [P, K2, P])
        rec = s.sb("rec", [P, T, PK])
        flat = rec[:].rearrange("p t f -> p (t f)")
        AREA = (H + 2) * (W + 2)
        padded = [flat[:, n * AREA:(n + 1) * AREA].rearrange("p (y x) -> p y x", x=W + 2) for n in range(2)]
        q_shift = s.sb("q_shift", [QROWS, H + 2, W])
        q_img, k_img, v_img = s.sb("q_img", [P, N]), s.sb("k_img", [P, N]), s.sb("v_img", [P, N])
        off = xT[:, 0:T * NOFF].rearrange("p (t n) -> p t n", t=T)
        w_pconv = xT[0:HC, 0:5 * K2 * HC].rearrange("p (i k o) -> p i k o", i=5, k=K2)
        kv = xt[:].rearrange("p t c -> p (t c)").rearrange("p (t c) -> p t c", t=T // 2)
        ps = [s.ps(f"ps{n}") for n in range(2)]
        ps_off, ps_tr = [s.ps(f"ps_off{n}") for n in range(2)], [s.ps(f"ps_tr{n}") for n in range(2)]
        ps_small = s.ps("ps_small")
        mean_ps, var_ps = ps_small[:, 0:1], ps_small[:, 1:2]

        consts, tap_ready, taps_used = s.sem("consts"), s.sem("tap_ready"), s.sem("taps_used")
        x_loaded, kv_free = s.sem("x_loaded"), s.sem("kv_free")
        ps_ready, ps_free = s.sem("ps_ready"), s.sem("ps_free")
        off_ready, off_free = s.sem("off_ready"), s.sem("off_free")
        tr_ready, tr_free = s.sem("tr_ready"), s.sem("tr_free")
        xT_ready, normed = s.sem("xT_ready"), s.sem("normed")
        moments, group_mean, group_var = s.sem("moments"), s.sem("group_mean"), s.sem("group_var")
        var_ready, std_ready = s.sem("var_ready"), s.sem("std_ready")
        dve_chain, act_chain = s.sem("dve_chain"), s.sem("act_chain")
        padded_ready = [s.sem("padded_ready0"), s.sem("padded_ready1")]
        v_padded_ready, padded_free = s.sem("v_padded_ready"), [s.sem("padded_free0"), s.sem("padded_free1")]
        v_ready, diag_ready = s.sem("v_ready"), s.sem("diag_ready")
        images_ready = s.sem("images_ready")
        images_free, v_free = s.sem("images_free"), s.sem("v_free")
        kv_ready, kv_stored = s.sem("kv_ready"), s.sem("kv_stored")
        evacuated, mask_in, mask_out = s.sem("evacuated"), s.sem("mask_in"), s.sem("mask_out")
        rec_ready, borders, rec_stored = s.sem("rec_ready"), s.sem("borders"), s.sem("rec_stored")
        zero_ready, shift_zero = s.sem("zero_ready"), s.sem("shift_zero")
        q_ready, shift_ready, shift_free = s.sem("q_ready"), s.sem("shift_ready"), s.sem("shift_free")
        block = s.block()

        loads = [(ident, w["ident"]), (group, w["group"]), (w_qkv, w["w_qkv"]), (b_qkv, w["b_qkv"]), (w_dw, w["w_dw"]),
                 (b_dw, w["b_dw"]), (w_off, w["w_off"]), (base, w["base"])]
        if START:
            loads.append((row0, w["row0"]))
        NC = 16 * (len(loads) + 2)

        @block.sync
        def _(sp):
            for dst, src in loads:
                sp.dma_start(dst[:], src).then_inc(consts, 16)
            sp.dma_start(w_pconv, w["w_pconv"]).then_inc(consts, 16)
            load_tokens(sp, xt, x, b, x_loaded)
            for place in first_places:
                more.sync(sp, *place)
            sp.wait_ge(shift_zero, 1)
            sp.dma_start(w_shift[3 * HC:QROWS, 0, :], w["b_off"]).then_inc(consts, 16)
            sp.wait_ge(zero_ready, 1)
            cells_b = table[bass.ds(in_table * (G * POS), G * POS), :].rearrange("(g y x) c -> g y x c", g=G, y=YT)
            for g in range(G):
                sp.dma_start(cells_b[g, :, 0, :], zeros[0:YT, 0:C]).then_inc(borders, 16)
                sp.dma_start(cells_b[g, :, XT - 2:XT, :].rearrange("y x c -> y (x c)"), zeros[0:YT, 0:2 * C]).then_inc(borders, 16)
                sp.dma_start(cells_b[g, 0, 1:XT - 2, 0:64], zeros[0:W, 0:64]).then_inc(borders, 16)
                sp.dma_start(cells_b[g, YT - 2, 1:XT - 2, 64:128], zeros[0:W, 0:64]).then_inc(borders, 16)
                sp.dma_start(cells_b[g, YT - 1, 1:XT - 2, :], zeros[0:W, 0:C]).then_inc(borders, 16)
            if START:
                sp.dma_start(records[B * T], zeros[:, 0:PK]).then_inc(borders, 16)
            half_rows = T // 2 * 2
            for places in (q_places, k_places0, k_places1):
                for place in places:
                    more.sync(sp, *place)
            for half in range(2):
                for places in tile_places[half * T // 2:(half + 1) * T // 2]:
                    for place in places:
                        more.sync(sp, *place)
                sp.wait_ge(kv_ready, 1)
                sp.sem_inc(kv_ready, -1)
                for g in range(G):
                    for r in range(2):
                        src = kv[r * W:(r + 1) * W, :, g * 64:(g + 1) * 64]
                        for slot in range(2):
                            y0 = half * half_rows + r + 1 - slot
                            dst = cells_b[g, y0:y0 + half_rows - 1:2, 1:1 + W, slot * 64:(slot + 1) * 64]
                            sp.dma_start(dst.rearrange("y x c -> x y c"), src).then_inc(kv_stored, 16)
                sp.wait_ge(kv_stored, 16 * 16)
                sp.sem_inc(kv_stored, -16 * 16)
                if half == 0:
                    sp.sem_inc(kv_free, 1)
            for place in mask_places + end_places:
                more.sync(sp, *place)
            sp.wait_ge(rec_ready, 1)
            sp.sem_inc(rec_ready, -1)
            h = T // LOADS
            for n in range(LOADS):
                tiles = records[bass.ds(b * T + n * h, h)].rearrange("t p f -> p t f")
                sp.dma_start(tiles, rec[:, n * h:(n + 1) * h, :]).then_inc(rec_stored, 16)
            sp.wait_ge(rec_stored, 16 * LOADS)
            sp.sem_inc(rec_stored, -16 * LOADS)
            sp.wait_ge(borders, 16 * (5 * G + START))

        q_rows = q_shift[:].rearrange("p y x -> p (y x)")

        @block.tensor
        def _(pe):
            for place in first_places:
                more.tensor(pe, *place)
            pe.wait_ge(consts, NC)
            for tap in range(K2):
                dst = ps_off[tap // 5][0:HC, tap % 5 * NOFF:(tap % 5 + 1) * NOFF]
                for i in range(G):
                    yx = dst[:, 0:2 * GK].rearrange("p (d n) -> p d n", d=2)[:, :, i * K2:(i + 1) * K2]
                    wyx = w_off[0:HC, 0:2 * GK].rearrange("p (d n) -> p d n", d=2)[:, :, i * K2:(i + 1) * K2]
                    nc.tensor.matmul(yx, w_pconv[:, i, tap, :], wyx, start=True, stop=True)
                ins = nc.tensor.matmul(dst[:, 2 * GK:], w_pconv[:, G, tap, :], w_off[0:HC, 2 * GK:], start=True, stop=True)
            ins.then_inc(tap_ready, 1)
            pe.wait_ge(taps_used, 1)
            pe.wait_ge(diag_ready, 1)
            pe.wait_ge(x_loaded, 16 * LOADS)
            pe.sem_inc(x_loaded, -16 * LOADS)
            for n in range(NB):
                pe.wait_ge(ps_free, 1)
                pe.sem_inc(ps_free, -1)
                for t in range(4):
                    ins = nc.tensor.transpose(ps[n % 2][:, t * P:(t + 1) * P], xt[:, 4 * n + t, :], ident[:])
                ins.then_inc(ps_ready, 1)
            group_norm_tensor(nc, pe, group, gn, moments, group_mean, group_var, mean_ps, var_ps)
            pe.wait_ge(normed, 1)
            pe.sem_inc(normed, -1)
            for j in range(3):
                for n in range(NB):
                    pe.wait_ge(ps_free, 1)
                    pe.sem_inc(ps_free, -1)
                    nc.tensor.matmul(ps[n % 2][:], w_qkv[:, j * C:(j + 1) * C], xT[:, n * BANK:(n + 1) * BANK],
                                     start=True, stop=True).then_inc(ps_ready, 1)
                for place in [(), q_places, k_places0][j]:
                    more.tensor(pe, *place)
            pe.wait_ge(v_padded_ready, 1)
            pe.sem_inc(v_padded_ready, -1)
            for n in range(NB):
                pe.wait_ge(ps_free, 1)
                pe.sem_inc(ps_free, -1)
                for tap in range(K2):
                    y, xx = n * ROWS + tap // 3, tap % 3
                    ins = nc.tensor.matmul(ps[n % 2][:], diag[:, tap, :], padded[0][:, y:y + ROWS, xx:xx + W],
                                           start=(tap == 0), stop=(tap == K2 - 1))
                ins.then_inc(ps_ready, 1)
                if n == NB // 2:
                    for place in k_places1:
                        more.tensor(pe, *place)
            pe.wait_ge(images_ready, 2)
            pe.sem_inc(images_ready, -2)
            pe.wait_ge(v_ready, 1)
            pe.sem_inc(v_ready, -1)
            pe.wait_ge(shift_ready, 1)
            pe.sem_inc(shift_ready, -1)
            for t in range(T):
                    k = t % 2
                    pe.wait_ge(off_free, 1)
                    pe.sem_inc(off_free, -1)
                    nc.tensor.matmul(ps_off[k][:, 0:NOFF], q_img[:, t * P:(t + 1) * P], w_off[:], start=True, stop=False)
                    for dy in range(3):
                        ins = nc.tensor.matmul(ps_off[k][:, 0:NOFF], q_rows[:, t * P + dy * W:t * P + dy * W + P], w_shift[:, dy, :],
                                               start=False, stop=(dy == 2))
                    ins.then_inc(off_ready, 1)
                    pe.wait_ge(tr_free, 1)
                    pe.sem_inc(tr_free, -1)
                    nc.tensor.transpose(ps_tr[k][:, 0:C], q_img[:, t * P:(t + 1) * P], ident[:])
                    nc.tensor.transpose(ps_tr[k][:, C:2 * C], k_img[:, t * P:(t + 1) * P], ident[:])
                    nc.tensor.transpose(ps_tr[k][:, 2 * C:3 * C], v_img[:, t * P:(t + 1) * P],
                                        ident[:]).then_inc(tr_ready, 1)
                    for place in tile_places[t]:
                        more.tensor(pe, *place)
            for place in mask_places + end_places:
                more.tensor(pe, *place)

        @block.scalar
        def _(act):
            act.sem_inc(ps_free, 2)
            act.sem_inc(off_free, 2)
            act.sem_inc(tr_free, 2)
            for place in first_places:
                more.scalar(act, *place)
            act.wait_ge(consts, NC)
            for n in range(NB):
                act.wait_ge(ps_ready, 1)
                act.sem_inc(ps_ready, -1)
                nc.scalar.copy(xT[:, n * BANK:(n + 1) * BANK], ps[n % 2][:]).then_inc(act_chain, 1)
                act.wait_ge(act_chain, 1)
                act.sem_inc(act_chain, -1)
                act.sem_inc(ps_free, 1)
            act.sem_inc(xT_ready, 1)
            act.wait_ge(var_ready, 1)
            act.sem_inc(var_ready, -1)
            nc.scalar.activation(gn[:, 6:7], gn[:, 5:6], ACT.Sqrt).then_inc(std_ready, 1)
            for j in range(3):
                act.wait_ge(padded_free[j % 2], 1)
                act.sem_inc(padded_free[j % 2], -1)
                for n in range(NB):
                    act.wait_ge(ps_ready, 1)
                    act.sem_inc(ps_ready, -1)
                    dst = padded[j % 2][:, 1 + n * ROWS:1 + (n + 1) * ROWS, 1:1 + W]
                    src = ps[n % 2][:].rearrange("p (y x) -> p y x", x=W)
                    nc.scalar.activation(dst, src, ACT.Identity, bias=b_qkv[:, j:j + 1]).then_inc(act_chain, 1)
                    act.wait_ge(act_chain, 1)
                    act.sem_inc(act_chain, -1)
                    act.sem_inc(ps_free, 1)
                act.sem_inc([padded_ready[0], padded_ready[1], v_padded_ready][j], 1)
                for place in [(), q_places, k_places0][j]:
                    more.scalar(act, *place)
            for n in range(NB):
                act.wait_ge(ps_ready, 1)
                act.sem_inc(ps_ready, -1)
                nc.scalar.activation(v_img[:, n * BANK:(n + 1) * BANK], ps[n % 2][:], ACT.Identity, bias=b_dw[:, 2:3]).then_inc(act_chain, 1)
                act.wait_ge(act_chain, 1)
                act.sem_inc(act_chain, -1)
                act.sem_inc(ps_free, 1)
                if n == NB // 2:
                    for place in k_places1:
                        more.scalar(act, *place)
            act.sem_inc(v_ready, 1)
            act.sem_inc(padded_free[0], 1)
            act.wait_ge(q_ready, 1)
            act.sem_inc(q_ready, -1)
            q3 = q_img[0:HC, :].rearrange("p (y x) -> p y x", x=W)
            nc.scalar.copy(q_shift[0:HC, 1:1 + H, 1:W], q3[:, :, 0:W - 1])
            nc.scalar.copy(q_shift[HC:2 * HC, 1:1 + H, :], q3)
            nc.scalar.copy(q_shift[2 * HC:3 * HC, 1:1 + H, 0:W - 1], q3[:, :, 1:W]).then_inc(act_chain, 1)
            act.wait_ge(act_chain, 1)
            act.sem_inc(act_chain, -1)
            act.sem_inc(shift_ready, 1)
            for half in range(2):
                act.wait_ge(kv_free, 1)
                act.sem_inc(kv_free, -1)
                for t in range(half * T // 2, (half + 1) * T // 2):
                    k = t % 2
                    act.wait_ge(off_ready, 1)
                    act.sem_inc(off_ready, -1)
                    nc.scalar.copy(off[:, t, :], ps_off[k][:, 0:NOFF]).then_inc(act_chain, 1)
                    act.wait_ge(act_chain, 1)
                    act.sem_inc(act_chain, -1)
                    act.sem_inc(off_free, 1)
                    act.wait_ge(tr_ready, 1)
                    act.sem_inc(tr_ready, -1)
                    nc.scalar.activation(rec[:, t, 0:C], ps_tr[k][:, 0:C], ACT.Copy, scale=SCALE)
                    dst = kv[:, t % (T // 2), :].rearrange("p (g s c) -> p g s c", g=G, s=2)
                    src = ps_tr[k][:, C:3 * C].rearrange("p (s g c) -> p g s c", s=2, g=G)
                    nc.scalar.copy(dst, src).then_inc(act_chain, 1)
                    act.wait_ge(act_chain, 1)
                    act.sem_inc(act_chain, -1)
                    act.sem_inc(tr_free, 1)
                    for place in tile_places[t]:
                        more.scalar(act, *place)
                act.sem_inc(kv_ready, 1)
            act.sem_inc(evacuated, 1)
            for place in mask_places:
                more.scalar(act, *place)
            act.wait_ge(mask_in, 1)
            act.sem_inc(mask_in, -1)
            nc.scalar.activation(off[:, :, 2 * GK:], off[:, :, 2 * GK:], ACT.Exp, scale=-1.0).then_inc(mask_out, 1)
            for place in end_places:
                more.scalar(act, *place)

        def convolve(eng, api, j, img, out_img, chain, places):
            for tap in range(K2):
                src = img[:, tap // 3:tap // 3 + H, tap % 3:tap % 3 + W]
                if tap == 0:
                    ins = api.tensor_scalar(out_img, src, w_dw[:, j, 0:1], b_dw[:, j:j + 1], ALU.mult, ALU.add)
                else:
                    ins = api.scalar_tensor_tensor(out=out_img, in0=src, scalar=w_dw[:, j, tap:tap + 1], in1=out_img,
                                                   op0=ALU.mult, op1=ALU.add)
                ins.then_inc(chain, 1)
                eng.wait_ge(chain, 1)
                eng.sem_inc(chain, -1)
                for place in places[tap * len(places) // K2:(tap + 1) * len(places) // K2]:
                    more.vector(eng, *place)

        @block.vector
        def _(dve):
            for place in first_places:
                more.vector(dve, *place)
            nc.vector.memset(zeros[:], 0.0).then_inc(zero_ready, 1)
            for area in (*padded, q_shift[0:3 * HC], w_shift[:]):
                ins = nc.vector.memset(area, 0.0)
            nc.vector.memset(q_shift[3 * HC:QROWS], 1.0)
            ins.then_inc(dve_chain, 1)
            dve.wait_ge(dve_chain, 1)
            dve.sem_inc(dve_chain, -1)
            dve.sem_inc(shift_zero, 1)
            dve.sem_inc(padded_free[0], 1)
            dve.sem_inc(padded_free[1], 1)
            dve.wait_ge(consts, NC)
            dve.wait_ge(tap_ready, 1)
            nc.vector.memset(w_off[0:HC, :], 0.0)
            for tap in range(K2):
                dx = tap % 3
                ins = nc.vector.tensor_copy(w_shift[dx * HC:(dx + 1) * HC, tap // 3, :],
                                            ps_off[tap // 5][0:HC, tap % 5 * NOFF:(tap % 5 + 1) * NOFF])
            ins.then_inc(dve_chain, 1)
            dve.wait_ge(dve_chain, 1)
            dve.sem_inc(dve_chain, -1)
            dve.sem_inc(taps_used, 1)
            dve.wait_ge(xT_ready, 1)
            dve.sem_inc(xT_ready, -1)
            dve.sem_inc(kv_free, 1)
            group_norm_vector(nc, dve, xT, stats, gn, dve_chain, moments, group_mean, group_var,
                              var_ready, std_ready, mean_ps, var_ps)
            dve.sem_inc(normed, 1)
            dve.wait_ge(padded_ready[0], 1)
            dve.sem_inc(padded_ready[0], -1)
            convolve(dve, nc.vector, 0, padded[0], q_img[:].rearrange("p (y x) -> p y x", x=W), dve_chain, q_places)
            dve.sem_inc(q_ready, 1)
            dve.sem_inc(images_ready, 1)
            dve.sem_inc(padded_free[0], 1)
            dve.wait_ge(padded_ready[1], 1)
            dve.sem_inc(padded_ready[1], -1)
            convolve(dve, nc.vector, 1, padded[1], k_img[:].rearrange("p (y x) -> p y x", x=W), dve_chain,
                     k_places0 + k_places1)
            dve.sem_inc(images_ready, 1)
            dve.sem_inc(padded_free[1], 1)
            for places in tile_places:
                for place in places:
                    more.vector(dve, *place)
            dve.wait_ge(evacuated, 1)
            dve.sem_inc(evacuated, -1)
            pt, cell, tmp = (q_buf[:, 0:T * 2 * GK].rearrange("p (t n) -> p t n", t=T) for q_buf in (k_img, v_img, q_img))
            cell_i = tmp.bitcast(I32)
            nc.vector.tensor_tensor(pt, off[:, :, 0:2 * GK], base[:], ALU.add).then_inc(dve_chain, 1)
            dve.wait_ge(dve_chain, 1)
            dve.sem_inc(dve_chain, -1)
            nc.vector.tensor_scalar(pt, pt, -1.0, float(H), ALU.max, ALU.min).then_inc(dve_chain, 1)
            dve.wait_ge(dve_chain, 1)
            dve.sem_inc(dve_chain, -1)
            for place in mask_places:
                more.vector(dve, *place)
            nc.vector.tensor_copy(cell_i, pt).then_inc(dve_chain, 1)
            dve.wait_ge(dve_chain, 1)
            dve.sem_inc(dve_chain, -1)
            nc.vector.tensor_copy(cell, cell_i).then_inc(dve_chain, 1)
            dve.wait_ge(dve_chain, 1)
            dve.sem_inc(dve_chain, -1)
            nc.vector.tensor_tensor(tmp, cell, pt, ALU.is_gt).then_inc(dve_chain, 1)
            dve.wait_ge(dve_chain, 1)
            dve.sem_inc(dve_chain, -1)
            nc.vector.tensor_tensor(cell, cell, tmp, ALU.subtract).then_inc(dve_chain, 1)
            dve.wait_ge(dve_chain, 1)
            dve.sem_inc(dve_chain, -1)
            nc.vector.tensor_tensor(pt, pt, cell, ALU.subtract).then_inc(dve_chain, 1)
            dve.wait_ge(dve_chain, 1)
            dve.sem_inc(dve_chain, -1)
            rows = tmp[:, :, 0:GK]
            nc.vector.scalar_tensor_tensor(out=rows, in0=cell[:, :, 0:GK], scalar=float(XT), in1=cell[:, :, GK:],
                                                     op0=ALU.mult, op1=ALU.add).then_inc(dve_chain, 1)
            dve.wait_ge(dve_chain, 1)
            dve.sem_inc(dve_chain, -1)
            row0_b = row0[:].unsqueeze(1).to_broadcast([P, T, GK])
            nc.vector.tensor_tensor(rows, rows, row0_b, ALU.add).then_inc(dve_chain, 1)
            dve.wait_ge(dve_chain, 1)
            dve.sem_inc(dve_chain, -1)
            nc.vector.tensor_copy(rec[:, :, PK_I:PK].bitcast(U32), rows).then_inc(dve_chain, 1)
            dve.wait_ge(dve_chain, 1)
            dve.sem_inc(dve_chain, -1)
            if not START:
                nc.vector.tensor_scalar(row0[:], row0[:], float(G * POS), None, ALU.add).then_inc(dve_chain, 1)
                dve.wait_ge(dve_chain, 1)
                dve.sem_inc(dve_chain, -1)
            dve.sem_inc(mask_in, 1)
            dve.wait_ge(mask_out, 1)
            dve.sem_inc(mask_out, -1)
            mask = off[:, :, 2 * GK:]
            nc.vector.tensor_scalar(mask, mask, 1.0, None, ALU.add).then_inc(dve_chain, 1)
            dve.wait_ge(dve_chain, 1)
            dve.sem_inc(dve_chain, -1)
            nc.vector.reciprocal(mask, mask).then_inc(dve_chain, 1)
            dve.wait_ge(dve_chain, 1)
            dve.sem_inc(dve_chain, -1)
            for place in end_places:
                more.vector(dve, *place)
            nc.vector.tensor_scalar(cell, pt, -1.0, 1.0, ALU.mult, ALU.add).then_inc(dve_chain, 1)
            dve.wait_ge(dve_chain, 1)
            dve.sem_inc(dve_chain, -1)
            for wy in (pt, cell):
                for g in range(G):
                    v = wy[:, :, g * K2:(g + 1) * K2]
                    ins = nc.vector.tensor_tensor(v, v, mask, ALU.mult)
            ins.then_inc(dve_chain, 1)
            dve.wait_ge(dve_chain, 1)
            dve.sem_inc(dve_chain, -1)
            corners = rec[:, :, PK_W:PK_I].rearrange("p t (n c) -> p t n c", c=4)
            for c in range(4):
                wx, wy = (cell, pt)[c // 2], (cell, pt)[c % 2]
                ins = nc.vector.tensor_tensor(corners[:, :, :, c], wx[:, :, GK:], wy[:, :, 0:GK], ALU.mult)
            ins.then_inc(dve_chain, 1)
            dve.wait_ge(dve_chain, 1)
            dve.sem_inc(dve_chain, -1)
            dve.sem_inc(rec_ready, 1)

        @block.gpsimd
        def _(pool):
            for place in first_places:
                for third in range(3):
                    more.pool(pool, *place, third)
            pool.wait_ge(consts, NC)
            for tap in range(K2):
                ins = nc.gpsimd.tensor_scalar(diag[:, tap, :], ident[:], w_dw[:, 2, tap:tap + 1], None, ALU.mult)
            ins.then_inc(diag_ready, 1)
            for places in (q_places, k_places0, k_places1, *tile_places, mask_places, end_places):
                for place in places:
                    for third in range(3):
                        more.pool(pool, *place, third)


class Attend:

    PLACES = 5
    UNIT = GK // 2
    CELL = 4 * 2 * HC

    def __init__(self, nc, stack, x, x1, records, table, w):
        s = Scope(nc, "att", stack)
        self.nc, self.x, self.x1, self.records, self.table, self.w = nc, x, x1, records, table, w
        self.ident, self.w_proj, self.b_proj = s.sb("ident", [P, P]), s.sb("w_proj", [P, C]), s.sb("b_proj", [P, C])
        self.rec = [s.sb(f"rec{k}", [P, PK]) for k in range(2)]
        self.xin, self.xout = s.sb("xin", [P, C]), s.sb("xout", [P, C])
        self.got = [s.sb(f"got{half}", [P, self.UNIT, self.CELL]) for half in range(2)]
        n = self.UNIT
        self.dots, self.coef = s.sb("dots", [P, 4 * n]), s.sb("coef", [P, 4 * n])
        self.logit, self.prob = s.sb("logit", [P, n]), s.sb("prob", [P, n])
        self.top, self.total = s.sb("top", [P, 2]), s.sb("total", [P, 2])
        self.o, self.oT = s.sb("o", [P, C]), s.sb("oT", [P, C])
        self.ps = s.ps("ps")
        self.gathered = [s.sem(f"gathered{half}") for half in range(2)]
        self.consts = s.sem("consts")
        self.rec_loaded = [s.sem(f"rec_loaded{k}") for k in range(2)]
        self.rec_free = [s.sem(f"rec_free{k}") for k in range(2)]
        self.rec_here = [s.sem(f"rec_here{k}") for k in range(2)]
        self.got_free = [s.sem(f"got_free{half}") for half in range(2)]
        self.chain, self.act_chain, self.logit_ready, self.prob_ready = (
            s.sem(n) for n in ("chain", "act_chain", "logit_ready", "prob_ready"))
        self.o_ready, self.o_free, self.turned, self.oT_ready, self.projected = (
            s.sem(n) for n in ("o_ready", "o_free", "turned", "oT_ready", "projected"))
        self.out_ready, self.out_free, self.stored = (s.sem(n) for n in ("out_ready", "out_free", "stored"))
        self.ps_free, self.xin_loaded, self.xin_free = (s.sem(n) for n in ("ps_free", "xin_loaded", "xin_free"))
        self.tile, self.count, self.fresh = 0, 0, False
        self.again = 0

    def tiles(self, tile, count, fresh=False):
        self.tile, self.count, self.fresh = tile, count, fresh
        return self

    def share(self, *weights):
        places = [(n // self.PLACES, n % self.PLACES) for n in range(self.count * self.PLACES)]
        ends = [round(len(places) * sum(weights[:n]) / sum(weights)) for n in range(len(weights) + 1)]
        return [places[a:b] for a, b in zip(ends, ends[1:])]

    def before(self, j):
        return j > 0 or not self.fresh

    def load(self, sp, j):
        sp.wait_ge(self.rec_free[j % 2], 1)
        sp.sem_inc(self.rec_free[j % 2], -1)
        row = self.records[bass.ds(self.tile + j, 1)].rearrange("a p f -> p (a f)")
        sp.dma_start(self.rec[j % 2][:], row).then_inc(self.rec_loaded[j % 2], 16)

    def sync(self, sp, j, place):
        if place == 0:
            self.load(sp, j + 1)
        elif place == 2 and self.before(j):
            self.sync_finish(sp, j - 1)
        elif place == 4:
            sp.wait_ge(self.xin_free, 1)
            sp.sem_inc(self.xin_free, -1)
            tokens = self.x[bass.ds(self.tile + j, 1)].rearrange("a p c -> p (a c)")
            sp.dma_start(self.xin[:], tokens).then_inc(self.xin_loaded, 16)

    def sync_finish(self, sp, j):
        sp.wait_ge(self.out_ready, 1)
        sp.sem_inc(self.out_ready, -1)
        tokens = self.x1[bass.ds(self.tile + j, 1)].rearrange("a p c -> p (a c)")
        sp.dma_start(tokens, self.xout[:]).then_inc(self.stored, 16)
        sp.wait_ge(self.stored, 16)
        sp.sem_inc(self.stored, -16)
        sp.sem_inc(self.out_free, 1)

    def gather(self, pool, j, half, start, end):
        k = j % 2
        if start == 0:
            if half == 0:
                pool.wait_ge(self.rec_loaded[k], 16)
                pool.sem_inc(self.rec_loaded[k], -16)
                pool.sem_inc(self.rec_here[k], 1)
            pool.wait_ge(self.got_free[half], 1)
            pool.sem_inc(self.got_free[half], -1)
        for at in range(start, end):
            row = PK_I + half * self.UNIT + at
            pool.indirect_dma_start(
                self.got[half][:, at, :], None, self.table,
                bass.IndirectOffsetOnAxis(ap=self.rec[k][:, row:row + 1].bitcast(U32), axis=0),
            ).then_inc(self.gathered[half], 16)

    def pool(self, pool, j, place, third):
        if place < 2:
            n = self.UNIT // 6
            self.gather(pool, j, 1, (3 * place + third) * n, (3 * place + third + 1) * n)
        else:
            n = self.UNIT // 9
            self.gather(pool, j + 1, 0, (3 * place - 6 + third) * n, (3 * place - 5 + third) * n)

    def vector(self, dve, j, place):
        nc, k, half = self.nc, j % 2, place // 2
        if place == 4:
            return
        if place == 2 and self.before(j):
            self.vector_finish(dve)
        n = self.UNIT
        cells = self.got[half][:].rearrange("p n (c f) -> p (n c) f", c=4)
        weights = self.rec[k][:, PK_W + half * 4 * n:PK_W + (half + 1) * 4 * n].rearrange("p (n c) -> p n c", c=4)
        by_tap = lambda ap: ap.rearrange("p (g n) -> p g n", g=2)
        per_group = lambda ap: ap.unsqueeze(2).to_broadcast([P, 2, K2])
        if place % 2 == 0:
            if half == 0:
                dve.wait_ge(self.rec_here[k], 1)
                dve.sem_inc(self.rec_here[k], -1)
            gathers = self.tile + (j + 1 + (self.again if half == 0 else 0))
            dve.wait_ge(self.gathered[half], gathers * (16 * n))
            keys = cells[:, :, 0:HC].rearrange("p (g n) f -> p g n f", g=2)
            q = self.rec[k][:, half * C // 2:(half + 1) * C // 2].rearrange("p (g f) -> p g f", g=2)
            nc.vector.tensor_tensor(keys, keys, q.unsqueeze(2).to_broadcast([P, 2, 4 * K2, HC]), ALU.mult).then_inc(self.chain, 1)
            dve.wait_ge(self.chain, 1)
            dve.sem_inc(self.chain, -1)
            nc.vector.tensor_reduce(self.dots[:], cells[:, :, 0:HC], AX.X, ALU.add).then_inc(self.chain, 1)
            dve.wait_ge(self.chain, 1)
            dve.sem_inc(self.chain, -1)
            dots = self.dots[:].rearrange("p (n c) -> p n c", c=4)
            nc.vector.tensor_tensor(dots, dots, weights, ALU.mult).then_inc(self.chain, 1)
            dve.wait_ge(self.chain, 1)
            dve.sem_inc(self.chain, -1)
            nc.vector.tensor_reduce(self.logit[:], dots, AX.X, ALU.add).then_inc(self.chain, 1)
            dve.wait_ge(self.chain, 1)
            dve.sem_inc(self.chain, -1)
            nc.vector.tensor_reduce(self.top[:], by_tap(self.logit[:]), AX.X, ALU.max).then_inc(self.chain, 1)
            dve.wait_ge(self.chain, 1)
            dve.sem_inc(self.chain, -1)
            nc.vector.tensor_tensor(by_tap(self.logit[:]), by_tap(self.logit[:]), per_group(self.top[:]), ALU.subtract).then_inc(self.chain, 1)
            dve.wait_ge(self.chain, 1)
            dve.sem_inc(self.chain, -1)
            dve.sem_inc(self.logit_ready, 1)
        else:
            dve.wait_ge(self.prob_ready, 1)
            dve.sem_inc(self.prob_ready, -1)
            nc.vector.tensor_reduce(self.total[:], by_tap(self.prob[:]), AX.X, ALU.add).then_inc(self.chain, 1)
            dve.wait_ge(self.chain, 1)
            dve.sem_inc(self.chain, -1)
            nc.vector.reciprocal(self.total[:], self.total[:]).then_inc(self.chain, 1)
            dve.wait_ge(self.chain, 1)
            dve.sem_inc(self.chain, -1)
            nc.vector.tensor_tensor(by_tap(self.prob[:]), by_tap(self.prob[:]), per_group(self.total[:]), ALU.mult).then_inc(self.chain, 1)
            dve.wait_ge(self.chain, 1)
            dve.sem_inc(self.chain, -1)
            nc.vector.tensor_tensor(self.coef[:].rearrange("p (n c) -> p n c", c=4), weights,
                                              self.prob[:].unsqueeze(2).to_broadcast([P, n, 4]), ALU.mult).then_inc(self.chain, 1)
            dve.wait_ge(self.chain, 1)
            dve.sem_inc(self.chain, -1)
            values = cells[:, :, HC:]
            nc.vector.tensor_tensor(values, values, self.coef[:].unsqueeze(2).to_broadcast([P, 4 * n, HC]), ALU.mult).then_inc(self.chain, 1)
            dve.wait_ge(self.chain, 1)
            dve.sem_inc(self.chain, -1)
            if half == 0:
                dve.wait_ge(self.o_free, 1)
                dve.sem_inc(self.o_free, -1)
            o = self.o[:, half * C // 2:(half + 1) * C // 2].rearrange("p (g f) -> p g f", g=2)
            nc.vector.tensor_reduce(o, values.rearrange("p (g n) f -> p g f n", g=2), AX.X, ALU.add).then_inc(self.chain, 1)
            dve.wait_ge(self.chain, 1)
            dve.sem_inc(self.chain, -1)
            dve.sem_inc(self.got_free[half], 1)
            if half == 1:
                dve.sem_inc(self.rec_free[k], 1)
                dve.sem_inc(self.o_ready, 1)

    def vector_finish(self, dve):
        nc = self.nc
        dve.wait_ge(self.xin_loaded, 16)
        dve.sem_inc(self.xin_loaded, -16)
        dve.wait_ge(self.out_free, 1)
        dve.sem_inc(self.out_free, -1)
        nc.vector.tensor_tensor(self.xout[:], self.xin[:], self.b_proj[:], ALU.add).then_inc(self.chain, 1)
        dve.wait_ge(self.chain, 1)
        dve.sem_inc(self.chain, -1)
        dve.wait_ge(self.projected, 1)
        dve.sem_inc(self.projected, -1)
        nc.vector.tensor_tensor(self.xout[:], self.xout[:], self.ps[:, P:2 * P], ALU.add).then_inc(self.chain, 1)
        dve.wait_ge(self.chain, 1)
        dve.sem_inc(self.chain, -1)
        dve.sem_inc(self.ps_free, 1)
        dve.sem_inc(self.xin_free, 1)
        dve.sem_inc(self.out_ready, 1)

    def scalar(self, act, j, place):
        if place == 0 and self.before(j):
            self.scalar_finish(act)
        if place in (0, 2):
            act.wait_ge(self.logit_ready, 1)
            act.sem_inc(self.logit_ready, -1)
            self.nc.scalar.activation(self.prob[:], self.logit[:], ACT.Exp).then_inc(self.prob_ready, 1)

    def scalar_finish(self, act):
        act.wait_ge(self.turned, 1)
        act.sem_inc(self.turned, -1)
        act.sem_inc(self.o_free, 1)
        self.nc.scalar.copy(self.oT[:], self.ps[:, 0:P]).then_inc(self.oT_ready, 1)

    def tensor(self, pe, j, place):
        if place == 1 and self.before(j):
            self.tensor_finish(pe)
        elif place == 4:
            pe.wait_ge(self.ps_free, 1)
            pe.sem_inc(self.ps_free, -1)
            pe.wait_ge(self.o_ready, 1)
            pe.sem_inc(self.o_ready, -1)
            self.nc.tensor.transpose(self.ps[:, 0:P], self.o[:], self.ident[:]).then_inc(self.turned, 1)

    def tensor_finish(self, pe):
        pe.wait_ge(self.oT_ready, 1)
        pe.sem_inc(self.oT_ready, -1)
        self.nc.tensor.matmul(self.ps[:, P:2 * P], self.oT[:], self.w_proj[:], start=True, stop=True).then_inc(self.projected, 1)


def attend_start(nc, attend, count):
    loads = [(attend.ident, attend.w["ident"]), (attend.w_proj, attend.w["w_proj"]), (attend.b_proj, attend.w["b_proj"])]
    attend.tiles(0, count, fresh=True)
    [places] = attend.share(1)
    with nc.Block() as block:
        @block.sync
        def _(sp):
            for dst, src in loads:
                sp.dma_start(dst[:], src).then_inc(attend.consts, 16)
            for k in range(2):
                sp.sem_inc(attend.rec_free[k], 1)
            sp.sem_inc(attend.xin_free, 1)
            attend.load(sp, 0)
            for place in places:
                attend.sync(sp, *place)

        @block.gpsimd
        def _(pool):
            pool.sem_inc(attend.got_free[0], 1)
            pool.sem_inc(attend.got_free[1], 1)
            attend.gather(pool, 0, 0, 0, attend.UNIT)
            for place in places:
                for third in range(3):
                    attend.pool(pool, *place, third)

        @block.vector
        def _(dve):
            dve.sem_inc(attend.out_free, 1)
            dve.wait_ge(attend.consts, 16 * len(loads))
            for place in places:
                attend.vector(dve, *place)

        @block.scalar
        def _(act):
            act.sem_inc(attend.o_free, 1)
            for place in places:
                attend.scalar(act, *place)

        @block.tensor
        def _(pe):
            pe.wait_ge(attend.consts, 16 * len(loads))
            pe.sem_inc(attend.ps_free, 1)
            for place in places:
                attend.tensor(pe, *place)


def attend_finish(nc, attend, table):
    attend.tiles(T, 0)
    attend.table, attend.again = table, 1
    with nc.Block() as block:
        @block.sync
        def _(sp):
            attend.sync_finish(sp, -1)

        @block.gpsimd
        def _(pool):
            pool.wait_ge(attend.gathered[0], 16 * attend.UNIT * (T + 1))
            for at in range(attend.UNIT):
                pool.indirect_dma_start(
                    attend.got[0][:, at, :], None, table,
                    bass.IndirectOffsetOnAxis(ap=attend.rec[0][:, PK_I + at:PK_I + at + 1].bitcast(U32), axis=0),
                ).then_inc(attend.gathered[0], 16)

        @block.vector
        def _(dve):
            attend.vector_finish(dve)

        @block.scalar
        def _(act):
            attend.scalar_finish(act)

        @block.tensor
        def _(pe):
            attend.tensor_finish(pe)


def layer0_inputs(i):
    f = np.float32
    w_off = np.concatenate([
        i["L0_conv_w_off"].reshape(G, K2, 2, C).transpose(2, 0, 1, 3).reshape(2 * GK, C), i["L0_conv_w_mask"]]).T
    b_off = np.concatenate([
        i["L0_conv_b_off"].reshape(G, K2, 2).transpose(2, 0, 1).reshape(2 * GK), i["L0_conv_b_mask"]])[None]
    pconv = np.concatenate([i["L0_conv_pconv_off_w"], i["L0_conv_pconv_mask_w"][None]])
    tok = np.arange(N).reshape(T, P).T
    tap, dil = np.arange(K2), 2 * np.arange(G)[:, None] + 1
    by, bx = ((tap // 3 * dil) - dil).reshape(-1), ((tap % 3 * dil) - dil).reshape(-1)
    base = np.concatenate([(tok // W)[:, :, None] + by, (tok % W)[:, :, None] + bx], -1)
    row0 = np.repeat(np.arange(G) * POS, K2) + XT + 1
    return {
        "w_qkv": i["L0_conv_w_qkv"], "b_qkv": i["L0_conv_b_qkv"].reshape(3, C).T,
        "w_dw": i["L0_conv_w_dw"].reshape(3, C, K2).transpose(1, 0, 2), "b_dw": i["L0_conv_b_dw"].reshape(3, C).T,
        "w_off": w_off, "b_off": b_off, "w_pconv": pconv.transpose(1, 0, 3, 4, 2).reshape(HC, 5, K2, HC),
        "base": base.astype(f), "row0": np.broadcast_to(row0, (P, GK)).astype(f),
        "w_proj": i["L0_conv_w_proj"], "b_proj": np.broadcast_to(i["L0_conv_b_proj"], (P, C)),
    }

def layer1(nc, x, out, w, b, mark, more):
    LEVELS = (3, 5, 7)
    PAD = LEVELS[-1] // 2
    TAPS = sum(k * k for k in LEVELS)
    FIRST = [sum(k * k for k in LEVELS[:n]) for n in range(3)]
    PE_BANKS = 4 if more.count else 3
    PE_ROWS = PE_BANKS * ROWS
    first_places, projection_places, *level_places = more.share(2, 4, *[n / PE_BANKS for n in (5, 9, 20) for _ in range(PE_BANKS)])
    level_places = [level_places[n * PE_BANKS:(n + 1) * PE_BANKS] for n in range(3)]
    with ExitStack() as stack:
        s = Scope(nc, "l1" + mark, stack)
        ident, group, center = s.sb("ident", [P, P]), s.sb("group", [P, P]), s.sb("center", [P, P])
        w_f, w_gate, b_gate = s.sb("w_f", [P, 2 * C]), s.sb("w_gate", [P, 4, P]), s.sb("b_gate", [P, 4])
        b_f, taps, diag = s.sb("b_f", [P, 2]), s.sb("taps", [P, TAPS]), s.sb("diag", [P, TAPS, P])
        w_h, b_h, gamma, beta = s.sb("w_h", [P, C]), s.sb("b_h", [P, 1]), s.sb("gamma", [P, 1]), s.sb("beta", [P, 1])
        w_p, b_p, beta_rows, ones = s.sb("w_p", [P, C]), s.sb("b_p", [P, C]), s.sb("beta_rows", [P, P]), s.sb("ones", [P, P])
        w_pg, row = s.sb("w_pg", [P, C]), s.sb("row", [P, C])
        xT = s.sb("xT", [P, N])
        stats, gn = s.sb("stats", [P, NB, 6]), s.sb("gn", [P, 8])
        q_img, acc, ctx_all = s.sb("q_img", [P, N]), s.sb("acc", [P, N]), s.sb("ctx_all", [P, N])
        xt, resid = (buf[:].rearrange("p (t c) -> p t c", c=C) for buf in (acc, ctx_all))
        img = [s.sb(f"img{n}", [P, H + 2 * PAD, W + 2 * PAD]) for n in range(2)]
        gated = [s.sb(f"gated{n}", [P, BANK]) for n in range(2)]
        sums, cg, rstd = s.sb("sums", [P, PE_BANKS + 1]), s.sb("cg", [P, 2]), s.sb("rstd", [P, T])
        ps, ps_conv, ps_gate = ([s.ps(f"{name}{n}") for n in range(2)] for name in ("ps", "ps_conv", "ps_gate"))
        ps_small = s.ps("ps_small")
        mean_ps, var_ps, ln_ps = ps_small[:, 0:1], ps_small[:, 1:2], ps_small[:, 64:64 + T]

        names = ("consts x_loaded ctx_free resid_loaded ps_ready xT_ready normed moments group_mean group_var var_ready std_ready "
                 "dve_chain act_chain pool_chain diag_ready row_ready row_out row_done pe_img_ready dve_img_ready conv_ready "
                 "conv_free rows_ready_dve gate_ready gate_free q_ready level_done mean_in mean_out "
                 "mod_ready mod_free mod_done center_ready center_free centered ln_ready lnstd_in lnstd_out "
                 "resid_ready out_ready out_free stored").split()
        sem = {n: s.sem(n) for n in names}
        (consts, x_loaded, ctx_free, resid_loaded, ps_ready, xT_ready, normed, moments, group_mean, group_var, var_ready, std_ready,
         dve_chain, act_chain, pool_chain, diag_ready, row_ready, row_out, row_done, pe_img_ready, dve_img_ready, conv_ready,
         conv_free, rows_ready_dve, gate_ready, gate_free, q_ready, level_done, mean_in, mean_out,
         mod_ready, mod_free, mod_done, center_ready, center_free, centered, ln_ready, lnstd_in, lnstd_out,
         resid_ready, out_ready, out_free, stored) = (sem[n] for n in names)
        ps_free = [s.sem(f"ps_free{n}") for n in range(2)]
        loads = [(ident, "ident"), (group, "group"), (center, "center"), (w_f, "w_f"), (w_gate, "w_gate"), (b_gate, "b_gate"),
                 (b_f, "b_f"), (taps, "taps"), (w_h, "w_h"), (b_h, "b_h"), (gamma, "gamma"), (beta, "beta"), (w_p, "w_p"),
                 (b_p, "b_p"), (ones, "ones")]
        NC = 16 * len(loads)
        block = s.block()

        @block.sync
        def _(sp):
            for dst, name in loads:
                sp.dma_start(dst[:], w[name]).then_inc(consts, 16)
            load_tokens(sp, xt, x, b, x_loaded)
            for places in (first_places, projection_places, *(part for level in level_places for part in level)):
                for place in places:
                    more.sync(sp, *place)
            sp.wait_ge(ctx_free, 1)
            sp.sem_inc(ctx_free, -1)
            load_tokens(sp, resid, x, b, resid_loaded)
            sp.wait_ge(out_ready, 1)
            sp.sem_inc(out_ready, -1)
            for n in range(LOADS):
                h = T // LOADS
                dst = out[bass.ds(b, 1), n * h * P:(n + 1) * h * P, :].rearrange("a (t p) c -> p (a t) c", p=P)
                sp.dma_start(dst, resid[:, n * h:(n + 1) * h, :]).then_inc(stored, 16)
            sp.wait_ge(stored, 16 * LOADS)
            sp.sem_inc(stored, -16 * LOADS)

        @block.tensor
        def _(pe):
            pe.wait_ge(consts, NC)
            pe.wait_ge(row_ready, 1)
            pe.sem_inc(row_ready, -1)
            nc.tensor.matmul(ps_small[:, 128:256], beta_rows[:], w_p[:], start=True, stop=True).then_inc(row_out, 1)
            pe.wait_ge(diag_ready, 1)
            for place in first_places:
                more.tensor(pe, *place)
            pe.wait_ge(x_loaded, 16 * LOADS)
            pe.sem_inc(x_loaded, -16 * LOADS)
            for n in range(NB):
                pe.wait_ge(ps_free[n % 2], 1)
                pe.sem_inc(ps_free[n % 2], -1)
                for t in range(4):
                    ins = nc.tensor.transpose(ps[n % 2][:, t * P:(t + 1) * P], xt[:, 4 * n + t, :], ident[:])
                ins.then_inc(ps_ready, 1)
            group_norm_tensor(nc, pe, group, gn, moments, group_mean, group_var, mean_ps, var_ps)
            pe.wait_ge(normed, 1)
            pe.sem_inc(normed, -1)
            for j in (1, 0):
                for n in range(NB):
                    pe.wait_ge(ps_free[n % 2], 1)
                    pe.sem_inc(ps_free[n % 2], -1)
                    nc.tensor.matmul(ps[n % 2][:], w_f[:, j * C:(j + 1) * C], xT[:, n * BANK:(n + 1) * BANK],
                                     start=True, stop=True).then_inc(ps_ready, 1)

            for place in projection_places:
                more.tensor(pe, *place)

            def convolve(level):
                k = LEVELS[level]
                o = PAD - k // 2
                pe.wait_ge(pe_img_ready, 1)
                pe.sem_inc(pe_img_ready, -1)
                for n in range(PE_BANKS):
                    pe.wait_ge(conv_free, 1)
                    pe.sem_inc(conv_free, -1)
                    for tap in range(k * k):
                        y, xx = n * ROWS + o + tap // k, o + tap % k
                        ins = nc.tensor.matmul(ps_conv[n % 2][:], diag[:, FIRST[level] + tap, :],
                                               img[level % 2][:, y:y + ROWS, xx:xx + W], start=(tap == 0), stop=(tap == k * k - 1))
                    ins.then_inc(conv_ready, 1)
                    for place in level_places[level][n]:
                        more.tensor(pe, *place)

            def gate(level):
                for n in range(NB):
                    pe.wait_ge(gate_free, 1)
                    pe.sem_inc(gate_free, -1)
                    nc.tensor.matmul(ps_gate[n % 2][:], w_gate[:, level, :], xT[:, n * BANK:(n + 1) * BANK],
                                     start=True, stop=True).then_inc(gate_ready, 1)

            convolve(0)
            convolve(1)
            gate(0)
            convolve(2)
            gate(1)
            gate(2)
            gate(3)
            for n in range(NB):
                pe.wait_ge(mod_ready, 1)
                pe.sem_inc(mod_ready, -1)
                pe.wait_ge(ps_free[n % 2], 1)
                pe.sem_inc(ps_free[n % 2], -1)
                nc.tensor.matmul(ps[n % 2][:], w_h[:], ctx_all[:, n * BANK:(n + 1) * BANK], start=True, stop=True
                                 ).then_inc(mod_free, 1)
            for n in range(NB):
                pe.wait_ge(mod_done, 1)
                pe.sem_inc(mod_done, -1)
                pe.wait_ge(ps_free[n % 2], 1)
                pe.sem_inc(ps_free[n % 2], -1)
                nc.tensor.matmul(ps[n % 2][:], center[:], q_img[:, n * BANK:(n + 1) * BANK], start=True, stop=True
                                 ).then_inc(center_ready, 1)
            pe.wait_ge(centered, 1)
            pe.sem_inc(centered, -1)
            for t in range(T):
                ins = nc.tensor.matmul(ln_ps[:, t:t + 1], xT[:, t * P:(t + 1) * P], ones[:, 0:1], start=True, stop=True)
            ins.then_inc(ln_ready, 1)
            for n in range(NB):
                pe.wait_ge(ps_free[n % 2], 1)
                pe.sem_inc(ps_free[n % 2], -1)
                for t in range(4):
                    ins = nc.tensor.matmul(ps[n % 2][:, t * P:(t + 1) * P], acc[:, (4 * n + t) * P:(4 * n + t + 1) * P], w_pg[:],
                                           start=True, stop=True)
                ins.then_inc(out_free, 1)

        @block.scalar
        def _(act):
            act.sem_inc(ps_free[0], 1)
            act.sem_inc(ps_free[1], 1)
            act.sem_inc(conv_free, 2)
            act.wait_ge(consts, NC)

            def gelu(dst, src, n, chain=True):
                nc.scalar.activation(dst, src, ACT.Gelu, accum_out=sums[:, n:n + 1]).then_inc(act_chain, 1)
                act.wait_ge(act_chain, 1)
                act.sem_inc(act_chain, -1)

            for place in first_places:
                more.scalar(act, *place)
            for n in range(NB):
                act.wait_ge(ps_ready, 1)
                act.sem_inc(ps_ready, -1)
                nc.scalar.copy(xT[:, n * BANK:(n + 1) * BANK], ps[n % 2][:]).then_inc(act_chain, 1)
                act.wait_ge(act_chain, 1)
                act.sem_inc(act_chain, -1)
                act.sem_inc(ps_free[n % 2], 1)
            act.sem_inc(xT_ready, 1)
            act.wait_ge(var_ready, 1)
            act.sem_inc(var_ready, -1)
            nc.scalar.activation(gn[:, 6:7], gn[:, 5:6], ACT.Sqrt).then_inc(std_ready, 1)
            for j in (1, 0):
                for n in range(NB):
                    act.wait_ge(ps_ready, 1)
                    act.sem_inc(ps_ready, -1)
                    src = ps[n % 2][:]
                    if j == 1:
                        dst = img[0][:, PAD + n * ROWS:PAD + (n + 1) * ROWS, PAD:PAD + W]
                        src = src.rearrange("p (y x) -> p y x", x=W)
                    else:
                        dst = q_img[:, n * BANK:(n + 1) * BANK]
                    nc.scalar.activation(dst, src, ACT.Identity, bias=b_f[:, j:j + 1]).then_inc(act_chain, 1)
                    act.wait_ge(act_chain, 1)
                    act.sem_inc(act_chain, -1)
                    act.sem_inc(ps_free[n % 2], 1)
                    if n == NB // 2 and j == 1:
                        for place in projection_places[:2]:
                            more.scalar(act, *place)
                if j == 1:
                    act.sem_inc(pe_img_ready, 1)
                    act.sem_inc(dve_img_ready, 1)
            act.sem_inc(q_ready, 1)
            for place in projection_places[2:]:
                more.scalar(act, *place)
            for level in range(3):
                dst = img[(level + 1) % 2]
                src = acc[:].rearrange("p (y x) -> p y x", x=W)
                if level == 2:
                    act.wait_ge(level_done, 1)
                    act.sem_inc(level_done, -1)
                for n in range(PE_BANKS):
                    for place in level_places[level][n]:
                        more.scalar(act, *place)
                    act.wait_ge(conv_ready, 1)
                    act.sem_inc(conv_ready, -1)
                    gelu(dst[:, PAD + n * ROWS:PAD + (n + 1) * ROWS, PAD:PAD + W],
                         ps_conv[n % 2][:].rearrange("p (y x) -> p y x", x=W), n)
                    act.sem_inc(conv_free, 1)
                act.wait_ge(rows_ready_dve, 1)
                act.sem_inc(rows_ready_dve, -1)
                gelu(dst[:, PAD + PE_ROWS:PAD + H, PAD:PAD + W], src[:, PE_ROWS:H, :], PE_BANKS)
                act.sem_inc(dve_img_ready, 1)
                if level < 2:
                    act.sem_inc(pe_img_ready, 1)
            act.wait_ge(mean_in, 1)
            act.sem_inc(mean_in, -1)
            nc.scalar.activation(cg[:, 1:2], cg[:, 0:1], ACT.Gelu).then_inc(mean_out, 1)
            for n in range(NB):
                act.wait_ge(center_ready, 1)
                act.sem_inc(center_ready, -1)
                nc.scalar.copy(acc[:, n * BANK:(n + 1) * BANK], ps[n % 2][:])
                nc.scalar.activation(xT[:, n * BANK:(n + 1) * BANK], ps[n % 2][:], ACT.Square).then_inc(act_chain, 1)
                act.wait_ge(act_chain, 1)
                act.sem_inc(act_chain, -1)
                act.sem_inc(ps_free[n % 2], 1)
            act.sem_inc(centered, 1)
            act.wait_ge(lnstd_in, 1)
            act.sem_inc(lnstd_in, -1)
            nc.scalar.activation(rstd[:], rstd[:], ACT.Sqrt).then_inc(lnstd_out, 1)

        def convolve_rows(dve, level):
            first, rows = PE_ROWS, H - PE_ROWS
            k = LEVELS[level]
            o = PAD - k // 2
            out_rows = acc[:].rearrange("p (y x) -> p y x", x=W)[:, first:first + rows, :]
            places = [place for part in level_places[level] for place in part]
            for tap in range(k * k):
                for place in places[tap * len(places) // (k * k):(tap + 1) * len(places) // (k * k)]:
                    more.vector(dve, *place)
                y, xx, c = first + o + tap // k, o + tap % k, FIRST[level] + tap
                src = img[level % 2][:, y:y + rows, xx:xx + W]
                if tap == 0:
                    ins = nc.vector.tensor_scalar(out_rows, src, taps[:, c:c + 1], None, ALU.mult)
                else:
                    ins = nc.vector.scalar_tensor_tensor(out=out_rows, in0=src, scalar=taps[:, c:c + 1], in1=out_rows,
                                                         op0=ALU.mult, op1=ALU.add)
                ins.then_inc(dve_chain, 1)
                dve.wait_ge(dve_chain, 1)
                dve.sem_inc(dve_chain, -1)

        @block.gpsimd
        def _(pool):
            pool.wait_ge(consts, NC)
            for n in range(TAPS):
                ins = nc.gpsimd.tensor_scalar(diag[:, n, :], ident[:], taps[:, n:n + 1], None, ALU.mult)
            ins.then_inc(pool_chain, 1)
            pool.wait_ge(pool_chain, 1)
            pool.sem_inc(pool_chain, -1)
            pool.sem_inc(diag_ready, 1)
            for places in (first_places, projection_places, *(part for level in level_places for part in level)):
                for place in places:
                    for third in range(3):
                        more.pool(pool, *place, third)
            pool.wait_ge(row_done, 1)
            pool.sem_inc(row_done, -1)
            pool.wait_ge(resid_loaded, 16 * LOADS)
            pool.sem_inc(resid_loaded, -16 * LOADS)
            nc.gpsimd.tensor_tensor(resid, resid, row[:].unsqueeze(1).to_broadcast([P, T, C]), ALU.add).then_inc(pool_chain, 1)
            pool.wait_ge(pool_chain, 1)
            pool.sem_inc(pool_chain, -1)
            pool.sem_inc(resid_ready, 1)

        @block.vector
        def _(dve):
            for im in img:
                nc.vector.memset(im[:], 0.0)
            dve.wait_ge(consts, NC)
            nc.vector.tensor_scalar(w_pg[:], w_p[:], gamma[:, 0:1], None, ALU.mult)
            nc.vector.tensor_scalar(beta_rows[:], ones[:], beta[:, 0:1], None, ALU.mult)
            dve.drain().then_inc(dve_chain, 1)
            dve.wait_ge(dve_chain, 1)
            dve.sem_inc(dve_chain, -1)
            dve.sem_inc(row_ready, 1)
            dve.wait_ge(diag_ready, 1)
            dve.wait_ge(row_out, 1)
            dve.sem_inc(row_out, -1)
            nc.vector.tensor_tensor(row[:], ps_small[:, 128:256], b_p[:], ALU.add).then_inc(dve_chain, 1)
            dve.wait_ge(dve_chain, 1)
            dve.sem_inc(dve_chain, -1)
            dve.sem_inc(row_done, 1)
            dve.sem_inc(gate_free, 2)

            def gate(level):
                for n in range(NB):
                    dve.wait_ge(gate_ready, 1)
                    dve.sem_inc(gate_ready, -1)
                    rows = slice(PAD + n * ROWS, PAD + (n + 1) * ROWS)
                    total = ctx_all[:, n * BANK:(n + 1) * BANK]
                    if level < 3:
                        dst = total if level == 0 else gated[n % 2][:]
                        nc.vector.scalar_tensor_tensor(
                            out=dst.rearrange("p (y x) -> p y x", x=W), in0=ps_gate[n % 2][:].rearrange("p (y x) -> p y x", x=W),
                            scalar=b_gate[:, level:level + 1], in1=img[(level + 1) % 2][:, rows, PAD:PAD + W],
                            op0=ALU.add, op1=ALU.mult).then_inc(dve_chain, 1)
                        dve.wait_ge(dve_chain, 1)
                        dve.sem_inc(dve_chain, -1)
                    else:
                        nc.vector.tensor_scalar(gated[n % 2][:], ps_gate[n % 2][:], b_gate[:, 3:4], cg[:, 1:2],
                                                          ALU.add, ALU.mult).then_inc(dve_chain, 1)
                        dve.wait_ge(dve_chain, 1)
                        dve.sem_inc(dve_chain, -1)
                    dve.sem_inc(gate_free, 1)
                    if level:
                        nc.vector.tensor_tensor(total, total, gated[n % 2][:], ALU.add).then_inc(dve_chain, 1)
                        dve.wait_ge(dve_chain, 1)
                        dve.sem_inc(dve_chain, -1)
                    if level == 3:
                        dve.sem_inc(mod_ready, 1)

            for place in first_places:
                more.vector(dve, *place)
            dve.wait_ge(xT_ready, 1)
            dve.sem_inc(xT_ready, -1)
            group_norm_vector(nc, dve, xT, stats, gn, dve_chain, moments, group_mean, group_var,
                              var_ready, std_ready, mean_ps, var_ps)
            dve.sem_inc(normed, 1)
            for place in projection_places:
                more.vector(dve, *place)
            for level in range(3):
                dve.wait_ge(dve_img_ready, 1)
                dve.sem_inc(dve_img_ready, -1)
                convolve_rows(dve, level)
                dve.sem_inc(rows_ready_dve, 1)
                if level:
                    gate(level - 1)
                if level == 1:
                    dve.sem_inc(level_done, 1)
            dve.wait_ge(dve_img_ready, 1)
            dve.sem_inc(dve_img_ready, -1)
            gate(2)
            nc.vector.tensor_reduce(cg[:, 0:1], sums[:], AX.X, ALU.add).then_inc(dve_chain, 1)
            dve.wait_ge(dve_chain, 1)
            dve.sem_inc(dve_chain, -1)
            nc.vector.tensor_scalar(cg[:, 0:1], cg[:, 0:1], 1.0 / N, None, ALU.mult).then_inc(dve_chain, 1)
            dve.wait_ge(dve_chain, 1)
            dve.sem_inc(dve_chain, -1)
            dve.sem_inc(mean_in, 1)
            dve.wait_ge(mean_out, 1)
            dve.sem_inc(mean_out, -1)
            gate(3)
            dve.wait_ge(q_ready, 1)
            dve.sem_inc(q_ready, -1)
            for n in range(NB):
                dve.wait_ge(mod_free, 1)
                dve.sem_inc(mod_free, -1)
                q = q_img[:, n * BANK:(n + 1) * BANK]
                nc.vector.scalar_tensor_tensor(out=q, in0=ps[n % 2][:], scalar=b_h[:, 0:1], in1=q,
                                                         op0=ALU.add, op1=ALU.mult).then_inc(dve_chain, 1)
                dve.wait_ge(dve_chain, 1)
                dve.sem_inc(dve_chain, -1)
                dve.sem_inc(ps_free[n % 2], 1)
                dve.sem_inc(mod_done, 1)
            dve.sem_inc(ctx_free, 1)
            dve.wait_ge(ln_ready, 1)
            dve.sem_inc(ln_ready, -1)
            nc.vector.tensor_scalar(rstd[:], ln_ps, 1.0 / C, 1e-3, ALU.mult, ALU.add).then_inc(dve_chain, 1)
            dve.wait_ge(dve_chain, 1)
            dve.sem_inc(dve_chain, -1)
            nc.vector.reciprocal(rstd[:], rstd[:]).then_inc(dve_chain, 1)
            dve.wait_ge(dve_chain, 1)
            dve.sem_inc(dve_chain, -1)
            dve.sem_inc(lnstd_in, 1)
            dve.wait_ge(lnstd_out, 1)
            dve.sem_inc(lnstd_out, -1)
            dve.wait_ge(resid_ready, 1)
            dve.sem_inc(resid_ready, -1)
            for n in range(NB):
                dve.wait_ge(out_free, 1)
                dve.sem_inc(out_free, -1)
                for t in range(4 * n, 4 * n + 4):
                    ins = nc.vector.scalar_tensor_tensor(out=resid[:, t, :], in0=ps[n % 2][:, t % 4 * P:(t % 4 + 1) * P],
                                                         scalar=rstd[:, t:t + 1], in1=resid[:, t, :], op0=ALU.mult, op1=ALU.add)
                ins.then_inc(dve_chain, 1)
                dve.wait_ge(dve_chain, 1)
                dve.sem_inc(dve_chain, -1)
                dve.sem_inc(ps_free[n % 2], 1)
            dve.sem_inc(out_ready, 1)


def layer1_inputs(i):
    wf = i["L1_conv_Wf"]
    col = {n: i[f"L1_conv_{n}"].reshape(C, 1) for n in ("bh", "gamma", "beta")}
    bf = i["L1_conv_bf"]
    return {
        "w_f": wf[:, :2 * C], "w_gate": np.broadcast_to(wf[:, 2 * C:, None], (C, 4, P)),
        "b_gate": np.broadcast_to(bf[2 * C:], (P, 4)), "b_f": bf[:2 * C].reshape(2, C).T,
        "taps": np.concatenate([i[f"L1_conv_k{n}"].reshape(-1, C) for n in range(3)]).T,
        "w_h": i["L1_conv_Wh"], "b_h": col["bh"], "gamma": col["gamma"], "beta": col["beta"],
        "w_p": i["L1_conv_Wp"], "b_p": np.broadcast_to(i["L1_conv_bp"], (P, C)),
    }

def token_norm_vector(nc, dve, xt, xn, stats, mv, rstd, eps, chain, var_ready, std_ready):
    for t in range(T):
        ins = nc.vector.bn_stats(stats[:, t, :], xt[:, t, :])
    ins.then_inc(chain, 1)
    dve.wait_ge(chain, 1)
    dve.sem_inc(chain, -1)
    for t in range(T):
        ins = nc.vector.bn_aggr(mv[:, t, :], stats[:, t, :])
    ins.then_inc(chain, 1)
    dve.wait_ge(chain, 1)
    dve.sem_inc(chain, -1)
    nc.vector.tensor_scalar(rstd[:], mv[:, :, 1], eps, None, ALU.add).then_inc(chain, 1)
    dve.wait_ge(chain, 1)
    dve.sem_inc(chain, -1)
    nc.vector.reciprocal(rstd[:], rstd[:]).then_inc(chain, 1)
    dve.wait_ge(chain, 1)
    dve.sem_inc(chain, -1)
    dve.sem_inc(var_ready, 1)
    dve.wait_ge(std_ready, 1)
    dve.sem_inc(std_ready, -1)
    for t in range(T):
        ins = nc.vector.tensor_scalar(xn[:, t, :], xt[:, t, :], mv[:, t, 0:1], rstd[:, t:t + 1], ALU.subtract, ALU.mult)
    ins.then_inc(chain, 1)
    dve.wait_ge(chain, 1)
    dve.sem_inc(chain, -1)


NH, HD, DS = 4, 64, 64
DI = NH * HD
CONV = DI + 2 * DS
KC = 4


def layer2_mamba(nc, x, out, w, b, mark, more):
    with ExitStack() as stack:
        s = Scope(nc, "l2a" + mark, stack)
        ident, ones = s.sb("ident", [P, P]), s.sb("ones", [P, P])
        upto, behind = s.sb("upto", [P, 2, P]), s.sb("behind", [P, 2, P])
        quarter = s.sb("quarter", [P, 2, P])
        w_conv = s.sb("w_conv", [P, 2, KC, CONV])
        w_xbc, w_z, w_dt = s.sb("w_xbc", [P, 2, CONV]), s.sb("w_z", [P, 2, DI]), s.sb("w_dt", [P, 2 * NH])
        b_conv, b_dt = s.sb("b_conv", [1, 2, CONV]), s.sb("b_dt", [P, 2 * NH])
        a_log, d_half = s.sb("a_log", [P, 2 * NH]), s.sb("d_half", [P, 2 * NH])
        w_out, norm = s.sb("w_out", [P, 2, 2, C]), s.sb("norm", [P, 2, 2])
        xt, xT = s.sb("xt", [P, T, C]), s.sb("xT", [P, KC - 1 + N + KC - 1])
        hidden = [s.sb(f"hidden{d}", [P, T, C]) for d in range(2)]
        stats, mv, rstd = s.sb("stats", [P, T, 6]), s.sb("mv", [P, T, 2]), s.sb("rstd", [P, T])
        dt, soft, dA = s.sb("dt", [P, 2, T, NH]), s.sb("soft", [P, 2, T, NH]), s.sb("dA", [P, 2, T, NH])
        decay = s.sb("decay", [P, 2, 3, T, NH])
        squares, rms = s.sb("squares", [P, 2, T]), s.sb("rms", [P, 2, T])
        tanh_x, tanh_z = s.sb("tanh_x", [P, CONV]), s.sb("tanh_z", [P, DI])
        xbc, gate_z = [[s.sb(f"{n}{d}", [P, k]) for d in range(2)] for n, k in (("xbc", CONV), ("gate_z", DI))]
        xdt, xdec, xD = [[s.sb(f"{n}{d}", [P, DI]) for d in range(2)] for n in ("xdt", "xdec", "xD")]
        steps_, L = [[s.sb(f"{n}{d}", [P, NH, P]) for d in range(2)] for n in ("steps", "L")]
        M, cb, bcT = s.sb("M", [P, NH, P]), s.sb("cb", [P, P]), s.sb("bcT", [DS, 2, P])
        state = [s.sb(f"state{d}", [DS, DI]) for d in range(2)]
        y, ygT, scrap = s.sb("y", [P, DI]), s.sb("ygT", [P, 2, P]), s.sb("scrap", [P, DI])
        ps_x, ps_z, ps_bc, ps_seg, ps_y, ps_s, ps_t = (s.ps("ps_" + n) for n in ("x", "z", "bc", "seg", "y", "s", "t"))
        ps_o = ps_t[:, DI:DI + C]

        names = ("consts x_loaded xt_free normed x_ready x_done var_ready std_ready dve_chain act_chain pool_chain weights_ready "
                 "setup_exp setup_done dt_ready dt_used abs_ready soft_ready dA_ready cum_ready decay_ready scan_go_pe scan_go_pool xbc_ready tanh_x_ready "
                 "bc_ready z_ready t_free z_free tanh_z_ready tr_ready bct_ready cb_ready cbm_ready steps_ready seg_ready l_ready m_ready "
                 "xdt_ready xdec_ready xd_ready y_ready yg_ready yg_ready_act yt_ready ygt_ready out_ready batch_done rms_in rms_out "
                 "result_ready stored").split()
        S = {n: s.sem(n) for n in names}
        loads = [(ident, "ident"), (ones, "ones"), (upto, "upto2"), (behind, "behind2"), (w_conv, "conv_w"), (w_xbc, "w_xbc"),
                 (w_z, "w_z"), (w_dt, "w_dt"), (b_conv, "conv_b"), (b_dt, "dt_bias"), (a_log, "A_log"), (d_half, "D"),
                 (w_out, "w_out"), (norm, "norm_w")]
        NC = 16 * len(loads)
        block = s.block()
        first_places, *beside = more.share(2 * T * 5 / 45, *[1] * (2 * T))
        STEPS = [(n % 2, n // 2 if n % 2 == 0 else T - 1 - n // 2) for n in range(2 * T)]

        @block.sync
        def _(sp):
            for dst, name in loads:
                sp.dma_start(dst[:], w[name]).then_inc(S["consts"], 16)
            sp.wait_ge(S["xt_free"], 1)
            sp.sem_inc(S["xt_free"], -1)
            load_tokens(sp, xt, x, b, S["x_loaded"])
            for places in (first_places, *beside):
                for place in places:
                    more.sync(sp, *place)
            sp.wait_ge(S["result_ready"], 1)
            sp.sem_inc(S["result_ready"], -1)
            for n in range(LOADS):
                h = T // LOADS
                dst = out[bass.ds(b, 1), n * h * P:(n + 1) * h * P, :].rearrange("a (t p) c -> p (a t) c", p=P)
                sp.dma_start(dst, xt[:, n * h:(n + 1) * h, :]).then_inc(S["stored"], 16)
            sp.wait_ge(S["stored"], 16 * LOADS)
            sp.sem_inc(S["stored"], -16 * LOADS)
            sp.sem_inc(S["xt_free"], 1)

        @block.tensor
        def _(pe):
            pe.wait_ge(S["consts"], NC)
            pe.wait_ge(S["weights_ready"], 1)
            banks = [ps_x, ps_z]

            def project_x(n):
                d, t = STEPS[n]
                for i in range(KC):
                    at = t * P + (i if d == 0 else 2 * (KC - 1) - i)
                    nc.tensor.matmul(ps_x[:, 0:CONV], xT[:, at:at + P], w_conv[:, d, i, :], start=(i == 0), stop=False)
                nc.tensor.matmul(ps_x[:, 0:CONV], ones[0:1, :], b_conv[:, d, :], start=False, stop=True).then_inc(S["xbc_ready"], 1)

            def project_z(n):
                d, t = STEPS[n]
                pe.wait_ge(S["z_free"], 1)
                pe.sem_inc(S["z_free"], -1)
                nc.tensor.matmul(ps_z[:, 0:DI], xT[:, KC - 1 + t * P:KC - 1 + (t + 1) * P], w_z[:, d, :], start=True, stop=True
                                 ).then_inc(S["z_ready"], 1)

            def segments(n):
                pe.wait_ge(S["steps_ready"], 1)
                pe.sem_inc(S["steps_ready"], -1)
                nc.tensor.matmul(ps_seg[:], behind[:, STEPS[n][0], :], steps_[n % 2][:].rearrange("p h l -> p (h l)"),
                                 start=True, stop=True).then_inc(S["seg_ready"], 1)

            def finish(n):
                d, t = STEPS[n]
                pe.wait_ge(S["yg_ready"], 1)
                pe.sem_inc(S["yg_ready"], -1)
                pe.wait_ge(S["t_free"], 1)
                pe.sem_inc(S["t_free"], -1)
                nc.tensor.transpose(ps_t[:, 0:P], y[:, 0:P], ident[:])
                nc.tensor.transpose(ps_t[:, P:2 * P], y[:, P:2 * P], ident[:]).then_inc(S["yt_ready"], 1)
                pe.wait_ge(S["ygt_ready"], 1)
                pe.sem_inc(S["ygt_ready"], -1)
                nc.tensor.matmul(ps_o, ygT[:, 0, :], w_out[:, d, 0, :], start=True, stop=False)
                nc.tensor.matmul(ps_o, ygT[:, 1, :], w_out[:, d, 1, :], start=False, stop=True).then_inc(S["out_ready"], 1)

            for place in first_places:
                more.tensor(pe, *place)
            pe.wait_ge(S["normed"], 1)
            pe.sem_inc(S["normed"], -1)
            for n in range(NB):
                if n >= 2:
                    pe.wait_ge(S["x_done"], 1)
                    pe.sem_inc(S["x_done"], -1)
                for k in range(4):
                    ins = nc.tensor.transpose(banks[n % 2][:, k * P:(k + 1) * P], hidden[0][:, 4 * n + k, :], ident[:])
                ins.then_inc(S["x_ready"], 1)
            pe.wait_ge(S["x_done"], 2)
            pe.sem_inc(S["x_done"], -2)
            for t in range(T):
                ins = nc.tensor.matmul(ps_seg[:, t * 2 * NH:(t + 1) * 2 * NH], xT[:, KC - 1 + t * P:KC - 1 + (t + 1) * P], w_dt[:],
                                       start=True, stop=True)
            ins.then_inc(S["dt_ready"], 1)
            pe.wait_ge(S["dA_ready"], 1)
            pe.sem_inc(S["dA_ready"], -1)
            for d, bank in ((0, ps_y), (1, ps_s)):
                rhs = dA[:, d].rearrange("p t h -> p (t h)")
                for k, mask in enumerate((upto[:, d, :], behind[:, d, :], ones[:])):
                    ins = nc.tensor.matmul(bank[:, k * P:(k + 1) * P], mask, rhs, start=True, stop=True)
            ins.then_inc(S["cum_ready"], 1)
            pe.wait_ge(S["scan_go_pe"], 1)
            pe.sem_inc(S["scan_go_pe"], -1)
            project_x(0)
            project_z(0)
            segments(0)
            for n, (d, t) in enumerate(STEPS):
                last = n == 2 * T - 1
                pe.wait_ge(S["bc_ready"], 1)
                pe.sem_inc(S["bc_ready"], -1)
                nc.tensor.transpose(ps_bc[0:DS, 0:P], xbc[d][:, DI:DI + DS], ident[:])
                nc.tensor.transpose(ps_bc[0:DS, P:2 * P], xbc[d][:, DI + DS:], ident[:]).then_inc(S["tr_ready"], 1)
                if not last:
                    project_x(n + 1)
                pe.wait_ge(S["bct_ready"], 1)
                pe.sem_inc(S["bct_ready"], -1)
                nc.tensor.matmul(ps_bc[:, 2 * P:3 * P], bcT[:, 0, :], bcT[:, 1, :], start=True, stop=True).then_inc(S["cb_ready"], 1)
                if not last:
                    project_z(n + 1)
                    segments(n + 1)
                if n:
                    finish(n - 1)
                pe.wait_ge(S["m_ready"], 1)
                pe.sem_inc(S["m_ready"], -1)
                for h in range(NH):
                    nc.tensor.matmul(ps_y[:, h * HD:(h + 1) * HD], M[:, h, :], xdt[d][:, h * HD:(h + 1) * HD], start=True, stop=True)
                nc.tensor.matmul(ps_y[:, DI:2 * DI], bcT[:, 1, :], state[d][:], start=True, stop=True)
                pe.wait_ge(S["xdec_ready"], 1)
                pe.sem_inc(S["xdec_ready"], -1)
                nc.tensor.matmul(ps_s[0:DS, 0:DI], xbc[d][:, DI:DI + DS], xdec[d][:], start=True, stop=True).then_inc(S["y_ready"], 1)
                for place in beside[n]:
                    more.tensor(pe, *place)
            finish(2 * T - 1)

        @block.scalar
        def _(act):
            act.wait_ge(S["consts"], NC)
            nc.scalar.activation(a_log[:], a_log[:], ACT.Exp).then_inc(S["setup_exp"], 1)

            def activate_x(n):
                act.wait_ge(S["xbc_ready"], 1)
                act.sem_inc(S["xbc_ready"], -1)
                nc.scalar.activation(tanh_x[:], ps_x[:, 0:CONV], ACT.Tanh, scale=0.5).then_inc(S["tanh_x_ready"], 1)

            def activate_z(n):
                act.wait_ge(S["z_ready"], 1)
                act.sem_inc(S["z_ready"], -1)
                nc.scalar.activation(tanh_z[:], ps_z[:, 0:DI], ACT.Tanh, scale=0.5).then_inc(S["tanh_z_ready"], 1)

            def exponentials(n):
                act.wait_ge(S["seg_ready"], 1)
                act.sem_inc(S["seg_ready"], -1)
                nc.scalar.activation(L[n % 2][:].rearrange("p h l -> p (h l)"), ps_seg[:], ACT.Exp).then_inc(S["l_ready"], 1)

            def finish(n):
                d, t = STEPS[n]
                act.wait_ge(S["yt_ready"], 1)
                act.sem_inc(S["yt_ready"], -1)
                nc.scalar.copy(ygT[:].rearrange("p a l -> p (a l)"), ps_t[:, 0:DI]).then_inc(S["ygt_ready"], 1)
                act.wait_ge(S["out_ready"], 1)
                act.sem_inc(S["out_ready"], -1)
                nc.scalar.copy(hidden[d][:, t, :], ps_o).then_inc(act_chain, 1)
                act.wait_ge(act_chain, 1)
                act.sem_inc(act_chain, -1)
                act.sem_inc(S["t_free"], 1)

            act_chain = S["act_chain"]
            act.sem_inc(S["t_free"], 1)
            for place in first_places:
                more.scalar(act, *place)
            act.wait_ge(S["var_ready"], 1)
            act.sem_inc(S["var_ready"], -1)
            nc.scalar.activation(rstd[:], rstd[:], ACT.Sqrt).then_inc(S["std_ready"], 1)
            for n in range(NB):
                act.wait_ge(S["x_ready"], 1)
                act.sem_inc(S["x_ready"], -1)
                nc.scalar.copy(xT[:, KC - 1 + n * BANK:KC - 1 + (n + 1) * BANK], (ps_x, ps_z)[n % 2][:]).then_inc(S["x_done"], 1)
            act.wait_ge(S["abs_ready"], 1)
            act.sem_inc(S["abs_ready"], -1)
            nc.scalar.activation(soft[:], soft[:], ACT.Exp, scale=-1.0).then_inc(act_chain, 1)
            act.wait_ge(act_chain, 1)
            act.sem_inc(act_chain, -1)
            nc.scalar.activation(soft[:], soft[:], ACT.Ln, bias=1.0).then_inc(S["soft_ready"], 1)
            act.wait_ge(S["cum_ready"], 1)
            act.sem_inc(S["cum_ready"], -1)
            for d, bank in ((0, ps_y), (1, ps_s)):
                ins = nc.scalar.activation(decay[:, d].rearrange("p k t h -> p (k t h)"), bank[:, 0:3 * P], ACT.Exp)
            ins.then_inc(S["decay_ready"], 1)
            activate_x(0)
            activate_z(0)
            exponentials(0)
            for n, (d, t) in enumerate(STEPS):
                act.wait_ge(S["tr_ready"], 1)
                act.sem_inc(S["tr_ready"], -1)
                nc.scalar.copy(bcT[:].rearrange("p a l -> p (a l)"), ps_bc[0:DS, 0:2 * P]).then_inc(S["bct_ready"], 1)
                if n < 2 * T - 1:
                    activate_x(n + 1)
                    activate_z(n + 1)
                    exponentials(n + 1)
                if n:
                    finish(n - 1)
                act.wait_ge(S["yg_ready_act"], 1)
                act.sem_inc(S["yg_ready_act"], -1)
                nc.scalar.activation(scrap[:], y[:], ACT.Square, accum_out=squares[:, d, t:t + 1]).then_inc(act_chain, 1)
                act.wait_ge(act_chain, 1)
                act.sem_inc(act_chain, -1)
                for place in beside[n]:
                    more.scalar(act, *place)
            finish(2 * T - 1)
            act.sem_inc(S["batch_done"], 1)
            act.wait_ge(S["rms_in"], 1)
            act.sem_inc(S["rms_in"], -1)
            nc.scalar.activation(rms[:], rms[:], ACT.Sqrt).then_inc(S["rms_out"], 1)

        def heads(ap):
            return ap.rearrange("p (h c) -> p h c", h=NH)

        def per_head(ap, parts=P, width=HD):
            return ap.unsqueeze(2).to_broadcast([parts, NH, width])

        @block.gpsimd
        def _(pool):
            pool.wait_ge(S["consts"], NC)

            def make_steps(n):
                d, t = STEPS[n]
                nc.gpsimd.tensor_tensor(steps_[n % 2][:], upto[:, d:d + 1, :].to_broadcast([P, NH, P]),
                                                   per_head(dA[:, d, t, :], P, P), ALU.mult).then_inc(S["pool_chain"], 1)
                pool.wait_ge(S["pool_chain"], 1)
                pool.sem_inc(S["pool_chain"], -1)
                pool.sem_inc(S["steps_ready"], 1)

            def scale_x(n):
                d, t = STEPS[n]
                pool.wait_ge(S["xdt_ready"], 1)
                pool.sem_inc(S["xdt_ready"], -1)
                nc.gpsimd.tensor_tensor(heads(xdec[d][:]), heads(xdt[d][:]), per_head(decay[:, d, 1, t, :]), ALU.mult).then_inc(S["pool_chain"], 1)
                pool.wait_ge(S["pool_chain"], 1)
                pool.sem_inc(S["pool_chain"], -1)
                pool.sem_inc(S["xdec_ready"], 1)
                nc.gpsimd.tensor_tensor(heads(xD[d][:]), heads(xbc[d][:, 0:DI]), per_head(d_half[:, d * NH:(d + 1) * NH]),
                                                   ALU.mult).then_inc(S["pool_chain"], 1)
                pool.wait_ge(S["pool_chain"], 1)
                pool.sem_inc(S["pool_chain"], -1)
                pool.sem_inc(S["xd_ready"], 1)

            for place in first_places:
                for third in range(3):
                    more.pool(pool, *place, third)
            pool.wait_ge(S["scan_go_pool"], 1)
            pool.sem_inc(S["scan_go_pool"], -1)
            make_steps(0)
            make_steps(1)
            scale_x(0)
            for n, (d, t) in enumerate(STEPS):
                pool.wait_ge(S["l_ready"], 1)
                pool.sem_inc(S["l_ready"], -1)
                pool.wait_ge(S["cbm_ready"], 1)
                pool.sem_inc(S["cbm_ready"], -1)
                nc.gpsimd.tensor_tensor(M[:], L[n % 2][:], cb[:].unsqueeze(1).to_broadcast([P, NH, P]), ALU.mult).then_inc(S["pool_chain"], 1)
                pool.wait_ge(S["pool_chain"], 1)
                pool.sem_inc(S["pool_chain"], -1)
                pool.sem_inc(S["m_ready"], 1)
                for third in range(3):
                    for place in beside[n]:
                        more.pool(pool, *place, third)
                    if third == 0 and n + 2 < 2 * T:
                        make_steps(n + 2)
                    if third == 1 and n + 1 < 2 * T:
                        scale_x(n + 1)

        @block.vector
        def _(dve):
            chain = S["dve_chain"]
            nc.vector.memset(xT[:, 0:KC - 1], 0.0)
            nc.vector.memset(xT[:, KC - 1 + N:], 0.0)
            dve.wait_ge(S["consts"], NC)
            for d in range(2):
                for i in range(KC):
                    nc.vector.tensor_tensor(w_conv[:, d, i, :], w_conv[:, d, i, :], w_xbc[:, d, :], ALU.mult)
                for k in range(2):
                    nc.vector.tensor_scalar(w_out[:, d, k, :], w_out[:, d, k, :], norm[:, d, k:k + 1], None, ALU.mult)
            nc.vector.tensor_scalar(quarter[:], upto[:], 0.25, None, ALU.mult)
            nc.vector.tensor_scalar(d_half[:], d_half[:], 0.5, None, ALU.mult)
            dve.wait_ge(S["setup_exp"], 1)
            nc.vector.tensor_scalar(a_log[:], a_log[:], -1.0, None, ALU.mult).then_inc(chain, 1)
            dve.wait_ge(chain, 1)
            dve.sem_inc(chain, -1)
            dve.sem_inc(S["weights_ready"], 1)
            dve.sem_inc(S["xt_free"], 1)

            def make_x(n):
                d, t = STEPS[n]
                dve.wait_ge(S["tanh_x_ready"], 1)
                dve.sem_inc(S["tanh_x_ready"], -1)
                nc.vector.scalar_tensor_tensor(out=xbc[d][:], in0=tanh_x[:], scalar=1.0, in1=ps_x[:, 0:CONV],
                                                         op0=ALU.add, op1=ALU.mult).then_inc(chain, 1)
                dve.wait_ge(chain, 1)
                dve.sem_inc(chain, -1)
                dve.sem_inc(S["bc_ready"], 1)
                nc.vector.tensor_tensor(heads(xdt[d][:]), heads(xbc[d][:, 0:DI]), per_head(dt[:, d, t, :]), ALU.mult).then_inc(chain, 1)
                dve.wait_ge(chain, 1)
                dve.sem_inc(chain, -1)
                dve.sem_inc(S["xdt_ready"], 1)

            def make_z(n):
                dve.wait_ge(S["tanh_z_ready"], 1)
                dve.sem_inc(S["tanh_z_ready"], -1)
                nc.vector.scalar_tensor_tensor(out=gate_z[STEPS[n][0]][:], in0=tanh_z[:], scalar=1.0, in1=ps_z[:, 0:DI],
                                                         op0=ALU.add, op1=ALU.mult).then_inc(chain, 1)
                dve.wait_ge(chain, 1)
                dve.sem_inc(chain, -1)
                dve.sem_inc(S["z_free"], 1)

            for place in first_places:
                more.vector(dve, *place)
            dve.wait_ge(S["x_loaded"], 16 * LOADS)
            dve.sem_inc(S["x_loaded"], -16 * LOADS)
            token_norm_vector(nc, dve, xt, hidden[0], stats, mv, rstd, 1e-5, chain, S["var_ready"], S["std_ready"])
            for d in range(2):
                ins = nc.vector.memset(state[d][:], 0.0)
            ins.then_inc(chain, 1)
            dve.wait_ge(chain, 1)
            dve.sem_inc(chain, -1)
            dve.sem_inc(S["normed"], 1)
            dve.wait_ge(S["dt_ready"], 1)
            dve.sem_inc(S["dt_ready"], -1)
            raw = ps_seg[:, 0:T * 2 * NH].rearrange("p (t d h) -> p d t h", d=2, h=NH)
            bias = b_dt[:].rearrange("p (d h) -> p d h", d=2).unsqueeze(2).to_broadcast([P, 2, T, NH])
            for d in range(2):
                ins = nc.vector.tensor_tensor(dt[:, d], raw[:, d], bias[:, d], ALU.add)
            ins.then_inc(chain, 1)
            dve.wait_ge(chain, 1)
            dve.sem_inc(chain, -1)
            flat = [v[:].rearrange("p d t h -> p (d t h)") for v in (dt, soft, dA)]
            nc.vector.scalar_tensor_tensor(out=flat[1], in0=flat[0], scalar=-1.0, in1=flat[0],
                                                     op0=ALU.mult, op1=ALU.max).then_inc(chain, 1)
            dve.wait_ge(chain, 1)
            dve.sem_inc(chain, -1)
            dve.sem_inc(S["abs_ready"], 1)
            dve.wait_ge(S["soft_ready"], 1)
            dve.sem_inc(S["soft_ready"], -1)
            nc.vector.scalar_tensor_tensor(out=flat[0], in0=flat[0], scalar=0.0, in1=flat[1],
                                                     op0=ALU.max, op1=ALU.add).then_inc(chain, 1)
            dve.wait_ge(chain, 1)
            dve.sem_inc(chain, -1)
            a = a_log[:].rearrange("p (d h) -> p d h", d=2)
            for d in range(2):
                ins = nc.vector.tensor_tensor(dA[:, d], dt[:, d], a[:, d:d + 1, :].to_broadcast([P, T, NH]), ALU.mult)
            ins.then_inc(chain, 1)
            dve.wait_ge(chain, 1)
            dve.sem_inc(chain, -1)
            dve.sem_inc(S["dA_ready"], 1)
            nc.vector.tensor_scalar(flat[0], flat[0], 0.5, None, ALU.mult).then_inc(chain, 1)
            dve.wait_ge(chain, 1)
            dve.sem_inc(chain, -1)
            dve.wait_ge(S["decay_ready"], 1)
            dve.sem_inc(S["decay_ready"], -1)
            for d in range(2):
                v = decay[:, d, 0:2].rearrange("p k t h -> p (k t h)")
                ins = nc.vector.tensor_scalar(v, v, 0.5, None, ALU.mult)
            ins.then_inc(chain, 1)
            dve.wait_ge(chain, 1)
            dve.sem_inc(chain, -1)
            dve.sem_inc(S["scan_go_pe"], 1)
            dve.sem_inc(S["scan_go_pool"], 1)
            dve.sem_inc(S["z_free"], 1)
            make_x(0)
            make_z(0)
            for n, (d, t) in enumerate(STEPS):
                dve.wait_ge(S["cb_ready"], 1)
                dve.sem_inc(S["cb_ready"], -1)
                nc.vector.tensor_tensor(cb[:], ps_bc[:, 2 * P:3 * P], quarter[:, d, :], ALU.mult).then_inc(chain, 1)
                dve.wait_ge(chain, 1)
                dve.sem_inc(chain, -1)
                dve.sem_inc(S["cbm_ready"], 1)
                if n < 2 * T - 1:
                    make_x(n + 1)
                    make_z(n + 1)
                for place in beside[n]:
                    more.vector(dve, *place)
                dve.wait_ge(S["y_ready"], 1)
                dve.sem_inc(S["y_ready"], -1)
                nc.vector.tensor_tensor(heads(y[:]), heads(ps_y[:, DI:2 * DI]), per_head(decay[:, d, 0, t, :]), ALU.mult).then_inc(chain, 1)
                dve.wait_ge(chain, 1)
                dve.sem_inc(chain, -1)
                nc.vector.tensor_tensor(y[:], y[:], ps_y[:, 0:DI], ALU.add).then_inc(chain, 1)
                dve.wait_ge(chain, 1)
                dve.sem_inc(chain, -1)
                dve.wait_ge(S["xd_ready"], 1)
                dve.sem_inc(S["xd_ready"], -1)
                nc.vector.tensor_tensor(y[:], y[:], xD[d][:], ALU.add).then_inc(chain, 1)
                dve.wait_ge(chain, 1)
                dve.sem_inc(chain, -1)
                nc.vector.tensor_tensor(y[:], y[:], gate_z[d][:], ALU.mult).then_inc(chain, 1)
                dve.wait_ge(chain, 1)
                dve.sem_inc(chain, -1)
                dve.sem_inc(S["yg_ready"], 1)
                dve.sem_inc(S["yg_ready_act"], 1)
                nc.vector.tensor_tensor(heads(state[d][:]), heads(state[d][:]), per_head(decay[0:DS, d, 2, t, :], DS), ALU.mult).then_inc(chain, 1)
                dve.wait_ge(chain, 1)
                dve.sem_inc(chain, -1)
                nc.vector.tensor_tensor(state[d][:], state[d][:], ps_s[0:DS, 0:DI], ALU.add).then_inc(chain, 1)
                dve.wait_ge(chain, 1)
                dve.sem_inc(chain, -1)
            dve.wait_ge(S["z_free"], 1)
            dve.sem_inc(S["z_free"], -1)
            dve.wait_ge(S["batch_done"], 1)
            dve.sem_inc(S["batch_done"], -1)
            nc.vector.tensor_scalar(rms[:], squares[:], 1.0 / DI, 4e-5, ALU.mult, ALU.add).then_inc(chain, 1)
            dve.wait_ge(chain, 1)
            dve.sem_inc(chain, -1)
            nc.vector.reciprocal(rms[:], rms[:]).then_inc(chain, 1)
            dve.wait_ge(chain, 1)
            dve.sem_inc(chain, -1)
            dve.sem_inc(S["rms_in"], 1)
            dve.wait_ge(S["rms_out"], 1)
            dve.sem_inc(S["rms_out"], -1)
            for d in range(2):
                for t in range(T):
                    ins = nc.vector.scalar_tensor_tensor(out=xt[:, t, :], in0=hidden[d][:, t, :], scalar=rms[:, d, t:t + 1],
                                                         in1=xt[:, t, :], op0=ALU.mult, op1=ALU.add)
                ins.then_inc(chain, 1)
                dve.wait_ge(chain, 1)
                dve.sem_inc(chain, -1)
            dve.sem_inc(S["result_ready"], 1)


def layer2_mamba_inputs(i):
    dirs = [{k[len(f"L2_attn_{d}_"):]: v for k, v in i.items() if k.startswith(f"L2_attn_{d}_")} for d in ("fwd", "bwd")]
    both = lambda name, f: np.stack([f(d[name]) for d in dirs], 1)
    rows = lambda a: np.broadcast_to(a.reshape(1, -1), (P, a.size))
    return {
        "conv_w": np.broadcast_to(np.stack([d["conv_w"].T for d in dirs])[None], (P, 2, KC, CONV)),
        "w_xbc": both("in_proj", lambda a: a[:, DI:DI + CONV]), "w_z": both("in_proj", lambda a: a[:, :DI]),
        "w_dt": both("in_proj", lambda a: a[:, DI + CONV:]).reshape(C, 2 * NH),
        "conv_b": np.stack([d["conv_b"] for d in dirs])[None], "dt_bias": rows(np.stack([d["dt_bias"] for d in dirs])),
        "A_log": rows(np.stack([d["A_log"] for d in dirs])), "D": rows(np.stack([d["D"] for d in dirs])),
        "w_out": both("out_proj", lambda a: a.reshape(2, P, C).transpose(1, 0, 2)),
        "norm_w": both("norm_w", lambda a: a.reshape(2, P).T),
    }

def store_tokens(engine, dst, src, b, stored):
    h = T // LOADS
    for n in range(LOADS):
        tokens = dst[bass.ds(b, 1), n * h * P:(n + 1) * h * P, :].rearrange("a (t p) c -> p (a t) c", p=P)
        engine.dma_start(tokens, src[:, n * h:(n + 1) * h, :]).then_inc(stored, 16)


NE = 8


def layer2_experts(nc, x, out, w, b, mark, more):
    with ExitStack() as stack:
        s = Scope(nc, "l2f" + mark, stack)
        ident, w_r, b_r = s.sb("ident", [P, P]), s.sb("w_r", [P, NE]), s.sb("b_r", [P, NE])
        w_e, b_e, order = s.sb("w_e", [P, NE * C]), s.sb("b_e", [NE, C]), s.sb("order", [P, NE])
        xt, xn, xT = s.sb("xt", [P, T, C]), s.sb("xn", [P, T, C]), s.sb("xT", [P, N])
        stats, mv, rstd = s.sb("stats", [P, T, 6]), s.sb("mv", [P, T, 2]), s.sb("rstd", [P, T])
        prob, pick, first, gates = (s.sb(n, [P, T, NE]) for n in ("prob", "pick", "first", "gates"))
        top = s.sb("top", [P, T])
        gT, other = s.sb("gT", [NE, N]), s.sb("other", [P, C])
        experts = [[s.ps(f"experts{n}{k}") for k in range(2)] for n in range(2)]
        ps_bias, ps_r, ps_t = s.ps("ps_bias"), s.ps("ps_r"), [s.ps(f"ps_t{n}") for n in range(1)]
        ps_tr = [ps_t[0], ps_bias]
        names = ("consts x_loaded xt_free var_ready std_ready normed tr_ready tr_free logits_ready exp_in exp_out gates_ready gT_ready gT_free "
                 "gT_done experts_ready stored result_ready dve_chain act_chain").split()
        S = {n: s.sem(n) for n in names}
        experts_free = [s.sem(f"experts_free{n}") for n in range(2)]
        bias_free = s.sem("bias_free")
        first_places, *beside = more.share(T / 2, *[1] * T)
        loads = [(ident, "ident"), (w_r, "w_r"), (b_r, "b_r"), (w_e, "w_e"), (b_e, "b_e"), (order, "order")]
        NC = 16 * len(loads)
        block = s.block()

        @block.sync
        def _(sp):
            for dst, name in loads:
                sp.dma_start(dst[:], w[name]).then_inc(S["consts"], 16)
            sp.wait_ge(S["xt_free"], 1)
            sp.sem_inc(S["xt_free"], -1)
            load_tokens(sp, xt, x, b, S["x_loaded"])
            for here in (first_places, *beside):
                for place in here:
                    more.sync(sp, *place)
            sp.wait_ge(S["result_ready"], 1)
            sp.sem_inc(S["result_ready"], -1)
            store_tokens(sp, out, xt, b, S["stored"])
            sp.wait_ge(S["stored"], 16 * LOADS)
            sp.sem_inc(S["stored"], -16 * LOADS)
            sp.sem_inc(S["xt_free"], 1)

        @block.tensor
        def _(pe):
            pe.wait_ge(S["consts"], NC)
            for place in first_places:
                more.tensor(pe, *place)
            pe.wait_ge(S["normed"], 1)
            pe.sem_inc(S["normed"], -1)
            for n in range(NB):
                pe.wait_ge(S["tr_free"], 1)
                pe.sem_inc(S["tr_free"], -1)
                for k in range(4):
                    ins = nc.tensor.transpose(ps_tr[n % 2][:, k * P:(k + 1) * P], xn[:, 4 * n + k, :], ident[:])
                ins.then_inc(S["tr_ready"], 1)
            pe.wait_ge(S["tr_free"], 2)
            pe.sem_inc(S["tr_free"], -2)
            for t in range(T):
                ins = nc.tensor.matmul(ps_r[:, t * NE:(t + 1) * NE], xT[:, t * P:(t + 1) * P], w_r[:], start=True, stop=True)
            ins.then_inc(S["logits_ready"], 1)

            def products(t):
                pe.wait_ge(experts_free[t % 2], 1)
                pe.sem_inc(experts_free[t % 2], -1)
                for k in range(2):
                    ins = nc.tensor.matmul(experts[t % 2][k][:], xT[:, t * P:(t + 1) * P], w_e[:, k * BANK:(k + 1) * BANK],
                                           start=True, stop=True)
                return ins

            products(0)
            products(1)
            pe.wait_ge(S["gates_ready"], 1)
            pe.sem_inc(S["gates_ready"], -1)
            for n in range(NB):
                pe.wait_ge(S["gT_free"], 1)
                pe.sem_inc(S["gT_free"], -1)
                for k in range(4):
                    ins = nc.tensor.transpose(ps_tr[n % 2][0:NE, k * P:(k + 1) * P], gates[:, 4 * n + k, :], ident[:])
                ins.then_inc(S["gT_ready"], 1)
            pe.wait_ge(S["gT_free"], 2)
            pe.sem_inc(S["gT_free"], -2)
            pe.sem_inc(S["gT_done"], 1)
            for t in range(T):
                if t >= 2:
                    products(t)
                pe.wait_ge(bias_free, 1)
                pe.sem_inc(bias_free, -1)
                nc.tensor.matmul(ps_bias[:, 0:C], gT[:, t * P:(t + 1) * P], b_e[:], start=True, stop=True
                                 ).then_inc(S["experts_ready"], 1)
                for place in beside[t]:
                    more.tensor(pe, *place)

        @block.scalar
        def _(act):
            act.wait_ge(S["consts"], NC)
            for place in first_places:
                more.scalar(act, *place)
            act.wait_ge(S["var_ready"], 1)
            act.sem_inc(S["var_ready"], -1)
            nc.scalar.activation(rstd[:], rstd[:], ACT.Sqrt).then_inc(S["std_ready"], 1)
            act.sem_inc(S["tr_free"], 2)
            for n in range(NB):
                act.wait_ge(S["tr_ready"], 1)
                act.sem_inc(S["tr_ready"], -1)
                nc.scalar.copy(xT[:, n * BANK:(n + 1) * BANK], ps_tr[n % 2][:]).then_inc(S["act_chain"], 1)
                act.wait_ge(S["act_chain"], 1)
                act.sem_inc(S["act_chain"], -1)
                act.sem_inc(S["tr_free"], 1)
            act.wait_ge(S["exp_in"], 1)
            act.sem_inc(S["exp_in"], -1)
            nc.scalar.activation(prob[:], prob[:], ACT.Exp).then_inc(S["exp_out"], 1)
            act.sem_inc(S["gT_free"], 2)
            for n in range(NB):
                act.wait_ge(S["gT_ready"], 1)
                act.sem_inc(S["gT_ready"], -1)
                nc.scalar.copy(gT[:, n * BANK:(n + 1) * BANK], ps_tr[n % 2][0:NE, :]).then_inc(S["act_chain"], 1)
                act.wait_ge(S["act_chain"], 1)
                act.sem_inc(S["act_chain"], -1)
                act.sem_inc(S["gT_free"], 1)
            for here in beside:
                for place in here:
                    more.scalar(act, *place)

        @block.gpsimd
        def _(pool):
            for here in (first_places, *beside):
                for place in here:
                    for third in range(3):
                        more.pool(pool, *place, third)

        @block.vector
        def _(dve):
            chain = S["dve_chain"]
            dve.wait_ge(S["consts"], NC)
            dve.sem_inc(S["xt_free"], 1)
            for n in range(2):
                dve.sem_inc(experts_free[n], 1)
            dve.sem_inc(bias_free, 1)

            def by_token(ap):
                return ap.unsqueeze(2).to_broadcast([P, T, NE])

            def one_hot(dst, scores):
                nc.vector.tensor_reduce(top[:], scores, AX.X, ALU.max).then_inc(chain, 1)
                dve.wait_ge(chain, 1)
                dve.sem_inc(chain, -1)
                nc.vector.tensor_tensor(dst, scores, by_token(top[:]), ALU.is_equal).then_inc(chain, 1)
                dve.wait_ge(chain, 1)
                dve.sem_inc(chain, -1)
                nc.vector.tensor_tensor(dst, dst, order[:].unsqueeze(1).to_broadcast([P, T, NE]), ALU.mult).then_inc(chain, 1)
                dve.wait_ge(chain, 1)
                dve.sem_inc(chain, -1)
                nc.vector.tensor_reduce(top[:], dst, AX.X, ALU.max).then_inc(chain, 1)
                dve.wait_ge(chain, 1)
                dve.sem_inc(chain, -1)
                nc.vector.tensor_tensor(dst, dst, by_token(top[:]), ALU.is_equal).then_inc(chain, 1)
                dve.wait_ge(chain, 1)
                dve.sem_inc(chain, -1)

            for place in first_places:
                more.vector(dve, *place)
            dve.wait_ge(S["x_loaded"], 16 * LOADS)
            dve.sem_inc(S["x_loaded"], -16 * LOADS)
            token_norm_vector(nc, dve, xt, xn, stats, mv, rstd, 1e-5, chain, S["var_ready"], S["std_ready"])
            dve.sem_inc(S["normed"], 1)
            dve.wait_ge(S["logits_ready"], 1)
            dve.sem_inc(S["logits_ready"], -1)
            logits = ps_r[:, 0:T * NE].rearrange("p (t e) -> p t e", e=NE)
            nc.vector.tensor_tensor(prob[:], logits, b_r[:].unsqueeze(1).to_broadcast([P, T, NE]), ALU.add).then_inc(chain, 1)
            dve.wait_ge(chain, 1)
            dve.sem_inc(chain, -1)
            nc.vector.tensor_reduce(top[:], prob[:], AX.X, ALU.max).then_inc(chain, 1)
            dve.wait_ge(chain, 1)
            dve.sem_inc(chain, -1)
            nc.vector.tensor_tensor(prob[:], prob[:], by_token(top[:]), ALU.subtract).then_inc(chain, 1)
            dve.wait_ge(chain, 1)
            dve.sem_inc(chain, -1)
            dve.sem_inc(S["exp_in"], 1)
            dve.wait_ge(S["exp_out"], 1)
            dve.sem_inc(S["exp_out"], -1)
            nc.vector.tensor_reduce(top[:], prob[:], AX.X, ALU.add).then_inc(chain, 1)
            dve.wait_ge(chain, 1)
            dve.sem_inc(chain, -1)
            nc.vector.reciprocal(top[:], top[:]).then_inc(chain, 1)
            dve.wait_ge(chain, 1)
            dve.sem_inc(chain, -1)
            nc.vector.tensor_tensor(prob[:], prob[:], by_token(top[:]), ALU.mult).then_inc(chain, 1)
            dve.wait_ge(chain, 1)
            dve.sem_inc(chain, -1)
            one_hot(first[:], prob[:])
            nc.vector.scalar_tensor_tensor(out=pick[:], in0=first[:], scalar=-2.0, in1=prob[:],
                                                     op0=ALU.mult, op1=ALU.add).then_inc(chain, 1)
            dve.wait_ge(chain, 1)
            dve.sem_inc(chain, -1)
            one_hot(gates[:], pick[:])
            nc.vector.tensor_tensor(gates[:], gates[:], first[:], ALU.add).then_inc(chain, 1)
            dve.wait_ge(chain, 1)
            dve.sem_inc(chain, -1)
            nc.vector.tensor_tensor(gates[:], gates[:], prob[:], ALU.mult).then_inc(chain, 1)
            dve.wait_ge(chain, 1)
            dve.sem_inc(chain, -1)
            nc.vector.tensor_reduce(top[:], gates[:], AX.X, ALU.add).then_inc(chain, 1)
            dve.wait_ge(chain, 1)
            dve.sem_inc(chain, -1)
            nc.vector.reciprocal(top[:], top[:]).then_inc(chain, 1)
            dve.wait_ge(chain, 1)
            dve.sem_inc(chain, -1)
            nc.vector.tensor_tensor(gates[:], gates[:], by_token(top[:]), ALU.mult).then_inc(chain, 1)
            dve.wait_ge(chain, 1)
            dve.sem_inc(chain, -1)
            dve.sem_inc(S["gates_ready"], 1)
            dve.wait_ge(S["gT_done"], 1)
            dve.sem_inc(S["gT_done"], -1)
            for t in range(T):
                dve.wait_ge(S["experts_ready"], 1)
                dve.sem_inc(S["experts_ready"], -1)
                nc.vector.tensor_tensor(xt[:, t, :], xt[:, t, :], ps_bias[:, 0:C], ALU.add)
                for e in range(NE // 2):
                    product, g = experts[t % 2][1][:, e * C:(e + 1) * C], gates[:, t, NE // 2 + e:NE // 2 + e + 1]
                    if e == 0:
                        nc.vector.tensor_scalar(other[:], product, g, None, ALU.mult).then_inc(chain, 1)
                        dve.wait_ge(chain, 1)
                        dve.sem_inc(chain, -1)
                        dve.sem_inc(bias_free, 1)
                    else:
                        nc.vector.scalar_tensor_tensor(out=other[:], in0=product, scalar=g, in1=other[:],
                                                                 op0=ALU.mult, op1=ALU.add).then_inc(chain, 1)
                        dve.wait_ge(chain, 1)
                        dve.sem_inc(chain, -1)
                    ins = nc.vector.scalar_tensor_tensor(out=xt[:, t, :], in0=experts[t % 2][0][:, e * C:(e + 1) * C],
                                                         scalar=gates[:, t, e:e + 1], in1=xt[:, t, :], op0=ALU.mult, op1=ALU.add)
                ins.then_inc(chain, 1)
                dve.wait_ge(chain, 1)
                dve.sem_inc(chain, -1)
                dve.sem_inc(experts_free[t % 2], 1)
                nc.vector.tensor_tensor(xt[:, t, :], xt[:, t, :], other[:], ALU.add).then_inc(chain, 1)
                dve.wait_ge(chain, 1)
                dve.sem_inc(chain, -1)
                for place in beside[t]:
                    more.vector(dve, *place)
            dve.sem_inc(S["result_ready"], 1)


def layer2_experts_inputs(i):
    return {
        "w_r": i["L2_ffn_router_w"], "b_r": np.broadcast_to(i["L2_ffn_router_b"], (P, NE)),
        "w_e": i["L2_ffn_expert_w"].transpose(1, 0, 2).reshape(C, NE * C), "b_e": i["L2_ffn_expert_b"],
        "order": np.broadcast_to(np.arange(NE, 0, -1, dtype=np.float32), (P, NE)),
    }


def layer3_attention(nc, x, out, w, b, mark, more):
    AHEAD = 2
    UNROLL = 4
    LOOPS = NB // UNROLL
    lead = 2 if more.count else 0
    first, count = more.tile, (more.count - lead) // LOOPS
    more.tiles(first, lead)
    [first_places] = more.share(1)
    more.tiles(first + lead, count)
    beside = more.share(*[1] * (UNROLL * T))
    with ExitStack() as stack:
        s = Scope(nc, "l3a" + mark, stack)
        ident = s.sb("ident", [P, P])
        shift = s.sb("shift", [P, 1])
        xt, xn, xT = s.sb("xt", [P, T, C]), s.sb("xn", [P, T, C]), s.sb("xT", [P, N])
        stats, mv, rstd = s.sb("stats", [P, T, 6]), s.sb("mv", [P, T, 2]), s.sb("rstd", [P, T])
        E = [s.sb(f"E{n}", [P, BANK]) for n in range(4)]
        sums, total, oT = s.sb("sums", [P, NB, T]), s.sb("total", [P, T]), s.sb("oT", [P, N])
        ps_s, ps_o = [s.ps(f"ps_s{n}") for n in range(4)], s.ps("ps_o")
        ps_t = [s.ps(f"ps_t{n}") for n in range(2)]
        names = ("consts x_loaded xt_free var_ready std_ready normed tr_ready tr_free s_ready s_free e_ready o_ready o_free oT_done "
                 "back_ready stored result_ready dve_chain act_chain sums_ready shift_ready").split()
        S = {n: s.sem(n) for n in names}
        back_free = s.sem("back_free")
        block = s.block()

        @block.sync
        def _(sp):
            sp.dma_start(ident[:], w["ident"]).then_inc(S["consts"], 16)
            sp.wait_ge(S["xt_free"], 1)
            sp.sem_inc(S["xt_free"], -1)
            load_tokens(sp, xt, x, b, S["x_loaded"])
            if count:
                more.tiles(first, lead)
                for place in first_places:
                    more.sync(sp, *place)
                with sp.Fori(0, LOOPS) as i:
                    more.tiles(first + lead + i * count, count)
                    for here in beside:
                        for place in here:
                            more.sync(sp, *place)
                more.tiles(first + lead + LOOPS * count, count)
                more.sync_finish(sp, -1)
            sp.wait_ge(S["result_ready"], 1)
            sp.sem_inc(S["result_ready"], -1)
            store_tokens(sp, out, xt, b, S["stored"])
            sp.wait_ge(S["stored"], 16 * LOADS)
            sp.sem_inc(S["stored"], -16 * LOADS)
            sp.sem_inc(S["xt_free"], 1)

        @block.tensor
        def _(pe):
            pe.wait_ge(S["consts"], 16)
            for place in first_places:
                more.tensor(pe, *place)
            pe.wait_ge(S["normed"], 1)
            pe.sem_inc(S["normed"], -1)
            for n in range(NB):
                pe.wait_ge(S["tr_free"], 1)
                pe.sem_inc(S["tr_free"], -1)
                for k in range(4):
                    ins = nc.tensor.transpose(ps_t[n % 2][:, k * P:(k + 1) * P], xn[:, 4 * n + k, :], ident[:])
                ins.then_inc(S["tr_ready"], 1)
            pe.wait_ge(S["tr_free"], 2)
            pe.sem_inc(S["tr_free"], -2)
            with pe.Fori(0, LOOPS) as i:
                def scores(u, m):
                    pe.wait_ge(S["s_free"], 1)
                    pe.sem_inc(S["s_free"], -1)
                    nc.tensor.matmul(ps_s[m % 4][:], xT[:, m * P:(m + 1) * P], xT[:, bass.ds(i * (UNROLL * BANK) + u * BANK, BANK)],
                                     start=True, stop=True).then_inc(S["s_ready"], 1)

                for m in range(AHEAD):
                    scores(0, m)
                for u in range(UNROLL):
                    pe.wait_ge(S["o_free"], 1)
                    pe.sem_inc(S["o_free"], -1)
                    for m in range(T):
                        if u * T + m + AHEAD < UNROLL * T:
                            scores(u + (m + AHEAD) // T, (m + AHEAD) % T)
                        pe.wait_ge(S["e_ready"], 1)
                        pe.sem_inc(S["e_ready"], -1)
                        ins = nc.tensor.matmul(ps_o[:], xn[:, m, :], E[m % 4][:], start=(m == 0), stop=(m == T - 1))
                        if m == T - 1:
                            ins.then_inc(S["o_ready"], 1)
                        for place in beside[u * T + m]:
                            more.tensor(pe, *place)
            if count:
                more.tensor_finish(pe)
            pe.wait_ge(S["oT_done"], 1)
            pe.sem_inc(S["oT_done"], -1)
            for n in range(NB):
                pe.wait_ge(back_free, 1)
                pe.sem_inc(back_free, -1)
                for k in range(4):
                    t = 4 * n + k
                    ins = nc.tensor.transpose(ps_t[n % 2][:, k * P:(k + 1) * P], oT[:, t * P:(t + 1) * P], ident[:])
                ins.then_inc(S["back_ready"], 1)

        @block.scalar
        def _(act):
            act.sem_inc(S["s_free"], 4)
            act.sem_inc(S["o_free"], 1)
            act.wait_ge(S["shift_ready"], 1)
            for place in first_places:
                more.scalar(act, *place)
            act.wait_ge(S["var_ready"], 1)
            act.sem_inc(S["var_ready"], -1)
            nc.scalar.activation(rstd[:], rstd[:], ACT.Sqrt).then_inc(S["std_ready"], 1)
            act.sem_inc(S["tr_free"], 2)
            for n in range(NB):
                act.wait_ge(S["tr_ready"], 1)
                act.sem_inc(S["tr_ready"], -1)
                nc.scalar.copy(xT[:, n * BANK:(n + 1) * BANK], ps_t[n % 2][:]).then_inc(S["act_chain"], 1)
                act.wait_ge(S["act_chain"], 1)
                act.sem_inc(S["act_chain"], -1)
                act.sem_inc(S["tr_free"], 1)
            with act.Fori(0, LOOPS) as i:
                for u in range(UNROLL):
                    n = i * UNROLL + u
                    for m in range(T):
                        act.wait_ge(S["s_ready"], 1)
                        act.sem_inc(S["s_ready"], -1)
                        row_sum = sums[:, bass.ds(n, 1), m:m + 1].rearrange("p a c -> p (a c)")
                        nc.scalar.activation(E[m % 4][:], ps_s[m % 4][:], ACT.Exp, bias=shift[:], accum_out=row_sum).then_inc(S["act_chain"], 1)
                        act.wait_ge(S["act_chain"], 1)
                        act.sem_inc(S["act_chain"], -1)
                        act.sem_inc(S["s_free"], 1)
                        act.sem_inc(S["e_ready"], 1)
                        for place in beside[u * T + m]:
                            more.scalar(act, *place)
                    act.wait_ge(S["o_ready"], 1)
                    act.sem_inc(S["o_ready"], -1)
                    nc.scalar.copy(oT[:, bass.ds(n * BANK, BANK)], ps_o[:]).then_inc(S["act_chain"], 1)
                    act.wait_ge(S["act_chain"], 1)
                    act.sem_inc(S["act_chain"], -1)
                    act.sem_inc(S["o_free"], 1)
            if count:
                more.scalar_finish(act)
            act.sem_inc(S["oT_done"], 1)
            act.sem_inc(S["sums_ready"], 1)

        @block.gpsimd
        def _(pool):
            if count:
                for place in first_places:
                    for third in range(3):
                        more.pool(pool, *place, third)
                with pool.Fori(0, LOOPS) as i:
                    for here in beside:
                        for place in here:
                            for third in range(3):
                                more.pool(pool, *place, third)

        @block.vector
        def _(dve):
            chain = S["dve_chain"]
            nc.vector.memset(shift[:], -C / 2.0).then_inc(S["shift_ready"], 1)
            dve.sem_inc(S["xt_free"], 1)
            dve.sem_inc(back_free, 2)
            more.tiles(first, lead)
            for place in first_places:
                more.vector(dve, *place)
            dve.wait_ge(S["x_loaded"], 16 * LOADS)
            dve.sem_inc(S["x_loaded"], -16 * LOADS)
            token_norm_vector(nc, dve, xt, xn, stats, mv, rstd, 1e-5, chain, S["var_ready"], S["std_ready"])
            dve.sem_inc(S["normed"], 1)
            if count:
                with dve.Fori(0, LOOPS) as i:
                    more.tiles(first + lead + i * count, count)
                    for here in beside:
                        for place in here:
                            more.vector(dve, *place)
                more.vector_finish(dve)
            dve.wait_ge(S["sums_ready"], 1)
            dve.sem_inc(S["sums_ready"], -1)
            nc.vector.tensor_reduce(total[:], sums[:].rearrange("p n t -> p t n"), AX.X, ALU.add).then_inc(chain, 1)
            dve.wait_ge(chain, 1)
            dve.sem_inc(chain, -1)
            nc.vector.reciprocal(total[:], total[:]).then_inc(chain, 1)
            dve.wait_ge(chain, 1)
            dve.sem_inc(chain, -1)
            for n in range(NB):
                dve.wait_ge(S["back_ready"], 1)
                dve.sem_inc(S["back_ready"], -1)
                for t in range(4 * n, 4 * n + 4):
                    ins = nc.vector.scalar_tensor_tensor(out=xt[:, t, :], in0=ps_t[n % 2][:, t % 4 * P:(t % 4 + 1) * P],
                                                         scalar=total[:, t:t + 1], in1=xt[:, t, :], op0=ALU.mult, op1=ALU.add)
                ins.then_inc(chain, 1)
                dve.wait_ge(chain, 1)
                dve.sem_inc(chain, -1)
                dve.sem_inc(back_free, 1)
            dve.sem_inc(S["result_ready"], 1)


EX, HID = 64, 512
KH = HID // P


def layer3_experts(nc, x, out, chosen, w):
    with ExitStack() as outer:
        so = Scope(nc, "l3f", outer)
        pooled = so.sb("pooled", [P, B, EX])
        rows = so.sb("rows", [EX, B, C])
        ident = so.sb("ident", [P, P])
        with ExitStack() as stack:
            s = Scope(nc, "l3g", stack)
            gate_w, gate_b = s.sb("gate_w", [P, EX]), s.sb("gate_b", [EX, 1])
            xt, xn, xT = s.sb("xt", [P, T, C]), s.sb("xn", [P, T, C]), s.sb("xT", [P, N])
            stats, mv, rstd = s.sb("stats", [P, T, 6]), s.sb("mv", [P, T, 2]), s.sb("rstd", [P, T])
            prob, rest = s.sb("prob", [EX, N]), s.sb("rest", [EX, N])
            small, best = s.sb("small", [EX, 4]), s.sb("best", [EX, 8])
            chosen_T = s.sb("chosen_T", [P, T, EX])
            ps_t, ps_p = [s.ps(f"ps_t{n}") for n in range(2)], s.ps("ps_p")
            names = ("consts x_loaded xt_free var_ready std_ready normed tr_ready tr_free l_ready l_free logits_ready exp_in exp_out "
                     "chosen_ready chosen_store chosen_stored c_ready c_free pooled_ready pooled_done prob_free dve_chain act_chain").split()
            S = {n: s.sem(n) for n in names}
            block = s.block()

            @block.sync
            def _(sp):
                for dst, name in ((ident, "ident"), (gate_w, "gate_w"), (gate_b, "gate_b")):
                    sp.dma_start(dst[:], w[name]).then_inc(S["consts"], 16)
                with sp.Fori(0, B) as b:
                    sp.wait_ge(S["xt_free"], 1)
                    sp.sem_inc(S["xt_free"], -1)
                    load_tokens(sp, xt, x, b, S["x_loaded"])
                    sp.wait_ge(S["chosen_store"], 1)
                    sp.sem_inc(S["chosen_store"], -1)
                    sp.dma_start(chosen[bass.ds(b, 1)].rearrange("a e n -> e (a n)"), rest[:]).then_inc(S["chosen_stored"], 16)
                    sp.wait_ge(S["chosen_stored"], 16)
                    sp.sem_inc(S["chosen_stored"], -16)
                    sp.sem_inc(S["prob_free"], 1)

            @block.tensor
            def _(pe):
                pe.wait_ge(S["consts"], 48)
                with pe.Fori(0, B) as b:
                    pe.wait_ge(S["normed"], 1)
                    pe.sem_inc(S["normed"], -1)
                    for n in range(NB):
                        pe.wait_ge(S["tr_free"], 1)
                        pe.sem_inc(S["tr_free"], -1)
                        for k in range(4):
                            ins = nc.tensor.transpose(ps_t[n % 2][:, k * P:(k + 1) * P], xn[:, 4 * n + k, :], ident[:])
                        ins.then_inc(S["tr_ready"], 1)
                    pe.wait_ge(S["tr_free"], 2)
                    pe.sem_inc(S["tr_free"], -2)
                    for n in range(NB):
                        pe.wait_ge(S["l_free"], 1)
                        pe.sem_inc(S["l_free"], -1)
                        nc.tensor.matmul(ps_t[n % 2][0:EX, :], gate_w[:], xT[:, n * BANK:(n + 1) * BANK], start=True, stop=True
                                         ).then_inc(S["l_ready"], 1)
                    pe.wait_ge(S["l_free"], 2)
                    pe.sem_inc(S["l_free"], -2)
                    pe.wait_ge(S["chosen_ready"], 1)
                    pe.sem_inc(S["chosen_ready"], -1)
                    for n in range(NB // 2):
                        pe.wait_ge(S["c_free"], 1)
                        pe.sem_inc(S["c_free"], -1)
                        for k in range(8):
                            t = 8 * n + k
                            ins = nc.tensor.transpose(ps_t[n % 2][:, k * EX:(k + 1) * EX], rest[:, t * P:(t + 1) * P], ident[0:EX, 0:EX])
                        ins.then_inc(S["c_ready"], 1)
                    pe.wait_ge(S["c_free"], 2)
                    pe.sem_inc(S["c_free"], -2)
                    for t in range(T):
                        ins = nc.tensor.matmul(ps_p[:, 0:EX], xn[:, t, :], chosen_T[:, t, :], start=(t == 0), stop=(t == T - 1))
                    ins.then_inc(S["pooled_ready"], 1)

            @block.scalar
            def _(act):
                act.wait_ge(S["consts"], 48)
                chain = S["act_chain"]
                with act.Fori(0, B) as b:
                    act.wait_ge(S["var_ready"], 1)
                    act.sem_inc(S["var_ready"], -1)
                    nc.scalar.activation(rstd[:], rstd[:], ACT.Sqrt).then_inc(S["std_ready"], 1)
                    act.sem_inc(S["tr_free"], 2)
                    for n in range(NB):
                        act.wait_ge(S["tr_ready"], 1)
                        act.sem_inc(S["tr_ready"], -1)
                        nc.scalar.copy(xT[:, n * BANK:(n + 1) * BANK], ps_t[n % 2][:]).then_inc(chain, 1)
                        act.wait_ge(chain, 1)
                        act.sem_inc(chain, -1)
                        act.sem_inc(S["tr_free"], 1)
                    act.sem_inc(S["l_free"], 2)
                    for n in range(NB):
                        act.wait_ge(S["l_ready"], 1)
                        act.sem_inc(S["l_ready"], -1)
                        nc.scalar.activation(prob[:, n * BANK:(n + 1) * BANK], ps_t[n % 2][0:EX, :], ACT.Identity,
                                                       bias=gate_b[:, 0:1]).then_inc(chain, 1)
                        act.wait_ge(chain, 1)
                        act.sem_inc(chain, -1)
                        act.sem_inc(S["l_free"], 1)
                    act.sem_inc(S["logits_ready"], 1)
                    act.wait_ge(S["exp_in"], 1)
                    act.sem_inc(S["exp_in"], -1)
                    nc.scalar.activation(prob[:], prob[:], ACT.Exp, bias=small[:, 1:2], accum_out=small[:, 2:3]).then_inc(S["exp_out"], 1)
                    act.sem_inc(S["c_free"], 2)
                    for n in range(NB // 2):
                        act.wait_ge(S["c_ready"], 1)
                        act.sem_inc(S["c_ready"], -1)
                        nc.scalar.copy(chosen_T[:, 8 * n:8 * n + 8, :].rearrange("p t e -> p (t e)"), ps_t[n % 2][:]).then_inc(chain, 1)
                        act.wait_ge(chain, 1)
                        act.sem_inc(chain, -1)
                        act.sem_inc(S["c_free"], 1)
                    act.wait_ge(S["pooled_ready"], 1)
                    act.sem_inc(S["pooled_ready"], -1)
                    nc.scalar.copy(pooled[:, bass.ds(b, 1), :].rearrange("p a e -> p (a e)"), ps_p[:, 0:EX]).then_inc(chain, 1)
                    act.wait_ge(chain, 1)
                    act.sem_inc(chain, -1)
                    act.sem_inc(S["pooled_done"], 1)

            @block.vector
            def _(dve):
                chain = S["dve_chain"]
                dve.sem_inc(S["xt_free"], 1)
                dve.sem_inc(S["prob_free"], 1)
                with dve.Fori(0, B) as b:
                    dve.wait_ge(S["x_loaded"], 16 * LOADS)
                    dve.sem_inc(S["x_loaded"], -16 * LOADS)
                    token_norm_vector(nc, dve, xt, xn, stats, mv, rstd, 1e-5, chain, S["var_ready"], S["std_ready"])
                    dve.sem_inc(S["normed"], 1)
                    dve.sem_inc(S["xt_free"], 1)
                    dve.wait_ge(S["logits_ready"], 1)
                    dve.sem_inc(S["logits_ready"], -1)
                    nc.vector.tensor_reduce(small[:, 0:1], prob[:], AX.X, ALU.max).then_inc(chain, 1)
                    dve.wait_ge(chain, 1)
                    dve.sem_inc(chain, -1)
                    nc.vector.tensor_scalar(small[:, 1:2], small[:, 0:1], -1.0, None, ALU.mult).then_inc(chain, 1)
                    dve.wait_ge(chain, 1)
                    dve.sem_inc(chain, -1)
                    dve.sem_inc(S["exp_in"], 1)
                    dve.wait_ge(S["exp_out"], 1)
                    dve.sem_inc(S["exp_out"], -1)
                    nc.vector.reciprocal(small[:, 3:4], small[:, 2:3]).then_inc(chain, 1)
                    dve.wait_ge(chain, 1)
                    dve.sem_inc(chain, -1)
                    nc.vector.tensor_scalar(prob[:], prob[:], small[:, 3:4], None, ALU.mult).then_inc(chain, 1)
                    dve.wait_ge(chain, 1)
                    dve.sem_inc(chain, -1)
                    nc.vector.max(best[:], prob[:]).then_inc(chain, 1)
                    dve.wait_ge(chain, 1)
                    dve.sem_inc(chain, -1)
                    dve.wait_ge(S["prob_free"], 1)
                    dve.sem_inc(S["prob_free"], -1)
                    nc.vector.match_replace(rest[:], best[:], prob[:], -1.0).then_inc(chain, 1)
                    dve.wait_ge(chain, 1)
                    dve.sem_inc(chain, -1)
                    nc.vector.scalar_tensor_tensor(out=rest[:], in0=rest[:], scalar=0.0, in1=prob[:],
                                                             op0=ALU.is_lt, op1=ALU.mult).then_inc(chain, 1)
                    dve.wait_ge(chain, 1)
                    dve.sem_inc(chain, -1)
                    dve.sem_inc(S["chosen_ready"], 1)
                    dve.sem_inc(S["chosen_store"], 1)
                    dve.wait_ge(S["pooled_done"], 1)
                    dve.sem_inc(S["pooled_done"], -1)

        EG = 4
        BUFS = 4
        with ExitStack() as stack:
            s = Scope(nc, "l3m", stack)
            w1 = [s.sb(f"w1_{n}", [P, EG, HID]) for n in range(BUFS)]
            w2 = [s.sb(f"w2_{n}", [P, EG, KH, C]) for n in range(BUFS)]
            b1, b2, b1T = s.sb("b1", [EX, HID]), s.sb("b2", [EX, C]), s.sb("b1T", [P, KH, EX])
            pre = [s.sb(f"pre{n}", [P, EG, KH, B]) for n in range(2)]
            hid = [s.sb(f"hid{n}", [P, EG, KH, B]) for n in range(2)]
            oT = s.sb("oT", [P, EX, B])
            ps_b = s.ps("ps_b")
            ps_h, ps_o = [s.ps(f"ps_h{n}") for n in range(2)], [s.ps(f"ps_o{n}") for n in range(2)]
            names = ("consts bias_ready bias_done h_ready pre_ready hid_ready o_ready o_done all_done rows_ready dve_chain act_chain").split()
            S = {n: s.sem(n) for n in names}
            loaded, weights_free = [s.sem(f"loaded{n}") for n in range(BUFS)], [s.sem(f"weights_free{n}") for n in range(BUFS)]
            block = s.block()

            @block.sync
            def _(sp):
                sp.dma_start(b1[:], w["weight1"][:, C, :]).then_inc(S["consts"], 16)
                sp.dma_start(b2[:], w["weight2"][:, HID, :]).then_inc(S["consts"], 16)
                with sp.Fori(0, EX // EG // BUFS) as pair:
                    for k in range(BUFS):
                        e0 = pair * (BUFS * EG) + k * EG
                        sp.wait_ge(weights_free[k], 1)
                        sp.sem_inc(weights_free[k], -1)
                        sp.dma_start(w1[k][:], w["weight1"][bass.ds(e0, EG), 0:C, :].rearrange("e c h -> c e h")).then_inc(loaded[k], 16)
                        src = w["weight2"][bass.ds(e0, EG), 0:HID, :].rearrange("e (h k) o -> h e (k o)", k=KH)
                        sp.dma_start(w2[k][:].rearrange("h e k o -> h e (k o)"), src).then_inc(loaded[k], 16)

            @block.tensor
            def _(pe):
                for k in range(BUFS):
                    pe.sem_inc(weights_free[k], 1)
                pe.wait_ge(S["consts"], 32)
                for k in range(KH):
                    ins = nc.tensor.transpose(ps_b[:, k * EX:(k + 1) * EX], b1[:, k:HID:KH], ident[0:EX, 0:EX])
                ins.then_inc(S["bias_ready"], 1)
                def outputs(k):
                    pe.wait_ge(S["hid_ready"], 1)
                    pe.sem_inc(S["hid_ready"], -1)
                    for e in range(EG):
                        for j in range(KH):
                            ins = nc.tensor.matmul(ps_o[k % 2][:, e * B:(e + 1) * B], w2[k][:, e, j, :], hid[k % 2][:, e, j, :],
                                                   start=(j == 0), stop=(j == KH - 1))
                    ins.then_inc(S["o_ready"], 1)
                    pe.wait_ge(S["o_done"], 1)
                    pe.sem_inc(S["o_done"], -1)
                    pe.sem_inc(weights_free[k], 1)

                with pe.Fori(0, EX // EG // BUFS) as pair:
                    for k in range(BUFS):
                        pe.wait_ge(loaded[k], 32)
                        pe.sem_inc(loaded[k], -32)
                        for e in range(EG):
                            rhs = pooled[:, :, bass.ds(pair * (BUFS * EG) + k * EG + e, 1)].rearrange("p b e -> p (b e)")
                            for j in range(KH):
                                at = (e * KH + j) * B
                                ins = nc.tensor.matmul(ps_h[k % 2][:, at:at + B], w1[k][:, e, j:HID:KH], rhs, start=True, stop=True)
                        ins.then_inc(S["h_ready"], 1)
                        if k:
                            outputs(k - 1)
                    outputs(BUFS - 1)
                for b in range(B):
                    ins = nc.tensor.transpose(ps_b[0:EX, b * P:(b + 1) * P], oT[:, :, b], ident[:])
                ins.then_inc(S["all_done"], 1)

            @block.scalar
            def _(act):
                def keep_outputs(pair, k):
                    act.wait_ge(S["o_ready"], 1)
                    act.sem_inc(S["o_ready"], -1)
                    dst = oT[:, bass.ds(pair * (BUFS * EG) + k * EG, EG), :].rearrange("p e b -> p (e b)")
                    nc.scalar.copy(dst, ps_o[k % 2][:, 0:EG * B]).then_inc(S["o_done"], 1)

                with act.Fori(0, EX // EG // BUFS) as pair:
                    for k in range(BUFS):
                        act.wait_ge(S["pre_ready"], 1)
                        act.sem_inc(S["pre_ready"], -1)
                        nc.scalar.activation(hid[k % 2][:], pre[k % 2][:], ACT.Gelu).then_inc(S["hid_ready"], 1)
                        if k:
                            keep_outputs(pair, k - 1)
                    keep_outputs(pair, BUFS - 1)

            @block.vector
            def _(dve):
                chain = S["dve_chain"]
                dve.wait_ge(S["consts"], 32)
                dve.wait_ge(S["bias_ready"], 1)
                dve.sem_inc(S["bias_ready"], -1)
                nc.vector.tensor_copy(b1T[:].rearrange("p k e -> p (k e)"), ps_b[:, 0:KH * EX]).then_inc(chain, 1)
                dve.wait_ge(chain, 1)
                dve.sem_inc(chain, -1)
                with dve.Fori(0, EX // EG // BUFS) as pair:
                    for k in range(BUFS):
                        dve.wait_ge(S["h_ready"], 1)
                        dve.sem_inc(S["h_ready"], -1)
                        for j in range(KH):
                            bias = b1T[:, j, bass.ds(pair * (BUFS * EG) + k * EG, EG)].unsqueeze(2).to_broadcast([P, EG, B])
                            src = ps_h[k % 2][:, 0:EG * KH * B].rearrange("p (e j b) -> p e j b", e=EG, j=KH)[:, :, j, :]
                            ins = nc.vector.tensor_tensor(pre[k % 2][:, :, j, :], src, bias, ALU.add)
                        ins.then_inc(S["pre_ready"], 1)
                dve.wait_ge(S["all_done"], 1)
                dve.sem_inc(S["all_done"], -1)
                bias = b2[:].unsqueeze(1).to_broadcast([EX, B, C])
                nc.vector.tensor_tensor(rows[:], ps_b[0:EX, 0:B * C].rearrange("p (b o) -> p b o", b=B), bias, ALU.add).then_inc(chain, 1)
                dve.wait_ge(chain, 1)
                dve.sem_inc(chain, -1)

        with ExitStack() as stack:
            s = Scope(nc, "l3s", stack)
            xt, pick = [s.sb(f"xt{n}", [P, T, C]) for n in range(2)], [s.sb(f"pick{n}", [EX, N]) for n in range(2)]
            ps = [s.ps(f"ps{n}") for n in range(4)]
            names = "ps_ready ps_free stored dve_chain".split()
            S = {n: s.sem(n) for n in names}
            loaded, ready, free = ([s.sem(f"{m}{n}") for n in range(2)] for m in ("loaded", "ready", "free"))
            block = s.block()
            pairs = B // 2

            @block.sync
            def _(sp):
                with sp.Fori(0, pairs) as pair:
                    for k in range(2):
                        b = pair * 2 + k
                        sp.wait_ge(free[k], 1)
                        sp.sem_inc(free[k], -1)
                        sp.dma_start(pick[k][:], chosen[bass.ds(b, 1)].rearrange("a e n -> e (a n)")).then_inc(loaded[k], 16)
                        load_tokens(sp, xt[k], x, b, loaded[k])

            @block.gpsimd
            def _(pool):
                pass

            @block.scalar
            def _(act):
                for k in range(2):
                    act.sem_inc(free[k], 1)
                with act.Fori(0, pairs) as pair:
                    for k in range(2):
                        act.wait_ge(ready[k], 1)
                        act.sem_inc(ready[k], -1)
                        store_tokens(act, out, xt[k], pair * 2 + k, S["stored"])
                        act.wait_ge(S["stored"], 16 * LOADS)
                        act.sem_inc(S["stored"], -16 * LOADS)
                        act.sem_inc(free[k], 1)

            @block.tensor
            def _(pe):
                with pe.Fori(0, pairs) as pair:
                    for k in range(2):
                        pe.wait_ge(loaded[k], 16 * (1 + LOADS))
                        pe.sem_inc(loaded[k], -16 * (1 + LOADS))
                        for n in range(NB):
                            pe.wait_ge(S["ps_free"], 1)
                            pe.sem_inc(S["ps_free"], -1)
                            rhs = rows[:, bass.ds(pair * 2 + k, 1), :].rearrange("p a o -> p (a o)")
                            for t in range(4 * n, 4 * n + 4):
                                ins = nc.tensor.matmul(ps[n % 4][:, t % 4 * P:(t % 4 + 1) * P], pick[k][:, t * P:(t + 1) * P], rhs,
                                                       start=True, stop=True)
                            ins.then_inc(S["ps_ready"], 1)

            @block.vector
            def _(dve):
                dve.sem_inc(S["ps_free"], 4)
                with dve.Fori(0, pairs) as pair:
                    for k in range(2):
                        for n in range(NB):
                            dve.wait_ge(S["ps_ready"], 1)
                            dve.sem_inc(S["ps_ready"], -1)
                            tokens = xt[k][:, 4 * n:4 * n + 4, :].rearrange("p t c -> p (t c)")
                            nc.vector.tensor_tensor(tokens, tokens, ps[n % 4][:], ALU.add).then_inc(S["dve_chain"], 1)
                            dve.wait_ge(S["dve_chain"], 1)
                            dve.sem_inc(S["dve_chain"], -1)
                            dve.sem_inc(S["ps_free"], 1)
                        dve.sem_inc(ready[k], 1)


def layer3_experts_inputs(i):
    return {"gate_w": i["L3_ffn_gate_w"].T, "gate_b": i["L3_ffn_gate_b"].reshape(EX, 1),
            "weight1": i["L3_ffn_weight1"], "weight2": i["L3_ffn_weight2"]}


def shape_tables():
    f = np.float32
    k = np.arange(P)
    return {
        "ident": np.eye(P, dtype=f), "ones": np.ones((P, P), f),
        "group": (k[:, None] // 4 == k[None] // 4).astype(f) / 4,
        "center": np.eye(P, dtype=f) - f(1) / P,
        "upto2": np.stack([k[:, None] <= k[None], k[:, None] >= k[None]], 1).astype(f),
        "behind2": np.stack([k[:, None] > k[None], k[:, None] < k[None]], 1).astype(f),
    }


BESIDE = (4, 10, 4, 14)

INPUTS = (("l0", layer0_inputs), ("l1", layer1_inputs), ("l2a", layer2_mamba_inputs), ("l2f", layer2_experts_inputs),
          ("l3f", layer3_experts_inputs), ("c", lambda i: shape_tables()))


def build(nc, aps, x, out):
    def scratch(name, shape):
        return nc.dram_tensor(name, shape, F32, kind="Internal").ap()

    tables = aps["c"]
    records, table = scratch("records", (B * T + 1, P, PK)), [scratch(f"table{n}", (m * G * POS, C)) for n, m in enumerate((1, B - 1))]
    t = [scratch(f"tokens{n}", (B, N, C)) for n in range(1, 6)]
    with ExitStack() as stack:
        by_tile = lambda tokens: tokens.rearrange("b (t p) c -> (b t) p c", p=P)
        weights = aps["l0"] | tables
        attend = Attend(nc, stack, by_tile(x), by_tile(t[0]), records, table[0], weights)
        row0 = stack.enter_context(nc.sbuf_tensor("row0", [P, GK], F32))
        layer0_prepare(nc, x, weights, records, table[0], 0, row0, 0, "a", attend.tiles(0, 0))
        per = T // (B - 1)
        per -= per % 2
        start = T - per * (B - 1)
        attend_start(nc, attend, start)
        with nc.Fori(0, B - 1) as b:
            layer0_prepare(nc, x, weights, records, table[1], b, row0, b + 1, "b", attend.tiles(b * per + start, per))
        attend_finish(nc, attend, table[1])

        def layers(b, mark, beside):
            first = 0
            for n, (layer, name) in enumerate(((layer1, "l1"), (layer2_mamba, "l2a"), (layer2_experts, "l2f"), (layer3_attention, "l3a"))):
                if beside:
                    more = attend.tiles((b + 1) * T + first, BESIDE[n], fresh=(n == 0))
                else:
                    more = attend.tiles(0, 0)
                layer(nc, t[n], t[n + 1], aps.get(name, {}) | tables, b, mark, more)
                first += BESIDE[n]

        with nc.Fori(0, B - 1) as b:
            layers(b, "", True)
        layers(B - 1, "z", False)
    layer3_experts(nc, t[4], out, scratch("chosen", (B, EX, N)), aps["l3f"] | tables)


def kernel(**inputs):
    import numpy as _np
    import concourse.bacc as _bacc
    from concourse import mybir as _mybir
    from concourse.bass_utils import run_bass_kernel_spmd as _run

    nc = _bacc.Bacc("TRN2", target_bir_lowering=False, num_devices=1)
    inputs = {k: _np.asarray(v) for k, v in inputs.items()}
    arrays, aps = {}, {}

    def give(name, a):
        a = _np.ascontiguousarray(a)
        arrays[f"in_{name}_dram"] = a
        return nc.dram_tensor(f"in_{name}_dram", a.shape, _mybir.dt.from_np(a.dtype), kind="ExternalInput").ap()

    for group, lay_out in INPUTS:
        aps[group] = {name: give(f"{group}_{name}", a) for name, a in lay_out(inputs).items()}
    x = give("x", inputs["x"].reshape(B, N, C))
    out = nc.dram_tensor("out_0_dram", (B, N, C), _mybir.dt.float32, kind="ExternalOutput").ap()
    build(nc, aps, x, out)
    r = _run(nc, [arrays], core_ids=[0])
    return r.results[0]["out_0_dram"].reshape(B, H, W, C)
```
